# Optimizing a Trainium2 kernel written in Bass

```python
import numpy as np
import jax
import jax.numpy as jnp

def _softmax(x, axis=-1):
    return jax.nn.softmax(x, axis=axis)

def _gelu(x):
    return jax.nn.gelu(x, approximate=True)

def _silu(x):
    return jax.nn.silu(x)

def _sigmoid(x):
    return jax.nn.sigmoid(x)

def _layernorm(x, axis=-1, eps=1e-05):
    m = jnp.mean(x, axis=axis, keepdims=True)
    v = jnp.var(x, axis=axis, keepdims=True)
    return (x - m) / jnp.sqrt(v + eps)

def _scatter_add(tgt, idx, src, axis=0):
    return tgt.at[idx].add(src)

def _segment_sum(src, seg, n):
    return jax.ops.segment_sum(src, seg, n)
kernel_name = 'mk_early_fusion_d2_tok_img1024_r4_232fd7'

def setup_inputs(seed: int=0):
    np.random.seed(seed)
    _w = jnp.asarray

    def _rec_inputs():
        import jax
        import jax.numpy as jnp
        _rk = jax.random.key(seed)
        x = -0.00016672 + 0.999947 * jax.random.normal(jax.random.fold_in(_rk, 1), (16, 3, 96, 96), jnp.float32)
        txt = 0.434251 + 1.14597 * jax.random.normal(jax.random.fold_in(_rk, 2), (16, 128, 256), jnp.float32)
        return (x, txt)
    x, txt = _rec_inputs()

    def _L0_tok_setup():
        import jax, jax.numpy as jnp
        import numpy as np
        DIM = 256
        IMG = 96
        P = 16
        C = 3
        TEMP = 10000.0
        EPS = 1e-05
        PATCH_DIM = C * P * P
        HP = IMG // P

        def layernorm(x, gamma, beta):
            mu = jnp.mean(x, axis=-1, keepdims=True)
            var = jnp.var(x, axis=-1, keepdims=True)
            return (x - mu) * jax.lax.rsqrt(var + EPS) * gamma + beta

        def posemb_sincos_2d(h, w, dim, dtype):
            y, x = jnp.meshgrid(jnp.arange(h), jnp.arange(w), indexing='ij')
            omega = jnp.arange(dim // 4, dtype=jnp.float32) / (dim // 4 - 1)
            omega = 1.0 / TEMP ** omega
            y = y.reshape(-1)[:, None] * omega[None, :]
            x = x.reshape(-1)[:, None] * omega[None, :]
            pe = jnp.concatenate((jnp.sin(x), jnp.cos(x), jnp.sin(y), jnp.cos(y)), axis=1)
            return pe.astype(dtype)
        key = jax.random.key(seed)
        ks = jax.random.split(key, 8)
        B = 64
        img = jax.random.normal(ks[0], (B, C, IMG, IMG), dtype=jnp.float32)
        cls_token = jax.random.normal(ks[1], (1, 1, DIM), dtype=jnp.float32)
        cls_pos_embedding = jax.random.normal(ks[2], (1, 1, DIM), dtype=jnp.float32)
        ln1_g = jnp.ones((PATCH_DIM,), jnp.float32)
        ln1_b = jnp.zeros((PATCH_DIM,), jnp.float32)
        W = jax.random.normal(ks[3], (PATCH_DIM, DIM), dtype=jnp.float32) / np.sqrt(PATCH_DIM)
        bias = jnp.zeros((DIM,), jnp.float32)
        ln2_g = jnp.ones((DIM,), jnp.float32)
        ln2_b = jnp.zeros((DIM,), jnp.float32)
        return {'img': img, 'cls_token': cls_token, 'cls_pos_embedding': cls_pos_embedding, 'ln1_g': ln1_g, 'ln1_b': ln1_b, 'W': W, 'bias': bias, 'ln2_g': ln2_g, 'ln2_b': ln2_b}
    _L0_tok_all = _L0_tok_setup()
    _L0_tok_in = {k: v for k, v in _L0_tok_all.items() if k in ('cls_token', 'cls_pos_embedding', 'ln1_g', 'ln1_b', 'W', 'bias', 'ln2_g', 'ln2_b')}
    del _L0_tok_all

    def _L0_attn_setup():
        import jax, jax.numpy as jnp
        import numpy as np
        DIM = 256
        NH = 16
        HD = DIM // NH
        DROPE = 16
        MAXSEQ = 512
        LAT = 64
        BATCH = 2
        SEQ = 512

        def _rope_freqs(max_seq, head_dim):
            inv = 1.0 / 10000.0 ** (jnp.arange(0, head_dim, 2, dtype=jnp.float32) / head_dim)
            ang = jnp.arange(max_seq, dtype=jnp.float32)[:, None] * inv[None, :]
            return (jnp.cos(ang), jnp.sin(ang))

        def _apply_decoupled_rope(x, cosf, sinf, d_rope):
            b, d1, d2, hd = x.shape
            half = d_rope // 2
            xr = x[..., :d_rope].astype(jnp.float32).reshape(b, d1, d2, half, 2)
            xa, xb = (xr[..., 0], xr[..., 1])
            c = cosf[:d1, :half][None, :, None, :]
            s = sinf[:d1, :half][None, :, None, :]
            rot = jnp.stack([xa * c - xb * s, xa * s + xb * c], axis=-1)
            rot = rot.reshape(b, d1, d2, d_rope)
            return jnp.concatenate([rot, x[..., d_rope:]], axis=-1)
        key = jax.random.key(seed)
        ks = jax.random.split(key, 8)

        def w(k, o, i):
            return jax.random.normal(k, (o, i), jnp.float32) / np.sqrt(i).astype(np.float32)
        return {'x': jax.random.normal(ks[0], (BATCH, SEQ, DIM), jnp.float32), 'wq': w(ks[1], NH * HD, DIM), 'wk_a': w(ks[2], LAT, DIM), 'wk_b': w(ks[3], NH * HD, LAT), 'wv_a': w(ks[4], LAT, DIM), 'wv_b': w(ks[5], NH * HD, LAT), 'wo': w(ks[6], DIM, NH * HD)}
    _L0_attn_all = _L0_attn_setup()
    _L0_attn_in = {k: v for k, v in _L0_attn_all.items() if k in ('wq', 'wk_a', 'wk_b', 'wv_a', 'wv_b', 'wo')}
    del _L0_attn_all

    def _L0_ffn_setup():
        import jax, jax.numpy as jnp
        import numpy as np
        E, D, F, GATE_DIM = (8, 256, 1024, 16)
        B, T = (2, 512)
        key = jax.random.key(seed)
        ks = jax.random.split(key, 7)
        s = 0.02
        return {'hidden_states': jax.random.normal(ks[0], (B, T, D), dtype=jnp.float32), 'w_red': jax.random.normal(ks[1], (D, GATE_DIM), dtype=jnp.float32) * s, 'wg': jax.random.normal(ks[2], (E, GATE_DIM), dtype=jnp.float32), 'w1': jax.random.normal(ks[3], (E, D, F), dtype=jnp.float32) * s, 'b1': jax.random.normal(ks[4], (E, F), dtype=jnp.float32) * s, 'w2': jax.random.normal(ks[5], (E, F, D), dtype=jnp.float32) * s, 'b2': jax.random.normal(ks[6], (E, D), dtype=jnp.float32) * s}
    _L0_ffn_all = _L0_ffn_setup()
    _L0_ffn_in = {k: v for k, v in _L0_ffn_all.items() if k in ('w_red', 'wg', 'w1', 'b1', 'w2', 'b2')}
    del _L0_ffn_all

    def _L1_attn_setup():
        import math
        import jax, jax.numpy as jnp
        import numpy as np
        DIM = 256
        DIM_QK = 128
        DIM_V = 256
        NUM_BUCKETS = 32
        MAX_DISTANCE = 128

        def _rel_pos_bucket_causal(seq_len):
            q = np.arange(seq_len)
            n = np.maximum(q[:, None] - q[None, :], 0)
            max_exact = NUM_BUCKETS // 2
            is_small = n < max_exact
            nf = np.maximum(n, 1).astype(np.float32)
            val_if_large = max_exact + (np.log(nf / max_exact) / math.log(MAX_DISTANCE / max_exact) * (NUM_BUCKETS - max_exact)).astype(np.int32)
            val_if_large = np.minimum(val_if_large, NUM_BUCKETS - 1)
            return jnp.asarray(np.where(is_small, n, val_if_large), dtype=jnp.int32)

        def laplacian_attn_fn(x):
            mu = math.sqrt(0.5)
            std = math.sqrt(0.25 * math.pi)
            return (1.0 + jax.lax.erf((x - mu) / (std * math.sqrt(2.0)))) * 0.5
        key = jax.random.key(seed)
        ks = jax.random.split(key, 8)
        B, S = (8, 512)
        x = jax.random.normal(ks[0], (B, S, DIM), dtype=jnp.float32)
        Wqk = jax.random.normal(ks[1], (DIM, DIM_QK), dtype=jnp.float32) * (1.0 / math.sqrt(DIM))
        bqk = jnp.zeros((DIM_QK,), dtype=jnp.float32)
        gamma = jax.random.normal(ks[2], (2, DIM_QK), dtype=jnp.float32) * 0.02
        beta = jnp.zeros((2, DIM_QK), dtype=jnp.float32)
        Wv = jax.random.normal(ks[3], (DIM, DIM_V), dtype=jnp.float32) * (1.0 / math.sqrt(DIM))
        bv = jnp.zeros((DIM_V,), dtype=jnp.float32)
        rel_emb = jax.random.normal(ks[4], (NUM_BUCKETS, 1), dtype=jnp.float32) * 0.02
        return {'x': x, 'Wqk': Wqk, 'bqk': bqk, 'gamma': gamma, 'beta': beta, 'Wv': Wv, 'bv': bv, 'rel_emb': rel_emb}
    _L1_attn_all = _L1_attn_setup()
    _L1_attn_in = {k: v for k, v in _L1_attn_all.items() if k in ('Wqk', 'bqk', 'gamma', 'beta', 'Wv', 'bv', 'rel_emb')}
    del _L1_attn_all

    def _L1_ffn_setup():
        import jax, jax.numpy as jnp
        import numpy as np
        B, S, HID, DFF, E, K = (4, 512, 256, 1024, 8, 512)
        key = jax.random.key(seed)
        ks = jax.random.split(key, 4)
        sc_h = 1.0 / np.sqrt(HID)
        sc_f = 1.0 / np.sqrt(DFF)
        return {'x': jax.random.normal(ks[0], (B, S, HID), jnp.float32), 'router_w': jax.random.normal(ks[1], (HID, E), jnp.float32) * sc_h, 'router_b': jnp.zeros((E,), jnp.float32), 'w1': jax.random.normal(ks[2], (E, HID, DFF), jnp.float32) * sc_h, 'b1': jnp.zeros((E, DFF), jnp.float32), 'w2': jax.random.normal(ks[3], (E, DFF, HID), jnp.float32) * sc_f, 'b2': jnp.zeros((E, HID), jnp.float32)}
    _L1_ffn_all = _L1_ffn_setup()
    _L1_ffn_in = {k: v for k, v in _L1_ffn_all.items() if k in ('router_w', 'router_b', 'w1', 'b1', 'w2', 'b2')}
    del _L1_ffn_all
    return {'x': x, 'txt': txt, 'L0_tok_cls_token': _L0_tok_in['cls_token'], 'L0_tok_cls_pos_embedding': _L0_tok_in['cls_pos_embedding'], 'L0_tok_ln1_g': _L0_tok_in['ln1_g'], 'L0_tok_ln1_b': _L0_tok_in['ln1_b'], 'L0_tok_W': _L0_tok_in['W'], 'L0_tok_bias': _L0_tok_in['bias'], 'L0_tok_ln2_g': _L0_tok_in['ln2_g'], 'L0_tok_ln2_b': _L0_tok_in['ln2_b'], 'L0_attn_wq': _L0_attn_in['wq'], 'L0_attn_wk_a': _L0_attn_in['wk_a'], 'L0_attn_wk_b': _L0_attn_in['wk_b'], 'L0_attn_wv_a': _L0_attn_in['wv_a'], 'L0_attn_wv_b': _L0_attn_in['wv_b'], 'L0_attn_wo': _L0_attn_in['wo'], 'L0_ffn_w_red': _L0_ffn_in['w_red'], 'L0_ffn_wg': _L0_ffn_in['wg'], 'L0_ffn_w1': _L0_ffn_in['w1'], 'L0_ffn_b1': _L0_ffn_in['b1'], 'L0_ffn_w2': _L0_ffn_in['w2'], 'L0_ffn_b2': _L0_ffn_in['b2'], 'L1_attn_Wqk': _L1_attn_in['Wqk'], 'L1_attn_bqk': _L1_attn_in['bqk'], 'L1_attn_gamma': _L1_attn_in['gamma'], 'L1_attn_beta': _L1_attn_in['beta'], 'L1_attn_Wv': _L1_attn_in['Wv'], 'L1_attn_bv': _L1_attn_in['bv'], 'L1_attn_rel_emb': _L1_attn_in['rel_emb'], 'L1_ffn_router_w': _L1_ffn_in['router_w'], 'L1_ffn_router_b': _L1_ffn_in['router_b'], 'L1_ffn_w1': _L1_ffn_in['w1'], 'L1_ffn_b1': _L1_ffn_in['b1'], 'L1_ffn_w2': _L1_ffn_in['w2'], 'L1_ffn_b2': _L1_ffn_in['b2']}

def reference(x, txt, L0_tok_cls_token, L0_tok_cls_pos_embedding, L0_tok_ln1_g, L0_tok_ln1_b, L0_tok_W, L0_tok_bias, L0_tok_ln2_g, L0_tok_ln2_b, L0_attn_wq, L0_attn_wk_a, L0_attn_wk_b, L0_attn_wv_a, L0_attn_wv_b, L0_attn_wo, L0_ffn_w_red, L0_ffn_wg, L0_ffn_w1, L0_ffn_b1, L0_ffn_w2, L0_ffn_b2, L1_attn_Wqk, L1_attn_bqk, L1_attn_gamma, L1_attn_beta, L1_attn_Wv, L1_attn_bv, L1_attn_rel_emb, L1_ffn_router_w, L1_ffn_router_b, L1_ffn_w1, L1_ffn_b1, L1_ffn_w2, L1_ffn_b2):
    import jax
    import jax.numpy as jnp

    def _L0_tok_ref(img, cls_token, cls_pos_embedding, ln1_g, ln1_b, W, bias, ln2_g, ln2_b):
        import jax, jax.numpy as jnp
        import numpy as np
        DIM = 256
        IMG = 96
        P = 16
        C = 3
        TEMP = 10000.0
        EPS = 1e-05
        PATCH_DIM = C * P * P
        HP = IMG // P

        def layernorm(x, gamma, beta):
            mu = jnp.mean(x, axis=-1, keepdims=True)
            var = jnp.var(x, axis=-1, keepdims=True)
            return (x - mu) * jax.lax.rsqrt(var + EPS) * gamma + beta

        def posemb_sincos_2d(h, w, dim, dtype):
            y, x = jnp.meshgrid(jnp.arange(h), jnp.arange(w), indexing='ij')
            omega = jnp.arange(dim // 4, dtype=jnp.float32) / (dim // 4 - 1)
            omega = 1.0 / TEMP ** omega
            y = y.reshape(-1)[:, None] * omega[None, :]
            x = x.reshape(-1)[:, None] * omega[None, :]
            pe = jnp.concatenate((jnp.sin(x), jnp.cos(x), jnp.sin(y), jnp.cos(y)), axis=1)
            return pe.astype(dtype)
        b = img.shape[0]
        x = img.reshape(b, C, HP, P, HP, P)
        x = jnp.transpose(x, (0, 2, 4, 3, 5, 1))
        x = x.reshape(b, HP, HP, PATCH_DIM)
        x = layernorm(x, ln1_g, ln1_b)
        x = jnp.einsum('bhwp,pd->bhwd', x, W) + bias
        x = layernorm(x, ln2_g, ln2_b)
        pe = posemb_sincos_2d(HP, HP, DIM, x.dtype)
        x = x.reshape(b, HP * HP, DIM) + pe[None]
        cls_tokens = jnp.broadcast_to(cls_token + cls_pos_embedding, (b, 1, DIM))
        return jnp.concatenate((cls_tokens, x), axis=1)

    def _L0_attn_ref(x, wq, wk_a, wk_b, wv_a, wv_b, wo):
        import jax, jax.numpy as jnp
        import numpy as np
        DIM = 256
        NH = 16
        HD = DIM // NH
        DROPE = 16
        MAXSEQ = 512
        LAT = 64
        BATCH = 2
        SEQ = 512

        def _rope_freqs(max_seq, head_dim):
            inv = 1.0 / 10000.0 ** (jnp.arange(0, head_dim, 2, dtype=jnp.float32) / head_dim)
            ang = jnp.arange(max_seq, dtype=jnp.float32)[:, None] * inv[None, :]
            return (jnp.cos(ang), jnp.sin(ang))

        def _apply_decoupled_rope(x, cosf, sinf, d_rope):
            b, d1, d2, hd = x.shape
            half = d_rope // 2
            xr = x[..., :d_rope].astype(jnp.float32).reshape(b, d1, d2, half, 2)
            xa, xb = (xr[..., 0], xr[..., 1])
            c = cosf[:d1, :half][None, :, None, :]
            s = sinf[:d1, :half][None, :, None, :]
            rot = jnp.stack([xa * c - xb * s, xa * s + xb * c], axis=-1)
            rot = rot.reshape(b, d1, d2, d_rope)
            return jnp.concatenate([rot, x[..., d_rope:]], axis=-1)
        b, s, _ = x.shape
        q = (x @ wq.T).reshape(b, s, NH, HD).transpose(0, 2, 1, 3)
        k = (x @ wk_a.T @ wk_b.T).reshape(b, s, NH, HD).transpose(0, 2, 1, 3)
        v = (x @ wv_a.T @ wv_b.T).reshape(b, s, NH, HD).transpose(0, 2, 1, 3)
        cosf, sinf = _rope_freqs(MAXSEQ, HD)
        q = _apply_decoupled_rope(q, cosf, sinf, DROPE)
        k = _apply_decoupled_rope(k, cosf, sinf, DROPE)
        scores = jnp.einsum('bhqd,bhkd->bhqk', q, k) / np.float32(np.sqrt(HD))
        attn = jax.nn.softmax(scores, axis=-1)
        out = jnp.einsum('bhqk,bhkd->bhqd', attn, v)
        out = out.transpose(0, 2, 1, 3).reshape(b, s, NH * HD)
        return out @ wo.T

    def _L0_ffn_ref(hidden_states, w_red, wg, w1, b1, w2, b2):
        import jax, jax.numpy as jnp
        import numpy as np
        E, D, F, GATE_DIM = (8, 256, 1024, 16)
        B, T = (2, 512)
        b, t, c = hidden_states.shape
        x = hidden_states.reshape(-1, c)
        red = x @ w_red
        wg_n = wg / jnp.maximum(jnp.linalg.norm(wg, axis=1, keepdims=True), 0.0001)
        logits = red @ wg_n.T
        gates = jax.nn.softmax(logits, axis=1)
        idx = jnp.argmax(gates, axis=1)
        scores = jnp.take_along_axis(gates, idx[:, None], axis=1)
        h = jax.nn.gelu(jnp.einsum('td,edf->etf', x, w1) + b1[:, None, :], approximate=False)
        y = jnp.einsum('etf,efd->etd', h, w2) + b2[:, None, :]
        out = jnp.take_along_axis(y, idx[None, :, None], axis=0)[0]
        out = out * scores
        return out.reshape(b, t, c)

    def _L1_attn_ref(x, Wqk, bqk, gamma, beta, Wv, bv, rel_emb):
        import math
        import jax, jax.numpy as jnp
        import numpy as np
        DIM = 256
        DIM_QK = 128
        DIM_V = 256
        NUM_BUCKETS = 32
        MAX_DISTANCE = 128

        def _rel_pos_bucket_causal(seq_len):
            q = np.arange(seq_len)
            n = np.maximum(q[:, None] - q[None, :], 0)
            max_exact = NUM_BUCKETS // 2
            is_small = n < max_exact
            nf = np.maximum(n, 1).astype(np.float32)
            val_if_large = max_exact + (np.log(nf / max_exact) / math.log(MAX_DISTANCE / max_exact) * (NUM_BUCKETS - max_exact)).astype(np.int32)
            val_if_large = np.minimum(val_if_large, NUM_BUCKETS - 1)
            return jnp.asarray(np.where(is_small, n, val_if_large), dtype=jnp.int32)

        def laplacian_attn_fn(x):
            mu = math.sqrt(0.5)
            std = math.sqrt(0.25 * math.pi)
            return (1.0 + jax.lax.erf((x - mu) / (std * math.sqrt(2.0)))) * 0.5
        B, S, _ = x.shape
        qk = jax.nn.swish(jnp.einsum('bsd,de->bse', x, Wqk) + bqk)
        q = qk * gamma[0] + beta[0]
        k = qk * gamma[1] + beta[1]
        v = jax.nn.swish(jnp.einsum('bsd,de->bse', x, Wv) + bv)
        scale = 1.0 / S
        sim = jnp.einsum('bid,bjd->bij', q, k) * scale
        buckets = _rel_pos_bucket_causal(S)
        bias = rel_emb[buckets, 0] * DIM_QK ** 0.5
        sim = sim + bias
        attn = laplacian_attn_fn(sim)
        i = jnp.arange(S)
        future = i[None, :] > i[:, None]
        attn = jnp.where(future, 0.0, attn)
        return jnp.einsum('bij,bjd->bid', attn, v)

    def _L1_ffn_ref(x, router_w, router_b, w1, b1, w2, b2):
        import jax, jax.numpy as jnp
        import numpy as np
        B, S, HID, DFF, E, K = (4, 512, 256, 1024, 8, 512)
        b, s, h = x.shape
        xf = x.reshape(-1, h)
        logits = xf @ router_w + router_b
        scores = jax.nn.softmax(logits, axis=-1)
        G, idx = jax.lax.top_k(scores.T, K)
        toks = xf[idx]
        h1 = jax.nn.relu(jnp.einsum('ekh,ehf->ekf', toks, w1) + b1[:, None, :])
        eo = jnp.einsum('ekf,efh->ekh', h1, w2) + b2[:, None, :]
        contrib = (eo * G[..., None]).reshape(-1, h)
        y = jnp.zeros_like(xf).at[idx.reshape(-1)].add(contrib)
        return y.reshape(b, s, h)
    h = _L0_tok_ref(x, L0_tok_cls_token, L0_tok_cls_pos_embedding, L0_tok_ln1_g, L0_tok_ln1_b, L0_tok_W, L0_tok_bias, L0_tok_ln2_g, L0_tok_ln2_b)
    h = jnp.concatenate([h, txt], axis=1)
    h = h + _L0_attn_ref(_layernorm(h, axis=-1), L0_attn_wq, L0_attn_wk_a, L0_attn_wk_b, L0_attn_wv_a, L0_attn_wv_b, L0_attn_wo)
    h = h + _L0_ffn_ref(_layernorm(h, axis=-1), L0_ffn_w_red, L0_ffn_wg, L0_ffn_w1, L0_ffn_b1, L0_ffn_w2, L0_ffn_b2)
    h = h + _L1_attn_ref(_layernorm(h, axis=-1), L1_attn_Wqk, L1_attn_bqk, L1_attn_gamma, L1_attn_beta, L1_attn_Wv, L1_attn_bv, L1_attn_rel_emb)
    h = h + _L1_ffn_ref(_layernorm(h, axis=-1), L1_ffn_router_w, L1_ffn_router_b, L1_ffn_w1, L1_ffn_b1, L1_ffn_w2, L1_ffn_b2)
    return h

_drawn_inputs = setup_inputs


def setup_inputs(seed=0):
    import zlib

    import numpy as np

    out = dict(_drawn_inputs(seed))
    spreads = {'L0_tok_ln1_g': (1.0, 0.2),
     'L0_tok_ln1_b': (0.0, 0.1),
     'L0_tok_bias': (0.0, 0.1),
     'L0_tok_ln2_g': (1.0, 0.2),
     'L0_tok_ln2_b': (0.0, 0.1),
     'L1_attn_bqk': (0.0, 2.0),
     'L1_attn_beta': (0.0, 0.8),
     'L1_attn_bv': (0.0, 0.1),
     'L1_ffn_router_b': (0.0, 0.8),
     'L1_ffn_b1': (0.0, 2.0),
     'L1_ffn_b2': (0.0, 0.8)}
    factors = {'L0_ffn_w_red': 8.0,
     'L0_ffn_wg': 8.0,
     'L0_ffn_w1': 7.71,
     'L0_ffn_b1': 8.0,
     'L0_ffn_w2': 7.279,
     'L0_ffn_b2': 24.656,
     'L1_attn_Wqk': 8.0,
     'L1_attn_gamma': 8.0}
    for name, (base, spread) in spreads.items():
        noise = np.random.default_rng([zlib.crc32(name.encode()), seed]).standard_normal(out[name].shape)
        drawn = base * np.exp(spread * noise) if base else spread * noise
        out[name] = jnp.asarray(drawn.astype(out[name].dtype))
    for name, factor in factors.items():
        out[name] = (out[name] * factor).astype(out[name].dtype)
    return out
```

```python
import math
from contextlib import ExitStack

import numpy as np

import concourse.bass as bass
from concourse import mybir

ALU = mybir.AluOpType
ACT = mybir.ActivationFunctionType
AX = mybir.AxisListType
F32 = mybir.dt.float32
F16 = mybir.dt.float16
BF16 = mybir.dt.bfloat16
I32 = mybir.dt.int32

EPS = 1e-5
B, D = 16, 256
PATCH, HP, NTXT = 768, 6, 128
NPATCH = HP * HP
SEQ = 1 + NPATCH + NTXT
TOK = B * SEQ
TP, NT = 120, 22
PT, NPT = 2 * NPATCH, B // 2
KP = PATCH // 128
GROUPS = (range(0, 6), range(6, 12), range(12, 17), range(17, 22))
DK = D // 128
NH, HD = 16, 16
LAT = 64
MAIN, REM = 128, SEQ - 128
PAIR = 2 * SEQ
REM_B = 64
NU = NH // 2
OW = HD + 1
E, F, GD = 8, 1024, 16
FK = F // 128
RB = 6
SLOT = 128
SLOT_TILES = (TOK + E * (SLOT - 1)) // SLOT
SLOTS = SLOT_TILES * SLOT
TOPK = 512
COLS, NCOLS = 440, 6


class Mem:
    pass


def tokenise(nc, sem, m, d):
    with ExitStack() as ctx:
        def sb(name, shape, dt=F32):
            return ctx.enter_context(nc.sbuf_tensor(name, shape, dt))

        x = sb("patches", [PT, NPT, PATCH])
        xn = sb("patches_normed", [PT, 2, PATCH])
        xg = sb("patches_scaled", [128, 2, KP, PT])
        xT = sb("patches_T", [128, 2, KP, PT])
        w = sb("tok_w", [128, KP, D])
        gb = sb("ln1_gb", [128, 2, KP])
        rows = sb("tok_rows", [PT, 3, D])
        pe_b = sb("pos_offset", [PT, D])
        cls = sb("cls_rows", [B, 2, D])
        tok = sb("tok", [PT, NPT, D])
        st = sb("stats1", [PT, NPT, 2, 6])
        mv = sb("mean_var1", [PT, NPT, 2])
        std = sb("std1", [PT, NPT])
        rstd = sb("rstd1", [PT, NPT])
        st2 = sb("stats2", [PT, NPT, 6])
        mv2 = sb("mean_var2", [PT, NPT, 2])
        std2 = sb("std2", [PT, NPT])
        rstd2 = sb("rstd2", [PT, NPT])
        eps = sb("eps_tok", [PT, 1])
        zrow = sb("zero_row", [128, D])
        zero_set = sem("zero_set")

        x_in = [sem("x_in_a"), sem("x_in_b")]
        small_in, w_in = sem("tok_small_in"), sem("tok_w_in")
        eps_set, psum_zero = sem("tok_eps_set"), sem("psum_zeroed")
        st1_done, mv1_done, std1_done, rstd1_done = (sem(n) for n in ("st1", "mv1", "std1", "rstd1"))
        xn_ready, xp_ready, xg_ready, xT_ready, y_ready, tok_ready = (
            sem(n) for n in ("xn_ready", "xp_ready", "xg_ready", "xT_ready", "y_ready", "tok_ready"))
        st2_done, mv2_done, std2_done, rstd2_done = (sem(n) for n in ("st2", "mv2", "std2", "rstd2"))
        peb_done, cls_done, n2_a, n2_b, n2_c = (sem(n) for n in ("peb", "cls", "n2a", "n2b", "n2c"))
        h0_out, rot_parts = sem("h0_out"), sem("rot_parts")
        ps = m.ps
        h0_b = m.h0.rearrange("(b s) d -> b s d", s=SEQ)
        h0_j = m.h0.rearrange("(j b s) d -> b s j d", j=NPT, b=2)
        half = NPT // 2
        with nc.Block() as block:
            @block.sync
            def _(sp):
                pd = d["patches"].rearrange("(j p) k -> p j k", p=PT)
                for n in range(2):
                    sp.dma_start(x[:, n * half:(n + 1) * half, :], pd[:, n * half:(n + 1) * half, :]).then_inc(x_in[n], 16)
                sp.dma_start(m.ident[:], d["ident"]).then_inc(small_in, 16)
                sp.dma_start(gb[:], d["ln1_gb"]).then_inc(small_in, 16)
                for n, name in enumerate(("tok_bias", "ln2_g", "ln2_b")):
                    sp.dma_start(rows[:, n, :], d[name].to_broadcast([PT, D])).then_inc(small_in, 16)
                sp.dma_start(pe_b[:], d["pos"]).then_inc(small_in, 16)
                for n, name in enumerate(("cls", "cls_pos")):
                    sp.dma_start(cls[:, n, :], d[name].to_broadcast([B, D])).then_inc(small_in, 16)
                sp.dma_start(w[:], d["tok_w"].rearrange("(c p) n -> p c n", p=128)).then_inc(w_in, 16)
                sp.wait_ge(zero_set, 1)
                sp.dma_start(m.xs.rearrange("(p r) d -> p r d", p=128),
                             zrow[:].unsqueeze(1).to_broadcast([128, SLOTS // 128, D])).then_inc(m.zero_out, 16)
                sp.dma_start(h0_b[:, 1 + NPATCH:, :], d["txt"]).then_inc(h0_out, 16)
                for dst, src in m.attn_loads:
                    sp.dma_start(dst, src).then_inc(m.attn_in, 16)
                sp.wait_ge(cls_done, 1)
                sp.dma_start(h0_b[:, 0, :], cls[:, 0, :]).then_inc(h0_out, 16)
                sp.wait_ge(n2_c, NPT)
                for b in range(2):
                    sp.dma_start(h0_j[b, 1:1 + NPATCH], tok[b * NPATCH:(b + 1) * NPATCH]).then_inc(h0_out, 16)
                sp.wait_ge(h0_out, 64)
                for g, ts in enumerate(GROUPS):
                    sp.dma_start(m.h[:, ts.start:ts.stop], m.h0.rearrange("(t p) d -> p t d", p=TP)[:, ts.start:ts.stop])\
                      .then_inc(m.h_in[g], 16)
                for dst, src in m.expert_loads:
                    sp.dma_start(dst, src).then_inc(m.expert_in, 16)

            @block.tensor
            def _(pe):
                pe.wait_ge(small_in, 128)
                pe.wait_ge(w_in, 16)
                pe.wait_ge(psum_zero, 1)
                with pe.Fori(0, half) as i:
                    for n in range(2):
                        pe.wait_ge(xn_ready, i * 2 + n + 1)
                        pe.wait_ge(xg_ready, i * 2)
                        for k in range(KP):
                            last = pe.transpose(ps[:, n, k * PT:(k + 1) * PT], xn[:, n, k * 128:(k + 1) * 128],
                                                m.ident[0:PT, 0:PT])
                        last.then_inc(xp_ready, 1)
                    for n in range(2):
                        pe.wait_ge(xT_ready, i * 2 + n + 1)
                        pe.wait_ge(tok_ready, i * 2)
                        for k in range(KP):
                            last = pe.matmul(ps[0:PT, 2 + n, 0:D], xT[:, n, k, :], w[:, k, :],
                                             start=(k == 0), stop=(k == KP - 1))
                        last.then_inc(y_ready, 1)

            @block.gpsimd
            def _(pool):
                pool.wait_ge(small_in, 128)
                pool.tensor_tensor(pe_b[:], pe_b[:], rows[:, 2, :], ALU.add).then_inc(peb_done, 1)
                pool.tensor_tensor(cls[:, 0, :], cls[:, 0, :], cls[:, 1, :], ALU.add).then_inc(cls_done, 1)
                pool.wait_ge(m.attn_in, m.attn_want)
                kb, kb_swap = m.wkb[0:LAT, :], m.wkb_swap[0:LAT, :]
                cos_q, sin_q = (a[:, 0, :].unsqueeze(1).to_broadcast([128, DK, D]) for a in (m.rot_cos, m.rot_sin))
                pool.tensor_tensor(m.wq[:], m.wq[:], cos_q, ALU.mult).then_inc(rot_parts, 1)
                pool.tensor_tensor(m.wq_swap[:], m.wq_swap[:], sin_q, ALU.mult).then_inc(rot_parts, 1)
                pool.tensor_tensor(kb, kb, m.rot_cos[0:LAT, 1, :], ALU.mult).then_inc(rot_parts, 1)
                pool.tensor_tensor(kb_swap, kb_swap, m.rot_sin[0:LAT, 1, :], ALU.mult).then_inc(rot_parts, 1)
                pool.wait_ge(rot_parts, 4)
                pool.tensor_tensor(m.wq[:], m.wq[:], m.wq_swap[:], ALU.add)
                pool.tensor_tensor(kb, kb, kb_swap, ALU.add)
                off = gb[:, 1, :].unsqueeze(2).to_broadcast([128, KP, PT])
                with pool.Fori(0, half) as i:
                    for n in range(2):
                        pool.wait_ge(xg_ready, i * 2 + n + 1)
                        pool.tensor_tensor(xT[:, n], xg[:, n], off, ALU.add).then_inc(xT_ready, 1)

            @block.scalar
            def _(act):
                act.wait_ge(eps_set, 1)
                act.wait_ge(mv1_done, NPT)
                act.activation(std[:], mv[:, :, 1], ACT.Sqrt, bias=eps[:, 0:1]).then_inc(std1_done, 1)
                act.wait_ge(mv2_done, NPT)
                act.activation(std2[:], mv2[:, :, 1], ACT.Sqrt, bias=eps[:, 0:1]).then_inc(std2_done, 1)

            @block.vector
            def _(dve):
                dve.memset(eps[:], EPS).then_inc(eps_set, 1)
                dve.memset(zrow[:], 0.0).then_inc(zero_set, 1)
                dve.memset(ps[:], 0.0).then_inc(psum_zero, 1)
                for n in range(2):
                    dve.wait_ge(x_in[n], 16)
                    with dve.Fori(n * half, (n + 1) * half) as j:
                        for c in range(2):
                            dve.bn_stats(st[:, bass.ds(j, 1), c, :], x[:, bass.ds(j, 1), c * (PATCH // 2):(c + 1) * (PATCH // 2)])\
                                .then_inc(st1_done, 1)
                dve.wait_ge(st1_done, 2 * NPT)
                for j in range(NPT):
                    dve.bn_aggr(mv[:, j, :], st[:, j].rearrange("p c s -> p (c s)")).then_inc(mv1_done, 1)
                dve.wait_ge(std1_done, 1)
                dve.reciprocal(rstd[:], std[:]).then_inc(rstd1_done, 1)
                dve.wait_ge(rstd1_done, 1)
                dve.wait_ge(mv1_done, NPT)
                dve.wait_ge(small_in, 128)
                gain = gb[:, 0, :].unsqueeze(2).to_broadcast([128, KP, PT])
                with dve.Fori(0, half) as i:
                    for n in range(2):
                        dve.wait_ge(xp_ready, i * 2)
                        j = i * 2 + n
                        dve.tensor_scalar(xn[:, n, :], x[:, bass.ds(j, 1), :].rearrange("p a k -> p (a k)"),
                                          mv[:, bass.ds(j, 1), 0], rstd[:, bass.ds(j, 1)],
                                          ALU.subtract, ALU.mult).then_inc(xn_ready, 1)
                    for n in range(2):
                        dve.wait_ge(xp_ready, i * 2 + n + 1)
                        dve.wait_ge(xT_ready, i * 2)
                        dve.tensor_tensor(xg[:, n], ps[:, n, 0:KP * PT].rearrange("p (k t) -> p k t", k=KP), gain,
                                          ALU.mult).then_inc(xg_ready, 1)
                    for n in range(2):
                        dve.wait_ge(y_ready, i * 2 + n + 1)
                        dve.tensor_tensor(tok[:, bass.ds(i * 2 + n, 1), :], ps[0:PT, 2 + n, 0:D].unsqueeze(1),
                                          rows[:, 0, :].unsqueeze(1), ALU.add).then_inc(tok_ready, 1)
                dve.wait_ge(tok_ready, NPT)
                with dve.Fori(0, NPT) as j:
                    dve.bn_stats(st2[:, bass.ds(j, 1), :], tok[:, bass.ds(j, 1), :]).then_inc(st2_done, 1)
                dve.wait_ge(st2_done, NPT)
                for j in range(NPT):
                    dve.bn_aggr(mv2[:, j, :], st2[:, j, :]).then_inc(mv2_done, 1)
                dve.wait_ge(std2_done, 1)
                dve.reciprocal(rstd2[:], std2[:]).then_inc(rstd2_done, 1)
                dve.wait_ge(rstd2_done, 1)
                dve.wait_ge(mv2_done, NPT)
                dve.wait_ge(peb_done, 1)
                with dve.Fori(0, NPT) as j:
                    row = tok[:, bass.ds(j, 1), :].rearrange("p a k -> p (a k)")
                    dve.tensor_scalar(row, row, mv2[:, bass.ds(j, 1), 0], rstd2[:, bass.ds(j, 1)],
                                      ALU.subtract, ALU.mult).then_inc(n2_a, 1)
                    dve.wait_ge(n2_a, j + 1)
                    dve.tensor_tensor(row, row, rows[:, 1, :], ALU.mult).then_inc(n2_b, 1)
                    dve.wait_ge(n2_b, j + 1)
                    dve.tensor_tensor(row, row, pe_b[:], ALU.add).then_inc(n2_c, 1)


def normalise(nc, sem, m, tag, source=None, source_pe=None, use_pe=None, on_sync=None, on_pool=None):
    with ExitStack() as ctx:
        def sb(name, shape, dt=F32):
            return ctx.enter_context(nc.sbuf_tensor(name + tag, shape, dt))

        st = sb("stats", [TP, NT, 6])
        mv = sb("mean_var", [TP, NT, 2])
        std = sb("std", [TP, NT])
        rstd = sb("rstd", [TP, NT])
        eps = sb("eps", [TP, 1])
        eps_set, h_ready, st_done, mv_done, std_done, rstd_done, xn_ready, xp_ready, xT_ready = (
            sem(n + tag) for n in ("eps_set", "h", "st", "mv", "std", "rstd", "xn", "xp", "xT"))
        ps = m.ps
        XB, BANKS = 2, 4
        last_group = len(GROUPS) - 1
        with nc.Block() as block:
            if on_sync is not None:
                @block.sync
                def _(sp):
                    on_sync(sp, h_ready, xn_ready)

            if on_pool is not None:
                @block.gpsimd
                def _(pool):
                    on_pool(pool)

            @block.vector
            def _(dve):
                dve.memset(eps[:], EPS).then_inc(eps_set, 1)

                def statistics(g):
                    if source is None:
                        dve.wait_ge(m.h_in[g], m.h_want)
                    else:
                        for t in GROUPS[g]:
                            source(dve, t, h_ready)
                    for t in GROUPS[g]:
                        if source is not None:
                            dve.wait_ge(h_ready, t + 1)
                        dve.bn_stats(st[:, t, :], m.h[:, t, :]).then_inc(st_done, 1)
                    for t in GROUPS[g]:
                        dve.wait_ge(st_done, t + 1)
                        dve.bn_aggr(mv[:, t, :], st[:, t, :]).then_inc(mv_done, 1)

                def scale(g):
                    a, b = GROUPS[g].start, GROUPS[g].stop
                    dve.wait_ge(std_done, g + 1)
                    dve.reciprocal(rstd[:, a:b], std[:, a:b]).then_inc(rstd_done, 1)
                    dve.wait_ge(rstd_done, g + 1)
                    for t in GROUPS[g]:
                        dve.tensor_scalar(m.xn[:, t, :], m.h[:, t, :], mv[:, t, 0:1], rstd[:, t:t + 1],
                                          ALU.subtract, ALU.mult).then_inc(xn_ready, 1)

                statistics(0)
                for g in range(last_group):
                    statistics(g + 1)
                    scale(g)
                scale(last_group)

            @block.tensor
            def _(pe):
                def make(t):
                    if source_pe is not None:
                        source_pe(pe, t, h_ready)

                def turn(t):
                    pe.wait_ge(xn_ready, t + 1)
                    if t >= BANKS:
                        pe.wait_ge(xT_ready, t - BANKS + 1)
                    for c in range(DK):
                        last = pe.transpose(ps[:, XB + t % BANKS, c * TP:(c + 1) * TP], m.xn[:, t, c * 128:(c + 1) * 128],
                                            m.ident[0:TP, 0:TP])
                    last.then_inc(xp_ready, 1)

                def use(t):
                    if use_pe is not None:
                        pe.wait_ge(xT_ready, t + 1)
                        use_pe(pe, t)

                for t in (*GROUPS[0], *GROUPS[1]):
                    make(t)
                for g in range(last_group + 1):
                    ahead = list(GROUPS[g + 2]) if g + 2 <= last_group else []
                    for n, t in enumerate(GROUPS[g]):
                        turn(t)
                        if n < len(ahead):
                            make(ahead[n])
                        if t >= 2:
                            use(t - 2)
                    assert len(ahead) <= len(GROUPS[g])
                use(NT - 2)
                use(NT - 1)

            @block.scalar
            def _(act):
                def deviation(g):
                    a, b = GROUPS[g].start, GROUPS[g].stop
                    act.wait_ge(mv_done, b)
                    act.activation(std[:, a:b], mv[:, a:b, 1], ACT.Sqrt, bias=eps[:, 0:1]).then_inc(std_done, 1)

                def keep(g):
                    for t in GROUPS[g]:
                        act.wait_ge(xp_ready, t + 1)
                        act.copy(m.xT[:, :, t * TP:(t + 1) * TP],
                                 ps[:, XB + t % BANKS, 0:DK * TP].rearrange("p (c t) -> p c t", c=DK)).then_inc(xT_ready, 1)

                act.wait_ge(eps_set, 1)
                deviation(0)
                for g in range(last_group):
                    deviation(g + 1)
                    keep(g)
                keep(last_group)


def attend0(nc, sem, m, d):
    with ExitStack() as ctx:
        def sb(name, shape, dt=F32):
            return ctx.enter_context(nc.sbuf_tensor(name, shape, dt))

        q = sb("q", [128, 2, DK, SEQ])
        k = sb("k", [128, 2, DK, SEQ])
        kd = sb("k_by_head", [128, 2, DK, 8, SEQ])
        qd = sb("q_rem_by_head", [128, 2, DK, 4, 2, REM_B])
        v = sb("v", [128, 2, NU, 3, 4 * OW])
        vr = sb("v_rem", [3 * REM, 2, NU, 4, OW])
        lat = sb("latents", [128, SEQ])
        lat3 = sb("latents_rem", [128, REM, 3])
        p = sb("probs", [128, 2, SEQ, 3])
        pT = sb("probs_T", [128, 2, 512])
        nmax = sb("neg_max", [128, 2, 3])
        rs = sb("recip_sum", [128, 2, 4, 4])
        o = sb("o", [128, 2, 2, NU, HD])

        names = ("v_blank qd_blank ones lat_ps lat_sb q_ps q_sb k_ps k_sb kd_ready qd_ready v_ps v_sb s_ready max_ready "
                 "exps_done pT_ready pT_sb o_ready recip_ready o_norm oT_ready oT_done").split()
        (v_blank, qd_blank, ones, lat_ps, lat_sb, q_ps, q_sb, k_ps, k_sb, kd_ready, qd_ready, v_ps, v_sb, s_ready, max_ready,
         exps_done, pT_ready, pT_sb, o_ready, recip_ready, o_norm, oT_ready, oT_done) = (sem("a0_" + n) for n in names)
        ps = m.ps
        S, T, O, QB, KB = 0, 2, 4, 6, 7
        LOOPS = (B - 2) // 2

        def turns(eng, step):
            step(0, 0, True, False)
            with eng.Fori(0, LOOPS) as i:
                step(i * 2 + 1, 1, False, False)
                step(i * 2 + 2, 0, False, False)
            step(B - 1, 1, False, True)

        with nc.Block() as block:
            @block.tensor
            def _(pe):
                def project_latents(t):
                    pe.wait_ge(oT_done, t)
                    for c in range(DK):
                        last = pe.matmul(ps[:, KB, 0:SEQ], m.wlat[:, c, :], m.xT[:, c, bass.ds(t * SEQ, SEQ)],
                                         start=(c == 0), stop=(c == DK - 1))
                    last.then_inc(lat_ps, 1)

                def project_q(t):
                    for n in range(DK):
                        for c in range(DK):
                            last = pe.matmul(ps[:, QB, n * SEQ:(n + 1) * SEQ], m.wq[:, c, n * 128:(n + 1) * 128],
                                             m.xT[:, c, bass.ds(t * SEQ, SEQ)], start=(c == 0), stop=(c == DK - 1))
                    last.then_inc(q_ps, 1)

                def project_k(t):
                    pe.wait_ge(lat_sb, t + 1)
                    for n in range(DK):
                        last = pe.matmul(ps[:, KB, n * SEQ:(n + 1) * SEQ], m.wkb[0:LAT, n * 128:(n + 1) * 128],
                                         lat[0:LAT, :], start=True, stop=True)
                    last.then_inc(k_ps, 1)

                def project_v(t):
                    pe.wait_ge(q_sb, t + 1)
                    pe.wait_ge(lat_sb, t + 1)
                    pe.matmul(ps[:, QB, 0:D], lat[LAT:128, 0:MAIN], m.wvb[LAT:128, :], start=True, stop=True)
                    pe.matmul(ps[0:3 * REM, QB, D:2 * D], lat3[LAT:128].rearrange("p t r -> p (t r)"),
                              m.wvb[LAT:128, :], start=True, stop=True).then_inc(v_ps, 1)

                def scores(t, n, u):
                    if u == 0:
                        pe.wait_ge(kd_ready, t + 1)
                        pe.wait_ge(qd_ready, t + 1)
                    pe.wait_ge(exps_done, t * NU + u + 1)
                    c, pr = u // 4, u % 4
                    pe.matmul(ps[:, S + u % 2, 0:2 * SEQ], q[:, n, c, 0:MAIN],
                              kd[:, n, c, 2 * pr:2 * pr + 2].rearrange("p h t -> p (h t)"), start=True, stop=True)
                    pe.matmul(ps[:, S + u % 2, 2 * SEQ:3 * SEQ], qd[:, n, c, pr].rearrange("p a t -> p (a t)"),
                              k[:, n, c, :], start=True, stop=True).then_inc(s_ready, 1)

                def turn_probs(g, n):
                    pe.wait_ge(exps_done, g + 3)
                    for s in range(3):
                        pe.transpose(ps[:, T + n, s * 128:(s + 1) * 128], p[:, n, 0:MAIN, s], m.ident[:])
                    pe.transpose(ps[0:3 * REM, T + n, 384:512], p[:, n, MAIN:SEQ, :].rearrange("p t s -> p (t s)"),
                                 m.ident[:]).then_inc(pT_ready, 1)

                def weigh_values(t, n, u):
                    bank, at = O + u // 4, (u % 4) * 4 * OW
                    if u == 0:
                        pe.wait_ge(v_sb, t + 1)
                    if u % 4 == 0:
                        pe.wait_ge(o_norm, t * 2 + u // 4 + 1)
                    pe.wait_ge(pT_sb, t * NU + u + 1)
                    out = ps[:, bank, at:at + 4 * OW]
                    for s in range(3):
                        pe.matmul(out, pT[:, u % 2, s * 128:(s + 1) * 128], v[:, n, u, s, :],
                                  start=(u % 4 == 0 and s == 0), stop=False, skip_group_check=True)
                    last = pe.matmul(out, pT[0:3 * REM, u % 2, 384:512], vr[:, n, u].rearrange("p a w -> p (a w)"),
                                     start=False, stop=True, skip_group_check=True)
                    if u % 4 == 3:
                        last.then_inc(o_ready, 1)

                def turn_out(t):
                    pe.wait_ge(o_norm, t * 2 + 4)
                    for s in range(2):
                        for ab in range(2):
                            last = pe.transpose(ps[:, KB, (2 * s + ab) * 128:(2 * s + ab + 1) * 128],
                                                o[:, s, ab].rearrange("p u w -> p (u w)"), m.ident[:])
                    last.then_inc(oT_ready, 1)

                def step(t, n, first, last):
                    for u in range(NU):
                        scores(t, n, u)
                        if not (first and u == 0):
                            turn_probs(t * NU + u - 1, (u - 1) % 2)
                        if u == 5 and not first:
                            pe.wait_ge(k_sb, t + 1 if last else t + 2)
                            turn_out(t - 1)
                        if u >= 2:
                            weigh_values(t, n, u - 2)
                        elif not first:
                            weigh_values(t - 1, 1 - n, u + 6)
                        if not last:
                            if u == 0:
                                project_latents(t + 1)
                            if u == 1:
                                pe.wait_ge(v_sb, t + 1)
                                project_q(t + 1)
                            if u == 2:
                                project_k(t + 1)
                            if u == 3:
                                project_v(t + 1)

                project_latents(0)
                project_q(0)
                project_k(0)
                project_v(0)
                turns(pe, step)
                turn_probs(B * NU - 1, 1)
                weigh_values(B - 1, 1, NU - 2)
                weigh_values(B - 1, 1, NU - 1)
                turn_out(B - 1)

            @block.vector
            def _(dve):
                dve.memset(v[:], 0.0).then_inc(v_blank, 1)
                dve.memset(ps[:, S:S + 4, :], 0.0)
                dve.wait_ge(v_blank, 1)
                for n in range(2):
                    for s, blk in ((0, 0), (1, 1), (2, 2), (2, 3)):
                        c = blk * OW + HD
                        dve.memset(v[:, n, :, s, c:c + 1], 1.0)
                    dve.tensor_copy(vr[:, n, :, :, HD], m.rem_mask[0:3 * REM, :].unsqueeze(1)
                                    .to_broadcast([3 * REM, NU, 4])).then_inc(ones, 1)

                def keep_k(t, n):
                    dve.wait_ge(k_ps, t + 1)
                    dve.tensor_copy(k[:, n], ps[:, KB, 0:DK * SEQ].rearrange("p (c t) -> p c t", c=DK)).then_inc(k_sb, 1)

                def keep_v(t, n):
                    dve.wait_ge(v_ps, t + 1)
                    vps = ps[:, QB, 0:D].rearrange("p (u a w) -> p u a w", u=NU, a=2)
                    rps = ps[0:3 * REM, QB, D:2 * D].rearrange("p (u a w) -> p u a w", u=NU, a=2)
                    vb = v[:, n].rearrange("p u s (a w) -> p u s a w", a=4)
                    for ab in range(2):
                        dve.tensor_copy(vb[:, :, ab, ab, 0:HD], vps[:, :, ab])
                    dve.tensor_copy(vb[:, :, 2, 2:4, 0:HD], vps)
                    for s in range(2):
                        last = dve.tensor_tensor(
                            vr[:, n, :, 2 * s:2 * s + 2, 0:HD], rps,
                            m.rem_mask[0:3 * REM, 2 * s:2 * s + 2].unsqueeze(1).unsqueeze(3)
                            .to_broadcast([3 * REM, NU, 2, HD]), ALU.mult)
                    last.then_inc(v_sb, 1)

                def normalise_out(t, half):
                    out = ps[:, O + half, 0:16 * OW].rearrange("p (u a w) -> p u a w", u=4, a=4)
                    dve.wait_ge(o_ready, t * 2 + half + 1)
                    dve.reciprocal(rs[:, half], out[:, :, :, HD]).then_inc(recip_ready, 1)
                    dve.wait_ge(recip_ready, t * 2 + half + 1)
                    dve.tensor_tensor(o[:].rearrange("p s a u w -> p u (s a) w")[:, 4 * half:4 * half + 4],
                                      out[:, :, :, 0:HD],
                                      rs[:, half].unsqueeze(3).to_broadcast([128, 4, 4, HD]), ALU.mult)\
                       .then_inc(o_norm, 1)

                def keep_probs(g, n):
                    dve.wait_ge(pT_ready, g + 1)
                    dve.tensor_copy(pT[:, n], ps[:, T + n, :]).then_inc(pT_sb, 1)

                def step(t, n, first, last):
                    for u in range(NU):
                        dve.wait_ge(s_ready, t * NU + u + 1)
                        dve.tensor_reduce(nmax[:, u % 2, :], ps[:, S + u % 2, 0:3 * SEQ]
                                          .rearrange("p (s t) -> p s t", s=3), AX.X, ALU.max, negate=True)\
                           .then_inc(max_ready, 1)
                        if not (first and u == 0):
                            keep_probs(t * NU + u - 1, (u - 1) % 2)
                        if u == 1 and not first:
                            normalise_out(t - 1, 1)
                        if u == 5:
                            normalise_out(t, 0)
                        if not last:
                            if u == 2:
                                keep_k(t + 1, 1 - n)
                            if u == 3:
                                keep_v(t + 1, 1 - n)

                dve.wait_ge(ones, 2)
                keep_k(0, 0)
                keep_v(0, 0)
                turns(dve, step)
                keep_probs(B * NU - 1, 1)
                normalise_out(B - 1, 1)

            @block.gpsimd
            def _(pool):
                pool.memset(qd[:], 0.0).then_inc(qd_blank, 1)
                pool.wait_ge(qd_blank, 1)

                def split_heads(t, n):
                    mask = m.head_mask[:]
                    pool.wait_ge(k_sb, t + 1)
                    for c in range(DK):
                        last = pool.tensor_tensor(kd[:, n, c], k[:, n, c].unsqueeze(1).to_broadcast([128, 8, SEQ]),
                                                  mask.unsqueeze(2).to_broadcast([128, 8, SEQ]), ALU.mult)
                    last.then_inc(kd_ready, 1)
                    pool.wait_ge(q_sb, t + 1)
                    for c in range(DK):
                        last = pool.tensor_tensor(
                            qd[:, n, c, :, :, 0:REM].rearrange("p u a t -> p (u a) t"),
                            q[:, n, c, MAIN:SEQ].unsqueeze(1).to_broadcast([128, 8, REM]),
                            mask.unsqueeze(2).to_broadcast([128, 8, REM]), ALU.mult)
                    last.then_inc(qd_ready, 1)

                with pool.Fori(0, B // 2) as i:
                    for n in range(2):
                        split_heads(i * 2 + n, n)

            @block.scalar
            def _(act):
                act.sem_inc(exps_done, 2)
                act.sem_inc(o_norm, 2)
                act.sem_inc(oT_done, 2)

                def keep_latents(t):
                    act.wait_ge(lat_ps, t + 1)
                    act.copy(lat[:], ps[:, KB, 0:SEQ])
                    act.copy(lat3[LAT:128], ps[LAT:128, KB, MAIN:SEQ].unsqueeze(2).to_broadcast([LAT, REM, 3]))\
                       .then_inc(lat_sb, 1)

                def keep_q(t, n):
                    act.wait_ge(q_ps, t + 1)
                    act.copy(q[:, n], ps[:, QB, 0:DK * SEQ].rearrange("p (c t) -> p c t", c=DK)).then_inc(q_sb, 1)

                def out_back(t):
                    act.wait_ge(oT_ready, t + 1)
                    act.copy(m.xT[:, :, bass.ds(t * SEQ, MAIN)],
                             ps[:, KB, 0:256].rearrange("p (a t) -> p a t", a=2))
                    for ab in range(2):
                        c0 = 256 + ab * (128 + REM_B)
                        last = act.copy(m.xT[:, ab, bass.ds(t * SEQ + MAIN, REM)], ps[:, KB, c0:c0 + REM])
                    last.then_inc(oT_done, 1)

                def step(t, n, first, last):
                    for u in range(NU):
                        act.wait_ge(max_ready, t * NU + u + 1)
                        for s in range(3):
                            x = act.activation(p[:, u % 2, :, s], ps[:, S + u % 2, s * SEQ:(s + 1) * SEQ], ACT.Exp,
                                               bias=nmax[:, u % 2, s:s + 1])
                        x.then_inc(exps_done, 1)
                        if u == 0 and not last:
                            keep_latents(t + 1)
                        if u == 1 and not last:
                            keep_q(t + 1, 1 - n)
                        if u == 6 and not first:
                            out_back(t - 1)

                keep_latents(0)
                keep_q(0, 0)
                turns(act, step)
                out_back(B - 1)


def project0_and_norm(nc, sem, m, d):
    y_ready = sem("wo_ready")
    ps = m.ps

    def on_sync(sp, h_ready, xn_ready):
        sp.dma_start(m.w_red[:], d["w_red"].rearrange("(c p) n -> p c n", p=128)).then_inc(m.w_red_in, 16)
        for e in range(E):
            sp.dma_start(m.w2[:, e], d["w2"][e].rearrange("(c p) n -> p c n", p=128)).then_inc(m.expert_in, 16)

    def source_pe(pe, t, h_ready):
        if t >= 2:
            pe.wait_ge(h_ready, t - 1)
        for c in range(DK):
            last = pe.matmul(ps[0:TP, t % 2, 0:D], m.xT[:, c, t * TP:(t + 1) * TP], m.wo[:, c, :],
                             start=(c == 0), stop=(c == DK - 1))
        last.then_inc(y_ready, 1)

    def source(dve, t, h_ready):
        dve.wait_ge(y_ready, t + 1)
        dve.tensor_tensor(m.h[:, t, :], m.h[:, t, :], ps[0:TP, t % 2, 0:D], ALU.add).then_inc(h_ready, 1)

    def use_pe(pe, t):
        if t == 0:
            pe.wait_ge(m.w_red_in, 16)
        for c in range(DK):
            pe.matmul(ps[0:TP, RB, t * GD:(t + 1) * GD], m.xT[:, c, t * TP:(t + 1) * TP], m.w_red[:, c, :],
                      start=(c == 0), stop=(c == DK - 1))

    normalise(nc, sem, m, "_1", source, source_pe, use_pe, on_sync)


def combine0_and_norm(nc, sem, m):
    gathered = [sem(f"c0_gathered_{g}") for g in range(len(GROUPS))]

    def on_pool(pool):
        for g, tiles in enumerate(GROUPS):
            for t in tiles:
                pool.indirect_dma_start(m.back[:, t, :], None, m.ys,
                                        bass.IndirectOffsetOnAxis(m.slot[:, t:t + 1], 0)).then_inc(gathered[g], 16)

    def source(dve, t, h_ready):
        g = next(g for g, tiles in enumerate(GROUPS) if t in tiles)
        if t == GROUPS[g].start:
            dve.wait_ge(gathered[g], 16 * len(GROUPS[g]))
        dve.scalar_tensor_tensor(m.h[:, t, :], m.back[:, t, :], m.gate[:, t:t + 1], m.h[:, t, :],
                                 ALU.mult, ALU.add).then_inc(h_ready, 1)

    normalise(nc, sem, m, "_2", source=source, on_pool=on_pool)


def norm_and_router1(nc, sem, m, d, out):
    def on_sync(sp, h_ready, xn_ready):
        sp.dma_start(m.rw[:], d["router_w"].rearrange("(c p) n -> p c n", p=128)).then_inc(m.router_in, 16)
        sp.dma_start(m.rb[:], d["router_b"].to_broadcast([TP, E])).then_inc(m.router_in, 16)
        sp.dma_start(out.rearrange("(t p) d -> p t d", p=TP), m.h[:]).then_inc(m.rows_out, 16)
        for tiles in GROUPS:
            sp.wait_ge(xn_ready, tiles.stop)
            sp.dma_start(m.xrows.rearrange("(t p) d -> p t d", p=TP)[:, tiles.start:tiles.stop],
                         m.xn[:, tiles.start:tiles.stop]).then_inc(m.rows_out, 16)

    def use_pe(pe, t):
        if t == 0:
            pe.wait_ge(m.router_in, 32)
        for c in range(DK):
            pe.matmul(ps[0:TP, RB, t * E:(t + 1) * E], m.xT[:, c, t * TP:(t + 1) * TP], m.rw[:, c, :],
                      start=(c == 0), stop=(c == DK - 1))

    ps = m.ps
    normalise(nc, sem, m, "_3", use_pe=use_pe, on_sync=on_sync)


def build(nc, d, out, upto=99):
    with ExitStack() as ctx:
        def sb(name, shape, dt=F32):
            return ctx.enter_context(nc.sbuf_tensor(name, shape, dt))

        def kept(name):
            return ctx.enter_context(nc.semaphore(name))

        stage_sems = []

        def sem(name):
            handle = nc.alloc_semaphore(name)
            stage_sems.append(handle)
            return handle

        m = Mem()
        m.ps = ctx.enter_context(nc.psum_tensor("psum", [128, 8, 512], F32))
        m.h0 = nc.dram_tensor("h0", [TOK, D], F32).ap()
        m.xs = nc.dram_tensor("expert_rows", [SLOTS, D], F32).ap()
        m.ident = sb("ident", [128, 128])
        m.h = sb("h", [TP, NT, D])
        m.xT = sb("xT", [128, DK, TOK])
        m.xn = None
        m.zero_out = kept("zero_out")
        m.attn_in, m.expert_in = kept("attn_in"), kept("expert_in")
        m.h_in, m.h_want = [kept(f"h_in_{g}") for g in range(len(GROUPS))], 16
        m.w1 = sb("w1", [128, E, DK, F])
        m.expert_loads = [(m.w1[:, e], d["w1"][e].rearrange("(c p) f -> p c f", p=128)) for e in range(E)]
        if True:
            m.wo = sb("wo", [128, DK, D])
            with ExitStack() as bctx:
                def bsb(name, shape, dt=F32):
                    return bctx.enter_context(nc.sbuf_tensor(name, shape, dt))
                m.wq = bsb("wq", [128, DK, D])
                m.wlat = bsb("wlat", [128, DK, 128])
                m.wkb = bsb("wkb", [128, D])
                m.wvb = bsb("wvb", [128, D])
                m.rem_mask = bsb("rem_mask", [128, 4])
                m.head_mask = bsb("head_mask", [128, 8])
                m.attn_loads = [
                    (m.wq[:], d["wq"].rearrange("(c p) n -> p c n", p=128)),
                    (m.wlat[:], d["wlat"].rearrange("(c p) n -> p c n", p=128)),
                    (m.wkb[0:LAT], d["wkb"]), (m.wvb[LAT:128], d["wvb"]),
                    (m.rem_mask[:], d["rem_mask"]), (m.head_mask[:], d["head_mask"]),
                    (m.wo[:], d["wo"].rearrange("(c p) n -> p c n", p=128)),
                ]
                with ExitStack() as cctx:
                    def csb(name, shape, dt=F32):
                        return cctx.enter_context(nc.sbuf_tensor(name, shape, dt))
                    m.wq_swap = csb("wq_swap", [128, DK, D])
                    m.wkb_swap = csb("wkb_swap", [128, D])
                    m.rot_cos = csb("rot_cos", [128, 2, D])
                    m.rot_sin = csb("rot_sin", [128, 2, D])
                    m.attn_loads += [
                        (m.wq_swap[:], d["wq_swap"].rearrange("(c p) n -> p c n", p=128)),
                        (m.wkb_swap[0:LAT], d["wkb_swap"]),
                        (m.rot_cos[:], d["rot_cos"].unsqueeze(0).to_broadcast([128, 2, D])),
                        (m.rot_sin[:], d["rot_sin"].unsqueeze(0).to_broadcast([128, 2, D]))]
                    m.attn_want = 16 * len(m.attn_loads)
                    tokenise(nc, sem, m, d)
                with nc.sbuf_tensor("xn_0", [TP, NT, D], F32) as xn:
                    m.xn = xn
                    normalise(nc, sem, m, "_0")
                attend0(nc, sem, m, d)
            m.w2 = sb("w2", [128, E, FK, D])
        m.ys = nc.dram_tensor("expert_outs", [SLOTS, D], F32).ap()
        m.relv = nc.dram_tensor("rel_values", [128, 512], F32).ap()
        m.xrows = nc.dram_tensor("normed_rows", [TOK, D], F32).ap()
        m.ring_in = [kept("expert1_in_0"), kept("expert1_in_1")]
        m.w_red_in, m.router_in, m.rows_out = kept("w_red_in"), kept("router_in"), kept("rows_out")

        def room(w):
            return w[0:TP, 2:].rearrange("p e c f -> p (e c f)")[:, 0:NT * D].rearrange("p (t n) -> p t n", n=D)

        with ExitStack() as ectx:
            def esb(name, shape, dt=F32):
                return ectx.enter_context(nc.sbuf_tensor(name, shape, dt))
            m.gate = esb("gate", [TP, NT])
            m.slot = esb("slot", [TP, NT], I32)
            m.tile_expert = esb("tile_expert", [1, SLOT_TILES], I32)
            m.w_red = esb("w_red", [128, DK, GD])
            with nc.sbuf_tensor("xn_1", [TP, NT, D], F32) as xn:
                m.xn = xn
                project0_and_norm(nc, sem, m, d)
                route0(nc, sem, esb, m, d)
            experts0(nc, sem, m, d)
            nc.clear_and_free_semaphores(stage_sems)
            nc.all_engine_barrier()
            stage_sems.clear()
            m.xn, m.back = room(m.w1), room(m.w2)
            combine0_and_norm(nc, sem, m)
        attend1(nc, sem, m, d)
        m.score = sb("score", [TP, NT, E])
        m.gate1 = sb("gate1", [128, E * 4])
        m.row1 = sb("row1", [128, E * 4], I32)
        m.rw = sb("router_w", [128, DK, E])
        m.rb = sb("router_b", [TP, E])
        norm_and_router1(nc, sem, m, d, out)
        scores1(nc, sem, m)
        choose1(nc, sem, m, d)
        experts1(nc, sem, m, d, out)


def route0(nc, sem, sb, m, d):
    with ExitStack() as ctx:
        def tmp(name, shape, dt=F32):
            return ctx.enter_context(nc.sbuf_tensor(name, shape, dt))

        wg = tmp("wg", [E, GD])
        wg2 = tmp("wg_squares", [E, GD])
        wgs = tmp("wg_norm", [E, 4])
        wgT = tmp("wg_T", [GD, E])
        red = tmp("reduced", [TP, NT * GD])
        redT = tmp("reduced_T", [128, 3, TP])
        spread = tmp("spread16", [GD, 128])
        diag = tmp("diag_mask", [128, 8, E])
        wgd = tmp("wg_diag", [128, 8, E])
        iota8 = tmp("iota8", [TP, E])
        rows128 = tmp("rows128", [TP, 21])
        tiles_j = tmp("tiles_j", [1, SLOT_TILES])
        keep = tmp("scan_keep", [TP, E, NT])
        before = tmp("before", [TP, TP])
        ones = tmp("ones_tp", [TP, TP])
        lg = tmp("logits", [TP, NT, E])
        mx = tmp("logit_max", [TP, NT])
        z = tmp("shifted", [TP, NT, E])
        eq = tmp("is_max", [TP, NT, E])
        first = tmp("first_max", [TP, NT])
        oh = tmp("one_hot", [TP, NT, E])
        cs = tmp("tile_counts", [TP, E, NT])
        incl = tmp("counts_incl", [TP, E, NT])
        big = tmp("over_128j", [TP, E, 21])
        ntile = tmp("expert_tiles", [TP, E])
        cumt = tmp("expert_tiles_incl", [TP, E])
        base = tmp("expert_base", [TP, E])
        rank = z
        slotf = tmp("slot_f", [TP, NT])
        past = tmp("past_expert", [1, SLOT_TILES, E])
        ejf = tmp("tile_expert_f", [1, SLOT_TILES])

        tabs_in, wg8_ps, wgd_sb = sem("r0_tabs_in"), sem("r0_wg8_ps"), sem("r0_wgd_sb")
        red_ps, red_sb, lg_ps, wg_ps, rank_ps, cnt_ps = (
            sem("r0_" + n) for n in ("red_ps", "red_sb", "lg_ps", "wg_ps", "rank_ps", "cnt_ps"))
        wgsq, wgsum, wgrt, wgmx, wgrc, wgn, wgT_sb = (
            sem("r0_" + n) for n in ("wgsq", "wgsum", "wgrt", "wgmx", "wgrc", "wgn", "wgT"))
        step, exps, slots_ready, scattered = sem("r0_step"), sem("r0_exps"), sem("r0_slots"), sem("r0_scattered")
        ps = m.ps
        with nc.Block() as block:
            @block.sync
            def _(sp):
                loads = [(wg[:], d["wg"]),
                         (iota8[:], d["iota8"].to_broadcast([TP, E])),
                         (rows128[:], d["rows128"].to_broadcast([TP, 21])),
                         (tiles_j[:], d["tiles_j"]), (keep[:], d["keep"].unsqueeze(0).to_broadcast([TP, E, NT])),
                         (before[:], d["before"]), (spread[:], d["spread16"]), (diag[:], d["diag_mask"])]
                for dst, src in loads:
                    sp.dma_start(dst, src).then_inc(tabs_in, 16)

            @block.tensor
            def _(pe):
                pe.wait_ge(tabs_in, 16 * 8)
                pe.wait_ge(wgn, 1)
                pe.transpose(ps[0:GD, 7, 0:E], wg2[:], m.ident[0:E, 0:E]).then_inc(wg_ps, 1)
                pe.wait_ge(wgT_sb, 1)
                pe.matmul(ps[:, 7, 64:64 + E], spread[:], wgT[:], start=True, stop=True).then_inc(wg8_ps, 1)
                pe.wait_ge(red_sb, 1)
                groups = [(g, min(8, NT - 8 * g)) for g in range(3)]
                for g, n in groups:
                    last = pe.transpose(ps[0:n * GD, 1, g * TP:(g + 1) * TP], red[:, g * 128:g * 128 + n * GD],
                                        m.ident[0:TP, 0:TP])
                last.then_inc(red_ps, 1)
                pe.wait_ge(red_sb, 2)
                pe.wait_ge(wgd_sb, 1)
                for g, n in groups:
                    last = pe.matmul(ps[0:TP, 2, g * 64:g * 64 + n * E], redT[0:n * GD, g, :],
                                     wgd[0:n * GD].rearrange("p t e -> p (t e)")[:, 0:n * E], start=True, stop=True)
                last.then_inc(lg_ps, 1)
                pe.wait_ge(step, 6)
                oh_f = oh[:].rearrange("p t e -> p (t e)")
                pe.matmul(ps[0:TP, 3, 0:NT * E], ones[:], oh_f, start=True, stop=True).then_inc(cnt_ps, 1)
                pe.matmul(ps[0:TP, 4, 0:NT * E], before[:], oh_f, start=True, stop=True).then_inc(rank_ps, 1)

            @block.scalar
            def _(act):
                act.wait_ge(wgsum, 1)
                act.activation(wgs[:, 1:2], wgs[:, 0:1], ACT.Sqrt).then_inc(wgrt, 1)
                act.copy(red[:], ps[0:TP, RB, 0:NT * GD]).then_inc(red_sb, 1)
                act.wait_ge(red_ps, 1)
                act.copy(redT[:], ps[:, 1, 0:3 * TP].rearrange("p (g t) -> p g t", g=3)).then_inc(red_sb, 1)
                act.wait_ge(step, 2)
                act.activation(z[:], z[:], ACT.Exp).then_inc(exps, 1)

            @block.vector
            def _(dve):
                dve.memset(ones[:], 1.0)
                dve.wait_ge(tabs_in, 16 * 8)
                dve.tensor_tensor(wg2[:], wg[:], wg[:], ALU.mult).then_inc(wgsq, 1)
                dve.wait_ge(wgsq, 1)
                dve.tensor_reduce(wgs[:, 0:1], wg2[:], AX.X, ALU.add).then_inc(wgsum, 1)
                dve.wait_ge(wgrt, 1)
                dve.tensor_scalar(wgs[:, 2:3], wgs[:, 1:2], 1e-4, None, ALU.max).then_inc(wgmx, 1)
                dve.wait_ge(wgmx, 1)
                dve.reciprocal(wgs[:, 3:4], wgs[:, 2:3]).then_inc(wgrc, 1)
                dve.wait_ge(wgrc, 1)
                dve.tensor_scalar(wg2[:], wg[:], wgs[:, 3:4], None, ALU.mult).then_inc(wgn, 1)
                dve.wait_ge(wg_ps, 1)
                dve.tensor_copy(wgT[:], ps[0:GD, 7, 0:E]).then_inc(wgT_sb, 1)
                dve.wait_ge(wg8_ps, 1)
                dve.tensor_tensor(wgd[:], ps[:, 7, 64:64 + E].unsqueeze(1).to_broadcast([128, 8, E]), diag[:],
                                  ALU.mult).then_inc(wgd_sb, 1)

                def over(a):
                    return a.unsqueeze(2).to_broadcast([TP, NT, E])

                dve.wait_ge(lg_ps, 1)
                lps = ps[0:TP, 2, 0:NT * E].rearrange("p (t e) -> p t e", e=E)
                dve.tensor_reduce(mx[:], lps, AX.X, ALU.max).then_inc(step, 1)
                dve.wait_ge(step, 1)
                dve.tensor_tensor(z[:], lps, over(mx[:]), ALU.subtract).then_inc(step, 1)
                dve.tensor_tensor(eq[:], lps, over(mx[:]), ALU.is_equal).then_inc(step, 1)
                dve.wait_ge(step, 3)
                i8 = iota8[:].unsqueeze(1).to_broadcast([TP, NT, E])
                dve.tensor_tensor(eq[:], eq[:], i8, ALU.mult).then_inc(step, 1)
                dve.wait_ge(step, 4)
                dve.tensor_reduce(first[:], eq[:], AX.X, ALU.min).then_inc(step, 1)
                dve.wait_ge(step, 5)
                dve.tensor_tensor(oh[:], over(first[:]), i8, ALU.is_equal).then_inc(step, 1)
                dve.wait_ge(exps, 1)
                dve.tensor_reduce(mx[:], z[:], AX.X, ALU.add).then_inc(step, 1)
                dve.wait_ge(step, 7)
                dve.reciprocal(m.gate[:], mx[:]).then_inc(step, 1)
                dve.wait_ge(cnt_ps, 1)
                dve.tensor_copy(cs[:], ps[0:TP, 3, 0:NT * E].rearrange("p (t e) -> p e t", e=E)).then_inc(step, 1)
                dve.wait_ge(step, 9)
                dve.tensor_tensor_scan(incl[:].rearrange("p e t -> p (e t)"), keep[:].rearrange("p e t -> p (e t)"),
                                       cs[:].rearrange("p e t -> p (e t)"), 0.0, ALU.mult, ALU.add).then_inc(step, 1)
                dve.wait_ge(step, 10)
                dve.tensor_tensor(big[:], incl[:, :, NT - 1].unsqueeze(2).to_broadcast([TP, E, 21]),
                                  rows128[:].unsqueeze(1).to_broadcast([TP, E, 21]), ALU.is_gt).then_inc(step, 1)
                dve.tensor_tensor(cs[:], incl[:], cs[:], ALU.subtract).then_inc(step, 1)
                dve.wait_ge(step, 12)
                dve.tensor_reduce(ntile[:], big[:], AX.X, ALU.add).then_inc(step, 1)
                dve.wait_ge(step, 13)
                dve.tensor_tensor_scan(cumt[:], ones[:, 0:E], ntile[:], 0.0, ALU.mult, ALU.add).then_inc(step, 1)
                dve.wait_ge(step, 14)
                dve.tensor_tensor(base[:], cumt[:], ntile[:], ALU.subtract).then_inc(step, 1)
                dve.wait_ge(step, 15)
                dve.tensor_scalar(base[:], base[:], float(SLOT), None, ALU.mult).then_inc(step, 1)
                dve.wait_ge(rank_ps, 1)
                dve.tensor_tensor(rank[:], ps[0:TP, 4, 0:NT * E].rearrange("p (t e) -> p t e", e=E),
                                  cs[:].rearrange("p e t -> p t e"), ALU.add).then_inc(step, 1)
                dve.wait_ge(step, 17)
                dve.tensor_tensor(rank[:], rank[:], base[:].unsqueeze(1).to_broadcast([TP, NT, E]), ALU.add)\
                   .then_inc(step, 1)
                dve.wait_ge(step, 18)
                dve.tensor_tensor(rank[:], rank[:], oh[:], ALU.mult).then_inc(step, 1)
                dve.wait_ge(step, 19)
                dve.tensor_reduce(slotf[:], rank[:], AX.X, ALU.add).then_inc(step, 1)
                dve.wait_ge(step, 20)
                dve.tensor_copy(m.slot[:], slotf[:]).then_inc(slots_ready, 1)
                dve.tensor_tensor(past[:], tiles_j[:].unsqueeze(2).to_broadcast([1, SLOT_TILES, E]),
                                  cumt[0:1, :].unsqueeze(1).to_broadcast([1, SLOT_TILES, E]), ALU.is_ge).then_inc(step, 1)
                dve.wait_ge(step, 21)
                dve.tensor_reduce(ejf[:], past[:], AX.X, ALU.add).then_inc(step, 1)
                dve.wait_ge(step, 22)
                dve.tensor_scalar(m.tile_expert[:], ejf[:], float(E - 1), None, ALU.min)

            @block.gpsimd
            def _(pool):
                pool.wait_ge(slots_ready, 1)
                pool.wait_ge(m.zero_out, 16)
                for t in range(NT):
                    pool.indirect_dma_start(m.xs, bass.IndirectOffsetOnAxis(m.slot[:, t:t + 1], 0),
                                            m.xn[:, t, :], None).then_inc(scattered, 16)
                pool.wait_ge(scattered, 16 * NT)


def experts0(nc, sem, m, d):
    with ExitStack() as ctx:
        def tmp(name, shape, dt=F32):
            return ctx.enter_context(nc.sbuf_tensor(name, shape, dt))

        b1T = tmp("b1T", [128, E * FK])
        b2 = tmp("b2", [128, E, D])
        b_in = sem("e0_b_in")
        x = tmp("e0_x", [128, 2, D])
        xT = tmp("e0_xT", [128, 2, DK, SLOT])
        u = tmp("e0_u", [128, F])
        hT = tmp("e0_hT", [128, FK, SLOT])
        y = tmp("e0_y", [128, 2, D])
        x_in, y_out = [sem("e0_x_in_0"), sem("e0_x_in_1")], sem("e0_y_out")
        xp_ready, xT_ready, u_ready, u_sb, up_ready, hT_ready, y_ready, y_sb = (
            sem("e0_" + n) for n in ("xp", "xT", "u", "u_sb", "up", "hT", "y", "y_sb"))
        ps = m.ps
        XB, UB, TB, YB = 0, 1, 3, 5
        xs_t = m.xs.rearrange("(t p) d -> p t d", p=SLOT)
        ys_t = m.ys.rearrange("(t p) d -> p t d", p=SLOT)
        LOOPS = (SLOT_TILES - 2) // 2
        assert SLOT_TILES % 2 == 0

        def expert_of(eng, j):
            return eng.value_load(m.tile_expert[0:1, bass.ds(j, 1)], min_val=0, max_val=E - 1)

        with nc.Block() as block:
            @block.sync
            def _(sp):
                sp.dma_start(b1T[:], d["b1T"]).then_inc(b_in, 16)
                sp.dma_start(b2[:], d["b2"].unsqueeze(0).to_broadcast([128, E, D])).then_inc(b_in, 16)
                for n in range(2):
                    sp.dma_start(x[:, n:n + 1, :], xs_t[:, n:n + 1, :]).then_inc(x_in[n], 16)
                with sp.Fori(0, SLOT_TILES // 2 - 1) as i:
                    for n in range(2):
                        sp.wait_ge(xp_ready, i * 2 + n + 1)
                        sp.dma_start(x[:, n:n + 1, :], xs_t[:, bass.ds(i * 2 + n + 2, 1), :]).then_inc(x_in[n], 16)

            @block.tensor
            def _(pe):
                w1f = m.w1[:].rearrange("p e c f -> p (e c f)")
                w2f = m.w2[:].rearrange("p e c f -> p (e c f)")

                def turn_x(j, n, loads):
                    pe.wait_ge(x_in[n], loads * 16)
                    for c in range(DK):
                        last = pe.transpose(ps[:, XB, c * 128:(c + 1) * 128], x[:, n, c * 128:(c + 1) * 128],
                                            m.ident[:])
                    last.then_inc(xp_ready, 1)

                def up(j, n):
                    e = expert_of(pe, j)
                    pe.wait_ge(xT_ready, j + 1)
                    for f in range(2):
                        for c in range(DK):
                            last = pe.matmul(ps[:, UB + f, :], xT[:, n, c, :],
                                             w1f[:, bass.ds(e * (DK * F) + c * F + f * 512, 512)],
                                             start=(c == 0), stop=(c == DK - 1))
                        last.then_inc(u_ready, 1)

                def turn_u(j):
                    for f in range(2):
                        pe.wait_ge(u_sb, j * 2 + f + 1)
                        for c in range(4):
                            last = pe.transpose(ps[:, TB + f, c * 128:(c + 1) * 128],
                                                u[:, f * 512 + c * 128:f * 512 + (c + 1) * 128], m.ident[:])
                        last.then_inc(up_ready, 1)

                def down(j, n):
                    e = expert_of(pe, j)
                    pe.wait_ge(hT_ready, j * 2 + 2)
                    pe.wait_ge(y_sb, j + 1)
                    for c in range(FK):
                        last = pe.matmul(ps[:, YB + n, 0:D], hT[:, c, :],
                                         w2f[:, bass.ds(e * (FK * D) + c * D, D)],
                                         start=(c == 0), stop=(c == FK - 1))
                    last.then_inc(y_ready, 1)

                def step(j, n, loads, more):
                    up(j, n)
                    down(j - 1, 1 - n)
                    if more:
                        turn_x(j + 1, 1 - n, loads)
                    turn_u(j)

                pe.wait_ge(m.expert_in, 32 * E)
                turn_x(0, 0, 1)
                up(0, 0)
                turn_x(1, 1, 1)
                turn_u(0)
                with pe.Fori(0, LOOPS) as i:
                    step(i * 2 + 1, 1, i + 2, True)
                    step(i * 2 + 2, 0, i + 2, True)
                step(SLOT_TILES - 1, 1, 0, False)
                down(SLOT_TILES - 1, 1)

            @block.scalar
            def _(act):
                act.sem_inc(y_sb, 2)
                act.wait_ge(b_in, 32)

                def tile(j):
                    e = expert_of(act, j)
                    for f in range(2):
                        act.wait_ge(up_ready, j * 2 + f + 1)
                        for c in range(4):
                            last = act.activation(hT[:, f * 4 + c, :], ps[:, TB + f, c * 128:(c + 1) * 128],
                                                  ACT.Gelu, bias=b1T[:, bass.ds(e * FK + f * 4 + c, 1)])
                        last.then_inc(hT_ready, 1)

                with act.Fori(0, SLOT_TILES // 4) as i:
                    for n in range(4):
                        tile(i * 4 + n)

            @block.vector
            def _(dve):
                dve.wait_ge(b_in, 32)

                def turned_x(n, count):
                    dve.wait_ge(xp_ready, count)
                    dve.tensor_copy(xT[:, n], ps[:, XB, 0:256].rearrange("p (c t) -> p c t", c=DK)).then_inc(xT_ready, 1)

                def hidden(j):
                    for f in range(2):
                        dve.wait_ge(u_ready, j * 2 + f + 1)
                        dve.tensor_copy(u[:, f * 512:(f + 1) * 512], ps[:, UB + f, :]).then_inc(u_sb, 1)

                def finish(j, n, stored):
                    e = expert_of(dve, j)
                    dve.wait_ge(y_ready, j + 1)
                    if stored is not None:
                        dve.wait_ge(y_out, stored)
                    dve.tensor_tensor(y[:, n:n + 1, :], ps[:, YB + n, 0:D].unsqueeze(1), b2[:, bass.ds(e, 1), :],
                                      ALU.add).then_inc(y_sb, 1)

                turned_x(0, 1)
                hidden(0)
                turned_x(1, 2)
                hidden(1)
                finish(0, 0, None)
                turned_x(0, 3)
                hidden(2)
                finish(1, 1, None)
                turned_x(1, 4)
                with dve.Fori(1, LOOPS) as i:
                    for n in range(2):
                        j = i * 2 + 1 + n
                        hidden(j)
                        finish(j - 1, n, i * 32)
                        turned_x(n, j + 2)
                hidden(SLOT_TILES - 1)
                finish(SLOT_TILES - 2, 0, 16 * (SLOT_TILES - 2))
                finish(SLOT_TILES - 1, 1, 16 * (SLOT_TILES - 2))

            @block.gpsimd
            def _(pool):
                with pool.Fori(0, SLOT_TILES // 2) as i:
                    for n in range(2):
                        pool.wait_ge(y_sb, i * 2 + n + 3)
                        pool.dma_start(ys_t[:, bass.ds(i * 2 + n, 1), :], y[:, n:n + 1, :]).then_inc(y_out, 16)
                pool.wait_ge(y_out, 16 * SLOT_TILES)


def attend1(nc, sem, m, d):
    with ExitStack() as ctx:
        def sb(name, shape, dt=F32):
            return ctx.enter_context(nc.sbuf_tensor(name, shape, dt))

        PAIRS = B // 2
        W = PAIR + REM
        wqk = sb("a1_wqk", [128, DK, 128])
        wv = sb("a1_wv", [128, DK, D])
        cst = sb("a1_cst", [128, 5])
        bv = sb("a1_bv", [128, D])
        rel1 = sb("a1_rel1", [32, 1])
        rel = sb("a1_rel", [32, 128])
        buckets = sb("a1_buckets", [32, 512])
        relv = sb("a1_relv", [128, 512])
        mask = sb("a1_mask", [128, W])
        bias = sb("a1_bias", [128, W])
        xr = sb("a1_x_rem", [128, 2, DK, 2, 64])
        qk = sb("a1_qk", [128, 2, PAIR])
        y = sb("a1_y", [128, 2, W])
        z = sb("a1_y_is_zero", [128, 2, W])
        r = sb("a1_recip", [128, 2, W])
        gl = sb("a1_gelu", [128, 2, W])
        at = sb("a1_attn", [128, 2, W])
        room1 = m.w1[:, 2:].rearrange("p e c f -> p (e c f)")
        room2 = m.w2[:, 2:].rearrange("p e c f -> p (e c f)")
        q, k = room1[:, 0:TOK], room1[:, TOK:2 * TOK]
        v = room2[:, 0:PAIRS * 3 * D].rearrange("p (i s n) -> p i s n", i=PAIRS, s=3)

        names = ("w_in zero rel_wide rel_ps rel_sb rel_out bias_in bias_sc x_rem qk_ps qk_sb q_sb k_sb v_ps v_sum v_sb "
                 "s_ps y_raw y_zero y_sb recip masked gelu attn o_ps o_sb turned added").split()
        (w_in, zero, rel_wide, rel_ps, rel_sb, rel_out, bias_in, bias_sc, x_rem, qk_ps, qk_sb, q_sb, k_sb, v_ps, v_sum,
         v_sb, s_ps, y_raw, y_zero, y_sb, recip, masked, gelu, attn, o_ps, o_sb, turned, added) = (
            sem("a1_" + n) for n in names)
        ps = m.ps
        QB, VB = 0, 2
        TB, OB, SB = 0, 2, 6
        REL = 7
        STD = float(np.sqrt(0.25 * np.pi))
        MU = float(np.sqrt(0.5))

        def tiles_of(p):
            return range(p * PAIR // TP, (p + 1) * PAIR // TP)

        with nc.Block() as block:
            @block.sync
            def _(sp):
                loads = [(wqk[:], d["wqk"].rearrange("(c p) n -> p c n", p=128)),
                         (wv[:], d["wv"].rearrange("(c p) n -> p c n", p=128)), (cst[:], d["a1_cst"]),
                         (bv[:], d["bv"].to_broadcast([128, D])), (rel1[:], d["rel_emb"]),
                         (buckets[:], d["buckets"]), (mask[:], d["mask1"])]
                for dst, src in loads:
                    sp.dma_start(dst, src).then_inc(w_in, 16)
                sp.wait_ge(rel_sb, 1)
                sp.dma_start(m.relv, relv[:]).then_inc(rel_out, 16)
                sp.wait_ge(rel_out, 16)
                def strip(rows, cols):
                    return bass.AP(m.relv.tensor, m.relv.offset + SEQ - 1, [[511, rows], [1, cols]])
                sp.wait_ge(zero, 2)
                for b in range(2):
                    sp.dma_start(bias[:, b * SEQ:(b + 1) * SEQ], strip(128, SEQ)).then_inc(bias_in, 16)
                    sp.dma_start(bias[64 * b:64 * b + REM, PAIR:W], strip(REM, REM)).then_inc(bias_in, 16)
                for e in range(2):
                    sp.dma_start(m.w1[:, e], d["w1_1"][e].rearrange("(c p) f -> p c f", p=128)).then_inc(m.ring_in[e], 16)
                    sp.dma_start(m.w2[:, e], d["w2_1"][e].rearrange("(c p) n -> p c n", p=128)).then_inc(m.ring_in[e], 16)

            @block.tensor
            def _(pe):
                pe.wait_ge(w_in, 16 * 7)
                pe.wait_ge(rel_wide, 1)
                pe.matmul(ps[:, REL, :], rel[:], buckets[:], start=True, stop=True).then_inc(rel_ps, 1)
                for p in range(PAIRS):
                    if p >= 2:
                        pe.wait_ge(qk_sb, p - 1)
                    for c in range(DK):
                        last = pe.matmul(ps[:, QB + p % 2, 0:PAIR], wqk[:, c, :], m.xT[:, c, p * PAIR:(p + 1) * PAIR],
                                         start=(c == 0), stop=(c == DK - 1))
                    last.then_inc(qk_ps, 1)
                    if p >= 2:
                        pe.wait_ge(v_sum, p - 1)
                    bank = VB + 2 * (p % 2)
                    for b in range(2):
                        o = (2 * p + b) * SEQ
                        for c in range(DK):
                            pe.matmul(ps[:, bank, b * D:(b + 1) * D], m.xT[:, c, o:o + MAIN], wv[:, c, :],
                                      start=(c == 0), stop=(c == DK - 1))
                    pe.wait_ge(x_rem, p + 1)
                    for c in range(DK):
                        last = pe.matmul(ps[:, bank + 1, 0:D], xr[:, p % 2, c].rearrange("p b t -> p (b t)"), wv[:, c, :],
                                         start=(c == 0), stop=(c == DK - 1))
                    last.then_inc(v_ps, 1)

                def scores(p):
                    if p >= 2:
                        pe.wait_ge(y_raw, p - 1)
                    for b in range(2):
                        o = (2 * p + b) * SEQ
                        pe.matmul(ps[:, SB + p % 2, b * SEQ:(b + 1) * SEQ], k[:, o:o + MAIN], q[:, o:o + SEQ],
                                  start=True, stop=True)
                    for b in range(2):
                        o = (2 * p + b) * SEQ
                        last = pe.matmul(ps[64 * b:64 * b + REM, SB + p % 2, PAIR:W], k[:, o + MAIN:o + SEQ],
                                         q[:, o + MAIN:o + SEQ], start=True, stop=True)
                    last.then_inc(s_ps, 1)

                def weigh_values(p):
                    pe.wait_ge(attn, p + 1)
                    if p >= 2:
                        pe.wait_ge(o_sb, p - 1)
                    for b in range(2):
                        bank = OB + 2 * (p % 2) + b
                        rows = slice(64 * b, 64 * b + REM)
                        for c in range(DK):
                            pe.matmul(ps[:, bank, c * SEQ:(c + 1) * SEQ], v[:, p, b, c * 128:(c + 1) * 128],
                                      at[:, p % 2, b * SEQ:(b + 1) * SEQ], start=True, stop=False, skip_group_check=True)
                            last = pe.matmul(ps[:, bank, c * SEQ + MAIN:(c + 1) * SEQ], v[rows, p, 2, c * 128:(c + 1) * 128],
                                             at[rows, p % 2, PAIR:W], start=False, stop=True, skip_group_check=True)
                    last.then_inc(o_ps, 1)

                def turn_back(p):
                    pe.wait_ge(o_sb, p + 1)
                    for t in tiles_of(p):
                        if t >= 2:
                            pe.wait_ge(added, t - 1)
                        for c in range(DK):
                            last = pe.transpose(ps[0:TP, TB + t % 2, c * 128:(c + 1) * 128],
                                                m.xT[:, c, t * TP:(t + 1) * TP], m.ident[:])
                        last.then_inc(turned, 1)

                pe.wait_ge(q_sb, PAIRS)
                pe.wait_ge(k_sb, PAIRS)
                pe.wait_ge(v_sb, PAIRS)
                scores(0)
                scores(1)
                for p in range(PAIRS):
                    if p + 2 < PAIRS:
                        scores(p + 2)
                    if p >= 2:
                        turn_back(p - 2)
                    if p >= 1:
                        weigh_values(p - 1)
                turn_back(PAIRS - 2)
                weigh_values(PAIRS - 1)
                turn_back(PAIRS - 1)

            @block.gpsimd
            def _(pool):
                pool.memset(xr[:], 0.0).then_inc(zero, 1)
                pool.memset(bias[:], 0.0).then_inc(zero, 1)
                pool.wait_ge(w_in, 16 * 7)
                pool.tensor_copy(rel[:], rel1[:].to_broadcast([32, 128])).then_inc(rel_wide, 1)
                pool.wait_ge(zero, 2)
                for p in range(PAIRS):
                    if p >= 2:
                        pool.wait_ge(v_ps, p - 1)
                    pair = m.xT[:, :, p * PAIR:(p + 1) * PAIR].rearrange("p c (b t) -> p c b t", b=2)
                    pool.tensor_copy(xr[:, p % 2, :, :, 0:REM], pair[:, :, :, MAIN:SEQ]).then_inc(x_rem, 1)

                def find_zeros(p):
                    pool.wait_ge(y_raw, p + 1)
                    if p >= 2:
                        pool.wait_ge(y_sb, p - 1)
                    pool.tensor_scalar(z[:, p % 2], y[:, p % 2], 0.0, 1e-6, ALU.is_equal, ALU.mult).then_inc(y_zero, 1)

                def apply_mask(p):
                    pool.wait_ge(recip, p + 1)
                    pool.tensor_tensor(r[:, p % 2], r[:, p % 2], mask[:], ALU.mult).then_inc(masked, 1)

                find_zeros(0)
                for p in range(PAIRS):
                    if p + 1 < PAIRS:
                        find_zeros(p + 1)
                    apply_mask(p)

            @block.vector
            def _(dve):
                dve.memset(ps[:, SB, :], 0.0)
                dve.wait_ge(rel_ps, 1)
                dve.tensor_scalar(relv[:], ps[:, REL, :], float(128 ** 0.5), None, ALU.mult).then_inc(rel_sb, 1)
                dve.wait_ge(w_in, 16 * 7)
                for p in range(PAIRS):
                    n, cols = p % 2, slice(p * PAIR, (p + 1) * PAIR)
                    dve.wait_ge(qk_sb, p + 1)
                    dve.tensor_scalar(q[:, cols], qk[:, n], cst[:, 1:2], cst[:, 3:4], ALU.mult, ALU.add).then_inc(q_sb, 1)
                    dve.tensor_scalar(k[:, cols], qk[:, n], cst[:, 2:3], cst[:, 4:5], ALU.mult, ALU.add).then_inc(k_sb, 1)
                    dve.wait_ge(v_ps, p + 1)
                    bank = VB + 2 * n
                    dve.tensor_tensor(v[:, p], ps[:, bank:bank + 2, :].rearrange("p k (b n) -> p (k b) n", b=2)[:, 0:3],
                                      bv[:].unsqueeze(1).to_broadcast([128, 3, D]), ALU.add).then_inc(v_sum, 1)
                dve.wait_ge(bias_in, 64)
                dve.tensor_scalar(bias[:], bias[:], 1.0 / STD, -MU / STD, ALU.mult, ALU.add).then_inc(bias_sc, 1)
                dve.wait_ge(bias_sc, 1)

                def argument(p):
                    dve.wait_ge(s_ps, p + 1)
                    if p >= 2:
                        dve.wait_ge(gelu, p - 1)
                        dve.wait_ge(recip, p - 1)
                    dve.scalar_tensor_tensor(y[:, p % 2], ps[:, SB + p % 2, 0:W], 1.0 / (SEQ * STD), bias[:],
                                             ALU.mult, ALU.add).then_inc(y_raw, 1)

                def invert(p):
                    dve.wait_ge(y_zero, p + 1)
                    dve.tensor_tensor(y[:, p % 2], y[:, p % 2], z[:, p % 2], ALU.add).then_inc(y_sb, 1)
                    dve.wait_ge(y_sb, p + 1)
                    dve.reciprocal(r[:, p % 2], y[:, p % 2]).then_inc(recip, 1)

                def attention(p):
                    dve.wait_ge(masked, p + 1)
                    dve.wait_ge(gelu, p + 1)
                    if p >= 2:
                        dve.wait_ge(o_ps, p - 1)
                    dve.tensor_tensor(at[:, p % 2], gl[:, p % 2], r[:, p % 2], ALU.mult).then_inc(attn, 1)

                def add_back(p):
                    for t in tiles_of(p):
                        dve.wait_ge(turned, t + 1)
                        dve.tensor_tensor(m.h[:, t, :], m.h[:, t, :], ps[0:TP, TB + t % 2, 0:D], ALU.add).then_inc(added, 1)

                argument(0)
                for p in range(PAIRS):
                    if p + 1 < PAIRS:
                        argument(p + 1)
                    invert(p)
                    if p >= 1:
                        attention(p - 1)
                    if p >= 2:
                        add_back(p - 2)
                attention(PAIRS - 1)
                add_back(PAIRS - 2)
                add_back(PAIRS - 1)

            @block.scalar
            def _(act):
                act.wait_ge(w_in, 16 * 7)
                for p in range(PAIRS):
                    act.wait_ge(qk_ps, p + 1)
                    if p >= 2:
                        act.wait_ge(q_sb, p - 1)
                        act.wait_ge(k_sb, p - 1)
                    act.activation(qk[:, p % 2], ps[:, QB + p % 2, 0:PAIR], ACT.Silu, bias=cst[:, 0:1]).then_inc(qk_sb, 1)
                    act.wait_ge(v_sum, p + 1)
                    act.activation(v[:, p], v[:, p], ACT.Silu).then_inc(v_sb, 1)

                def phi(p):
                    act.wait_ge(y_sb, p + 1)
                    if p >= 2:
                        act.wait_ge(attn, p - 1)
                    act.activation(gl[:, p % 2], y[:, p % 2], ACT.Gelu).then_inc(gelu, 1)

                def keep_out(p):
                    act.wait_ge(o_ps, p + 1)
                    bank = OB + 2 * (p % 2)
                    pair = m.xT[:, :, p * PAIR:(p + 1) * PAIR].rearrange("p c (b t) -> p b c t", b=2)
                    act.copy(pair, ps[:, bank:bank + 2, 0:2 * SEQ].rearrange("p b (c t) -> p b c t", c=DK))\
                       .then_inc(o_sb, 1)

                for p in range(PAIRS):
                    phi(p)
                    if p >= 2:
                        keep_out(p - 2)
                keep_out(PAIRS - 2)
                keep_out(PAIRS - 1)


def scores1(nc, sem, m):
    with ExitStack() as ctx:
        def tmp(name, shape, dt=F32):
            return ctx.enter_context(nc.sbuf_tensor(name, shape, dt))

        mx = tmp("s1_max", [TP, NT])
        rsum = tmp("s1_rsum", [TP, NT])
        z = tmp("s1_z", [TP, NT, E])
        step, exps = sem("s1_step"), sem("s1_exps")
        ps = m.ps
        with nc.Block() as block:
            @block.scalar
            def _(act):
                act.wait_ge(step, 3)
                act.activation(z[:], z[:], ACT.Exp).then_inc(exps, 1)

            @block.vector
            def _(dve):
                def over(a):
                    return a.unsqueeze(2).to_broadcast([TP, NT, E])

                dve.tensor_tensor(z[:], ps[0:TP, RB, 0:NT * E].rearrange("p (t e) -> p t e", e=E),
                                  m.rb[:].unsqueeze(1).to_broadcast([TP, NT, E]), ALU.add).then_inc(step, 1)
                dve.wait_ge(step, 1)
                dve.tensor_reduce(mx[:], z[:], AX.X, ALU.max).then_inc(step, 1)
                dve.wait_ge(step, 2)
                dve.tensor_tensor(z[:], z[:], over(mx[:]), ALU.subtract).then_inc(step, 1)
                dve.wait_ge(exps, 1)
                dve.tensor_reduce(mx[:], z[:], AX.X, ALU.add).then_inc(step, 1)
                dve.wait_ge(step, 4)
                dve.reciprocal(rsum[:], mx[:]).then_inc(step, 1)
                dve.wait_ge(step, 5)
                dve.tensor_tensor(m.score[:], z[:], over(rsum[:]), ALU.mult)


def choose1(nc, sem, m, d):
    with ExitStack() as ctx:
        def tmp(name, shape, dt=F32):
            return ctx.enter_context(nc.sbuf_tensor(name, shape, dt))

        NB = 15
        UNROLL = 3
        bits = tmp("bits", [TP, NB, 3], I32)
        thr = tmp("threshold", [TP, UNROLL, 4, E])
        cand = tmp("candidates", [TP, 3, E], I32)
        ge = tmp("at_least", [TP, 3, NT, E])
        cnts = tmp("candidate_counts", [TP, 3, E])
        cnt = tmp("count", [TP, E])
        ones = tmp("ones_c1", [TP, TP])
        before = tmp("before_c1", [TP, TP])
        keep = tmp("keep_c1", [TP, E, NT])
        gt = tmp("above", [TP, NT, E])
        eq = tmp("ties", [TP, NT, E])
        need = tmp("need", [TP, E])
        cs = tmp("c1_counts", [TP, E, NT])
        incl = tmp("c1_incl", [TP, E, NT])
        rank = tmp("c1_rank", [TP, NT, E])
        rest = tmp("c1_rest", [TP, NT, E])
        left = tmp("c1_left", [TP, NT, E])
        rec = tmp("records", [TP, NT, E, 5], BF16)
        place = tmp("placed_records", [TP, NT, E, 4, 5], BF16)
        quart = tmp("row_tile", [TP, NT, E])
        inq = tmp("in_row_tile", [TP, NT, E, 4], BF16)
        part = tmp("row_in_tile", [TP, NT, E], F16)
        tilerow = tmp("tile_row", [TP, NT, 2])
        iota = tmp("iota128", [TP, 128], F16)
        zeros = tmp("c1_zeros", [TP, 256], BF16)
        hot = tmp("slot_hot", [TP, 2, E, 128], BF16)
        found = tmp("found", [128, E * 4, 5])
        rowf = tmp("row_f", [128, E * 4])

        ld, init = sem("c1_in"), sem("c1_init")
        c_cand, c_ge, c_cnt, c_tot, c_ok, c_thr = (sem("c1_" + n) for n in ("cand", "ge", "cnt", "tot", "ok", "thr"))
        rec_step, part_ready = sem("c1_rec"), sem("c1_part")
        step, tie_ps, pos_ps, hot_ready, hot_used, found_ps = (
            sem("c1_" + n) for n in ("step", "tie_ps", "pos_ps", "hot", "hot_used", "found_ps"))
        ps = m.ps
        NE = NT * E

        def flat(a):
            return a[:].rearrange("p t e -> p (t e)")

        def by_tile(a):
            return a.rearrange("p (t e) -> p t e", e=E)

        def spread(a):
            return a.unsqueeze(1).to_broadcast([TP, NT, E])

        with nc.Block() as block:
            @block.sync
            def _(sp):
                for dst, src in [(bits[:], d["bits"]), (before[:], d["before"]),
                                 (keep[:], d["keep"].unsqueeze(0).to_broadcast([TP, E, NT])),
                                 (tilerow[:], d["tile_row"]), (iota[:], d["iota128"].to_broadcast([TP, 128]))]:
                    sp.dma_start(dst, src).then_inc(ld, 16)

            @block.vector
            def _(dve):
                dve.memset(thr[:], 0).then_inc(init, 1)
                dve.memset(ones[:], 1.0).then_inc(init, 1)
                dve.memset(zeros[:], 0.0).then_inc(init, 1)
                dve.wait_ge(ld, 16 * 5)
                dve.wait_ge(init, 3)
                dve.sem_inc(c_thr, 1)
                with dve.Fori(0, NB // UNROLL) as i:
                    for n in range(UNROLL):
                        k = i * UNROLL + n
                        dve.wait_ge(c_thr, k + 1)
                        dve.tensor_tensor(cand[:], thr[:, n, 0, :].bitcast(I32).unsqueeze(1).to_broadcast([TP, 3, E]),
                                          bits[:, bass.ds(k, 1), :].rearrange("p a b -> p (a b)").unsqueeze(2)
                                          .to_broadcast([TP, 3, E]), ALU.bitwise_or).then_inc(c_cand, 1)
                        dve.wait_ge(c_cand, k + 1)
                        dve.tensor_tensor(ge[:], m.score[:].unsqueeze(1).to_broadcast([TP, 3, NT, E]),
                                          cand[:].bitcast(F32).unsqueeze(2).to_broadcast([TP, 3, NT, E]), ALU.is_ge)\
                           .then_inc(c_ge, 1)
                        dve.wait_ge(c_ge, k + 1)
                        dve.tensor_reduce(cnts[:], ge[:].rearrange("p c t e -> p c e t"), AX.X, ALU.add).then_inc(c_cnt, 1)
                        dve.wait_ge(c_tot, k + 1)
                        dve.scalar_tensor_tensor(thr[:, n, 1:4, :], ps[0:TP, 0, 0:3 * E].rearrange("p (c e) -> p c e", e=E),
                                                 float(TOPK), cand[:].bitcast(F32), ALU.is_ge, ALU.mult).then_inc(c_ok, 1)
                        dve.wait_ge(c_ok, k + 1)
                        dve.tensor_reduce(thr[:, (n + 1) % UNROLL, 0, :], thr[:, n].rearrange("p c e -> p e c"), AX.X, ALU.max)\
                           .then_inc(c_thr, 1)
                dve.wait_ge(c_thr, NB + 1)
                tf = spread(thr[:, 0, 0, :])
                dve.tensor_tensor(gt[:], m.score[:], tf, ALU.is_gt).then_inc(step, 1)
                dve.tensor_tensor(eq[:], m.score[:], tf, ALU.is_equal).then_inc(step, 1)
                dve.wait_ge(step, 2)
                dve.tensor_reduce(cnt[:], gt[:].rearrange("p t e -> p e t"), AX.X, ALU.add).then_inc(step, 1)
                dve.wait_ge(tie_ps, 1)
                dve.tensor_scalar(need[:], ps[0:TP, 1, 0:E], -1.0, float(TOPK), ALU.mult, ALU.add).then_inc(step, 1)

                def prefix(bank, at):
                    dve.tensor_copy(cs[:], by_tile(ps[0:TP, bank, 0:NE]).rearrange("p t e -> p e t")).then_inc(step, 1)
                    dve.wait_ge(step, at + 1)
                    dve.tensor_tensor_scan(incl[:].rearrange("p e t -> p (e t)"), keep[:].rearrange("p e t -> p (e t)"),
                                           cs[:].rearrange("p e t -> p (e t)"), 0.0, ALU.mult, ALU.add).then_inc(step, 1)
                    dve.wait_ge(step, at + 2)
                    dve.tensor_tensor(cs[:], incl[:], cs[:], ALU.subtract).then_inc(step, 1)
                    dve.wait_ge(step, at + 3)
                    dve.tensor_tensor(rank[:], by_tile(ps[0:TP, bank + 1, 0:NE]), cs[:].rearrange("p e t -> p t e"),
                                      ALU.add).then_inc(step, 1)
                    dve.wait_ge(step, at + 4)

                prefix(2, 4)
                dve.tensor_tensor(rest[:], rank[:], spread(need[:]), ALU.is_lt).then_inc(step, 1)
                dve.wait_ge(step, 9)
                dve.tensor_tensor(eq[:], eq[:], rest[:], ALU.mult).then_inc(step, 1)
                dve.wait_ge(step, 10)
                dve.tensor_tensor(gt[:], gt[:], eq[:], ALU.add).then_inc(step, 1)
                dve.wait_ge(pos_ps, 1)
                prefix(4, 11)
                dve.scalar_tensor_tensor(rank[:], rank[:], 1.0, gt[:], ALU.add, ALU.mult).then_inc(step, 1)
                dve.wait_ge(step, 16)
                dve.tensor_scalar(rank[:], rank[:], -1.0, None, ALU.add).then_inc(step, 1)
                dve.wait_ge(step, 17)
                dve.tensor_scalar(quart[:], rank[:], 128.0, None, ALU.is_ge).then_inc(step, 1)
                for c in (2, 3):
                    dve.wait_ge(step, 16 + c)
                    dve.scalar_tensor_tensor(quart[:], rank[:], 128.0 * c, quart[:], ALU.is_ge, ALU.add).then_inc(step, 1)
                dve.wait_ge(step, 20)
                dve.scalar_tensor_tensor(part[:], quart[:], -128.0, rank[:], ALU.mult, ALU.add).then_inc(part_ready, 1)
                for c in range(4):
                    dve.tensor_scalar(inq[:, :, :, c], quart[:], float(c), None, ALU.is_equal).then_inc(step, 1)
                dve.wait_ge(step, 24)
                dve.wait_ge(rec_step, 6)
                for c in range(5):
                    dve.tensor_tensor(place[:, :, :, :, c], inq[:],
                                      rec[:, :, :, c].unsqueeze(3).to_broadcast([TP, NT, E, 4]), ALU.mult).then_inc(step, 1)
                dve.wait_ge(part_ready, 1)

                with dve.Fori(0, NT // 2) as i:
                    for n in range(2):
                        dve.wait_ge(hot_used, i * 2 + n + 1)
                        dve.tensor_tensor(hot[:, n], iota[:].unsqueeze(1).to_broadcast([TP, E, 128]),
                                          part[:, bass.ds(i * 2 + n, 1), :].rearrange("p a e -> p (a e)")
                                          .unsqueeze(2).to_broadcast([TP, E, 128]), ALU.is_equal).then_inc(hot_ready, 1)
                dve.wait_ge(found_ps, 1)
                dve.tensor_copy(found[:], ps[:, 6, 0:E * 20].rearrange("p (s r) -> p s r", r=5)).then_inc(step, 1)
                dve.wait_ge(step, 30)
                dve.scalar_tensor_tensor(rowf[:], found[:, :, 0], float(TP), found[:, :, 1], ALU.mult, ALU.add)\
                   .then_inc(step, 1)
                dve.tensor_tensor(m.gate1[:], found[:, :, 2], found[:, :, 3], ALU.add).then_inc(step, 1)
                dve.wait_ge(step, 32)
                dve.tensor_copy(m.row1[:], rowf[:])
                dve.tensor_tensor(m.gate1[:], m.gate1[:], found[:, :, 4], ALU.add)

            @block.gpsimd
            def _(pool):
                pool.wait_ge(ld, 16 * 5)
                pool.tensor_copy(rec[:, :, :, 2], m.score[:]).then_inc(rec_step, 1)
                for c in range(2):
                    pool.tensor_copy(rec[:, :, :, c], tilerow[:, :, c].unsqueeze(2).to_broadcast([TP, NT, E]))\
                        .then_inc(rec_step, 1)
                pool.wait_ge(rec_step, 3)
                pool.tensor_tensor(left[:], m.score[:], rec[:, :, :, 2], ALU.subtract).then_inc(rec_step, 1)
                pool.wait_ge(rec_step, 4)
                pool.tensor_copy(rec[:, :, :, 3], left[:]).then_inc(rec_step, 1)
                pool.wait_ge(rec_step, 5)
                pool.tensor_tensor(rec[:, :, :, 4], left[:], rec[:, :, :, 3], ALU.subtract).then_inc(rec_step, 1)

            @block.tensor
            def _(pe):
                pe.wait_ge(init, 3)
                pe.wait_ge(ld, 16 * 5)
                with pe.Fori(0, NB // UNROLL) as i:
                    for n in range(UNROLL):
                        pe.wait_ge(c_cnt, i * UNROLL + n + 1)
                        pe.matmul(ps[0:TP, 0, 0:3 * E], ones[:], cnts[:].rearrange("p c e -> p (c e)"),
                                  start=True, stop=True).then_inc(c_tot, 1)
                pe.wait_ge(step, 3)
                pe.matmul(ps[0:TP, 1, 0:E], ones[:], cnt[:], start=True, stop=True)
                pe.matmul(ps[0:TP, 2, 0:NE], ones[:], flat(eq), start=True, stop=True)
                pe.matmul(ps[0:TP, 3, 0:NE], before[:], flat(eq), start=True, stop=True).then_inc(tie_ps, 1)
                pe.wait_ge(step, 11)
                pe.matmul(ps[0:TP, 4, 0:NE], ones[:], flat(gt), start=True, stop=True)
                pe.matmul(ps[0:TP, 5, 0:NE], before[:], flat(gt), start=True, stop=True).then_inc(pos_ps, 1)
                pe.matmul(ps[:, 6, 0:E * 20], zeros[:, 0:128], zeros[:, 0:E * 20], start=True, stop=False,
                          skip_group_check=True)
                pe.wait_ge(step, 29)
                pe.sem_inc(hot_used, 2)
                with pe.Fori(0, NT // 2) as i:
                    for n in range(2):
                        pe.wait_ge(hot_ready, i * 2 + n + 1)
                        for e in range(E):
                            r = place[:, bass.ds(i * 2 + n, 1), e].rearrange("p a s r -> p (a s r)")
                            last = pe.matmul(ps[:, 6, e * 20:(e + 1) * 20], hot[:, n, e, :], r,
                                             start=False, stop=False, skip_group_check=True)
                        last.then_inc(hot_used, 1)
                pe.matmul(ps[:, 6, 0:E * 20], zeros[:, 0:128], zeros[:, 0:E * 20], start=False, stop=True,
                          skip_group_check=True).then_inc(found_ps, 1)


def experts1(nc, sem, m, d, out):
    with ExitStack() as ctx:
        def tmp(name, shape, dt=F32):
            return ctx.enter_context(nc.sbuf_tensor(name, shape, dt))

        NS = TOPK // 128
        b1T = tmp("e1_b1T", [128, E, FK])
        b2 = tmp("e1_b2", [128, E, D])
        x = tmp("e1_x", [128, 2, NS, D])
        xT = tmp("e1_xT", [128, DK, TOPK])
        hT = m.xT[:].rearrange("p c t -> p (c t)")[:, 0:FK * TOPK].rearrange("p (f t) -> p f t", f=FK)
        ysum = tmp("e1_ysum", [128, 2, D])
        y = tmp("e1_y", [128, 2, NS, D])
        b_in, x_in = sem("e1_b_in"), [sem("e1_x_in_0"), sem("e1_x_in_1")]
        xp_ready, xT_ready, h_ready, hT_ready, y_ready, ysum_ready, y_sb, added = (
            sem("e1_" + n) for n in ("xp", "xT", "h", "hT", "y", "ysum", "y_sb", "added"))
        ps = m.ps
        HB, XB, YB = 0, 4, 6
        w_in = m.ring_in
        with nc.Block() as block:
            @block.sync
            def _(sp):
                sp.dma_start(b1T[:], d["b1T_1"]).then_inc(b_in, 16)
                sp.dma_start(b2[:], d["b2_1"].unsqueeze(0).to_broadcast([128, E, D])).then_inc(b_in, 16)
                with sp.Fori(0, E // 2 - 1) as i:
                    for n in range(2):
                        sp.wait_ge(h_ready, i * 2 * FK + (n + 1) * FK)
                        sp.dma_start(m.w1[:, n:n + 1], d["w1_1"].rearrange("e (c p) f -> p e c f", p=128)
                                     [:, bass.ds(i * 2 + n + 2, 1)]).then_inc(w_in[n], 16)
                        sp.wait_ge(y_ready, i * 2 * NS + (n + 1) * NS)
                        sp.dma_start(m.w2[:, n:n + 1], d["w2_1"].rearrange("e (c p) f -> p e c f", p=128)
                                     [:, bass.ds(i * 2 + n + 2, 1)]).then_inc(w_in[n], 16)

            @block.gpsimd
            def _(pool):
                def gather(e):
                    for s in range(NS):
                        c = e * NS + s
                        pool.indirect_dma_start(x[:, e % 2, s, :], None, m.xrows,
                                                bass.IndirectOffsetOnAxis(m.row1[:, c:c + 1], 0)).then_inc(x_in[e % 2], 16)

                pool.wait_ge(m.rows_out, 16 * (1 + len(GROUPS)))
                gather(0)
                gather(1)
                for e in range(E):
                    if e >= 1:
                        pool.wait_ge(added, 16 * NS * e)
                    for s in range(NS):
                        pool.wait_ge(y_sb, e * NS + s + 1)
                        c = e * NS + s
                        pool.indirect_dma_start(out, bass.IndirectOffsetOnAxis(m.row1[:, c:c + 1], 0),
                                                y[:, e % 2, s, :], None, compute_op=ALU.add).then_inc(added, 16)
                    if e + 2 < E:
                        pool.wait_ge(xp_ready, 2 * (e + 1))
                        gather(e + 2)
                pool.wait_ge(added, 16 * NS * E)

            @block.tensor
            def _(pe):
                with pe.Fori(0, E // 2) as i:
                    for n in range(2):
                        pe.wait_ge(x_in[n], i * 16 * NS + 16 * NS)
                        for c in range(DK):
                            pe.wait_ge(xT_ready, i * 4 + n * 2)
                            for s in range(NS):
                                last = pe.transpose(ps[:, XB + c, s * 128:(s + 1) * 128],
                                                    x[:, n, s, c * 128:(c + 1) * 128], m.ident[:])
                            last.then_inc(xp_ready, 1)
                        pe.wait_ge(w_in[n], i * 32 + 32)
                        pe.wait_ge(xT_ready, i * 4 + n * 2 + 2)
                        for f in range(FK):
                            pe.wait_ge(hT_ready, i * 2 * FK + n * FK + f + 1)
                            for c in range(DK):
                                last = pe.matmul(ps[:, HB + f % 4, :], m.w1[:, n, c, f * 128:(f + 1) * 128], xT[:, c, :],
                                                 start=(c == 0), stop=(c == DK - 1))
                            last.then_inc(h_ready, 1)
                        pe.wait_ge(hT_ready, i * 2 * FK + (n + 1) * FK + 4)
                        for s in range(NS):
                            pe.wait_ge(ysum_ready, i * 2 * NS + n * NS + s + 1)
                            for f in range(FK):
                                last = pe.matmul(ps[:, YB + s % 2, 0:D], hT[:, f, s * 128:(s + 1) * 128], m.w2[:, n, f, :],
                                                 start=(f == 0), stop=(f == FK - 1))
                            last.then_inc(y_ready, 1)

            @block.scalar
            def _(act):
                act.sem_inc(hT_ready, 4)
                act.wait_ge(b_in, 32)
                with act.Fori(0, E // 2) as i:
                    for n in range(2):
                        for f in range(FK):
                            act.wait_ge(h_ready, i * 2 * FK + n * FK + f + 1)
                            act.activation(hT[:, f, :], ps[:, HB + f % 4, :], ACT.Relu,
                                           bias=b1T[:, bass.ds(i * 2 + n, 1), f]).then_inc(hT_ready, 1)

            @block.vector
            def _(dve):
                dve.sem_inc(ysum_ready, 2)
                dve.wait_ge(b_in, 32)
                with dve.Fori(0, E // 2) as i:
                    for n in range(2):
                        for c in range(DK):
                            dve.wait_ge(xp_ready, i * 4 + n * 2 + c + 1)
                            dve.tensor_copy(xT[:, c, :], ps[:, XB + c, :]).then_inc(xT_ready, 1)
                        for s in range(NS):
                            k = n * NS + s
                            dve.wait_ge(y_ready, i * 2 * NS + k + 1)
                            dve.tensor_tensor(ysum[:, s % 2:s % 2 + 1], ps[:, YB + s % 2, 0:D].unsqueeze(1),
                                              b2[:, bass.ds(i * 2 + n, 1)], ALU.add).then_inc(ysum_ready, 1)
                            dve.wait_ge(ysum_ready, i * 2 * NS + k + 3)
                            dve.wait_ge(added, i * 32 * NS)
                            dve.tensor_scalar(y[:, n, s, :], ysum[:, s % 2, :],
                                              m.gate1[:, bass.ds((i * 2 + n) * NS + s, 1)], None, ALU.mult)\
                               .then_inc(y_sb, 1)


def layouts(inputs):
    f32 = np.float32
    g = {n: np.asarray(a) for n, a in inputs.items()}
    x = g["x"].reshape(B, 3, HP, 16, HP, 16).transpose(0, 2, 4, 3, 5, 1).reshape(B * NPATCH, PATCH)
    inv = (1.0 / 10000.0 ** (np.arange(0, HD, 2, dtype=f32) / f32(HD))).astype(f32)
    ang = np.repeat(np.arange(NH, dtype=f32)[:, None] * inv[None, :], 2, 1).reshape(-1)
    sign = np.where(np.arange(D) % 2, 1, -1)
    scale = np.array([[0.25], [1.0]], f32)
    cos, sin = (np.cos(ang) * scale).astype(f32), (np.sin(ang) * sign * scale).astype(f32)
    swap = np.arange(D) ^ 1
    rem_mask = np.zeros((128, 4), f32)
    rem_mask[0:3 * REM:3, 0] = 1
    rem_mask[1:3 * REM:3, 1] = 1
    rem_mask[2:3 * REM:3, 2:4] = 1
    head_mask = (np.arange(128)[:, None] // HD == np.arange(8)[None]).astype(f32)
    o_order = np.concatenate([(2 * u + ab) * HD + np.arange(HD) for ab in range(2) for u in range(NU)])

    yy, xx = np.meshgrid(np.arange(HP), np.arange(HP), indexing="ij")
    omega = (1.0 / 10000.0 ** (np.arange(D // 4, dtype=f32) / f32(D // 4 - 1))).astype(f32)
    yy, xx = yy.reshape(-1, 1).astype(f32) * omega, xx.reshape(-1, 1).astype(f32) * omega
    pos = np.concatenate([np.sin(xx), np.cos(xx), np.sin(yy), np.cos(yy)], 1).astype(f32)

    n = np.maximum(np.arange(512) - (SEQ - 1), 0)
    large = 16 + (np.log(np.maximum(n, 1).astype(f32) / 16) / math.log(128 / 16) * 16).astype(np.int32)
    bucket = np.where(n < 16, n, np.minimum(large, 31))
    buckets = (np.arange(32)[:, None] == bucket[None, :]).astype(f32)
    j, i = np.arange(128)[:, None], np.arange(SEQ)[None, :]
    main, rem = j <= i, (j[:, :1] % 64 <= i[:, :REM]) & (j % 64 < REM)
    mask1 = np.concatenate([main, main, rem], 1).astype(f32)

    def gb(a):
        return a.reshape(KP, 128).T

    d = {
        "patches": x, "txt": g["txt"], "ident": np.eye(128, dtype=f32),
        "ln1_gb": np.stack([gb(g["L0_tok_ln1_g"]), gb(g["L0_tok_ln1_b"])], 1),
        "tok_bias": g["L0_tok_bias"][None], "ln2_g": g["L0_tok_ln2_g"][None], "ln2_b": g["L0_tok_ln2_b"][None],
        "pos": np.concatenate([pos, pos], 0), "cls": g["L0_tok_cls_token"][0],
        "cls_pos": g["L0_tok_cls_pos_embedding"][0], "tok_w": g["L0_tok_W"],
        "wq": g["L0_attn_wq"].T, "wq_swap": g["L0_attn_wq"][swap].T,
        "wlat": np.concatenate([g["L0_attn_wk_a"].T, g["L0_attn_wv_a"].T], 1),
        "wkb": g["L0_attn_wk_b"].T, "wkb_swap": g["L0_attn_wk_b"][swap].T, "head_mask": head_mask,
        "wvb": g["L0_attn_wv_b"].T, "wo": g["L0_attn_wo"].T[o_order],
        "rot_cos": cos, "rot_sin": sin, "rem_mask": rem_mask,
        "w1": g["L0_ffn_w1"], "w2": g["L0_ffn_w2"], "w_red": g["L0_ffn_w_red"], "wg": g["L0_ffn_wg"],
        "b1T": g["L0_ffn_b1"].reshape(E, FK, 128).transpose(2, 0, 1).reshape(128, E * FK), "b2": g["L0_ffn_b2"],
        "iota8": (np.arange(E, dtype=f32) - E)[None], "rows128": (np.arange(21, dtype=f32) * 128)[None],
        "tiles_j": np.arange(SLOT_TILES, dtype=f32)[None],
        "keep": np.tile(np.arange(NT) > 0, (E, 1)).astype(f32),
        "spread16": np.tile(np.eye(GD, dtype=f32), (1, 8)),
        "diag_mask": np.repeat(np.eye(8, dtype=f32), GD, 0)[:, :, None] * np.ones((1, 1, E), f32),
        "before": np.triu(np.ones((TP, TP), f32), 1),
        "wqk": g["L1_attn_Wqk"], "wv": g["L1_attn_Wv"], "bv": g["L1_attn_bv"][None],
        "a1_cst": np.stack([g["L1_attn_bqk"], *g["L1_attn_gamma"], *g["L1_attn_beta"]], 1),
        "rel_emb": g["L1_attn_rel_emb"], "buckets": buckets, "mask1": mask1,
        "router_w": g["L1_ffn_router_w"], "router_b": g["L1_ffn_router_b"][None],
        "bits": np.tile((np.arange(1, 4) << np.arange(28, -1, -2)[:, None]).astype(np.int32), (TP, 1, 1)),
        "tile_row": np.stack(np.broadcast_arrays(np.arange(NT)[None], np.arange(TP)[:, None]), 2).astype(f32),
        "iota128": np.arange(128).astype(np.float16)[None],
        "b1T_1": g["L1_ffn_b1"].reshape(E, FK, 128).transpose(2, 0, 1), "b2_1": g["L1_ffn_b2"],
        "w1_1": g["L1_ffn_w1"], "w2_1": g["L1_ffn_w2"],
    }
    return {n: np.ascontiguousarray(a) for n, a in d.items()}


def kernel(**inputs):
    import concourse.bacc as _bacc
    from concourse.bass_utils import run_bass_kernel_spmd as _run

    nc = _bacc.Bacc("TRN2", target_bir_lowering=False, num_devices=1)
    arrays = {f"in_{n}": a for n, a in layouts(inputs).items()}
    d = {n[3:]: nc.dram_tensor(n, a.shape, mybir.dt.from_np(a.dtype), kind="ExternalInput").ap()
         for n, a in arrays.items()}
    out = nc.dram_tensor("out", (TOK, D), F32, kind="ExternalOutput").ap()
    build(nc, d, out)
    r = _run(nc, [arrays], core_ids=[0])
    return r.results[0]["out"].reshape(B, SEQ, D)
```

```python
import math
from contextlib import ExitStack

import numpy as np

import concourse.bass as bass
from concourse import mybir

ALU = mybir.AluOpType
ACT = mybir.ActivationFunctionType
AX = mybir.AxisListType
F32 = mybir.dt.float32
F16 = mybir.dt.float16
F32R = mybir.dt.float32r
BF16 = mybir.dt.bfloat16
I32 = mybir.dt.int32

EPS = 1e-5
B, D = 16, 256
PATCH, HP, NTXT = 768, 6, 128
NPATCH = HP * HP
SEQ = 1 + NPATCH + NTXT
TOK = B * SEQ
TP, NT = 120, 22
PT, NPT = 2 * NPATCH, B // 2
KP = PATCH // 128
GROUPS = (range(0, 5), range(5, 11), range(11, 16), range(16, 22))
DK = D // 128
NH, HD = 16, 16
LAT = 64
MAIN, REM = 128, SEQ - 128
PAIR = 2 * SEQ
REM_B = 64
NU = NH // 2
OW = HD + 1
E, F, GD = 8, 1024, 16
FK = F // 128
NBITS = 30
RB = 6
SLOT = 128
SLOT_TILES = (TOK + E * (SLOT - 1)) // SLOT
SLOTS = SLOT_TILES * SLOT
TOPK = 512

PARTS = ((0, 0), (1, 0), (0, 1))


class Mem:
    pass


def tokenise(nc, sem, m, d):
    with ExitStack() as ctx:
        def sb(name, shape, dt=F32):
            return ctx.enter_context(nc.sbuf_tensor(name, shape, dt))

        NX = 3
        x = sb("patches", [PT, NPT, PATCH])
        xn = sb("patches_normed", [PT, NX, PATCH])
        xg = sb("patches_scaled", [128, 2, KP, PT])
        xT = sb("patches_T", [128, 2, KP, PT])
        w = sb("tok_w", [128, KP, D])
        gb = sb("ln1_gb", [128, 2, KP])
        rows = sb("tok_rows", [PT, 3, D])
        pe_b = sb("pos_offset", [PT, D])
        cls = sb("cls_rows", [B, 2, D])
        tok = sb("tok", [PT, NPT, D])
        st = sb("stats1", [PT, NPT, 2, 6])
        mv = sb("mean_var1", [PT, NPT, 2])
        std = sb("std1", [PT, NPT])
        rstd = sb("rstd1", [PT, NPT])
        st2 = sb("stats2", [PT, NPT, 6])
        mv2 = sb("mean_var2", [PT, NPT, 2])
        std2 = sb("std2", [PT, NPT])
        rstd2 = sb("rstd2", [PT, NPT])
        eps = sb("eps_tok", [PT, 1])

        x_in = [sem("x_in_a"), sem("x_in_b")]
        small_in, w_in = sem("tok_small_in"), sem("tok_w_in")
        eps_set, zero_set = sem("tok_eps_set"), sem("zero_set")
        st1_done, mv1_done, std1_done, rstd1_done = (sem(n) for n in ("st1", "mv1", "std1", "rstd1"))
        xn_ready, xp_ready, xg_ready, xT_ready, y_ready, tok_ready = (
            sem(n) for n in ("xn_ready", "xp_ready", "xg_ready", "xT_ready", "y_ready", "tok_ready"))
        st2_done, mv2_done, std2_done, rstd2_done = (sem(n) for n in ("st2", "mv2", "std2", "rstd2"))
        peb_done, cls_done, scaled, placed = (sem(n) for n in ("peb", "cls", "tok_scaled", "tok_placed"))
        others_out, half_out, rot_parts = sem("h0_others_out"), [sem("h0_out_a"), sem("h0_out_b")], sem("rot_parts")
        ps = m.ps
        YB = NX
        h0_b = m.h0.rearrange("(b s) d -> b s d", s=SEQ)
        h0_j = m.h0.rearrange("(j b s) d -> b s j d", j=NPT, b=2)
        h0_t = m.h0.rearrange("(t p) d -> p t d", p=TP)
        half = NPT // 2
        HALVES = (range(0, half), range(half, NPT))
        in_first = [g for g, ts in enumerate(GROUPS) if ts.stop * TP <= B // 2 * SEQ]
        in_second = [g for g in range(len(GROUPS)) if g not in in_first]
        with nc.Block() as block:
            @block.sync
            def _(sp):
                pd = d["patches"].rearrange("(j p) k -> p j k", p=PT)
                for n, js in enumerate(HALVES):
                    sp.dma_start(x[:, js.start:js.stop, :], pd[:, js.start:js.stop, :]).then_inc(x_in[n], 16)
                sp.dma_start(m.ident[:], d["ident"]).then_inc(small_in, 16)
                sp.dma_start(gb[:], d["ln1_gb"]).then_inc(small_in, 16)
                for n, name in enumerate(("tok_bias", "ln2_g", "ln2_b")):
                    sp.dma_start(rows[:, n, :], d[name].to_broadcast([PT, D])).then_inc(small_in, 16)
                sp.dma_start(pe_b[:], d["pos"]).then_inc(small_in, 16)
                for n, name in enumerate(("cls", "cls_pos")):
                    sp.dma_start(cls[:, n, :], d[name].to_broadcast([B, D])).then_inc(small_in, 16)
                sp.dma_start(w[:], d["tok_w"].rearrange("(c p) n -> p c n", p=128)).then_inc(w_in, 16)
                sp.dma_start(h0_b[:, 1 + NPATCH:, :], d["txt"]).then_inc(others_out, 16)
                for dst, src in m.attn_loads:
                    sp.dma_start(dst, src).then_inc(m.attn_in, 16)
                sp.wait_ge(cls_done, 1)
                sp.dma_start(h0_b[:, 0, :], cls[:, 0, :]).then_inc(others_out, 16)
                for n, js in enumerate(HALVES):
                    sp.wait_ge(placed, js.stop)
                    for b in range(2):
                        sp.dma_start(h0_j[b, 1:1 + NPATCH, js.start:js.stop],
                                     tok[b * NPATCH:(b + 1) * NPATCH, js.start:js.stop]).then_inc(half_out[n], 16)
                    sp.wait_ge(half_out[n], 32)
                    if n == 0:
                        sp.wait_ge(others_out, 32)
                    for g in (in_first, in_second)[n]:
                        ts = GROUPS[g]
                        sp.dma_start(m.h[:, ts.start:ts.stop], h0_t[:, ts.start:ts.stop]).then_inc(m.h_in[g], 16)
                sp.wait_ge(zero_set, 1)
                sp.dma_start(m.xs.rearrange("(p r) d -> p r d", p=128),
                             m.zero_row[:].unsqueeze(1).to_broadcast([128, SLOTS // 128, D])).then_inc(m.zero_out, 16)
                for dst, src in m.expert_loads:
                    sp.dma_start(dst, src).then_inc(m.expert_in, 16)

            @block.tensor
            def _(pe):
                def turn(j):
                    pe.wait_ge(xn_ready, j + 1)
                    if j >= NX:
                        pe.wait_ge(xg_ready, j - NX + 1)
                    for k in range(KP):
                        last = pe.transpose(ps[:, j % NX, k * PT:(k + 1) * PT], xn[:, j % NX, k * 128:(k + 1) * 128],
                                            m.ident[0:PT, 0:PT])
                    last.then_inc(xp_ready, 1)

                pe.wait_ge(small_in, 128)
                turn(0)
                turn(1)
                pe.wait_ge(w_in, 16)
                for j in range(NPT):
                    if j + 2 < NPT:
                        turn(j + 2)
                    pe.wait_ge(xT_ready, j + 1)
                    if j >= 2:
                        pe.wait_ge(tok_ready, j - 1)
                    for k in range(KP):
                        last = pe.matmul(ps[0:PT, YB + j % 2, 0:D], xT[:, j % 2, k, :], w[:, k, :],
                                         start=(k == 0), stop=(k == KP - 1))
                    last.then_inc(y_ready, 1)

            @block.gpsimd
            def _(pool):
                pool.wait_ge(small_in, 128)
                pool.tensor_tensor(pe_b[:], pe_b[:], rows[:, 2, :], ALU.add).then_inc(peb_done, 1)
                pool.tensor_tensor(cls[:, 0, :], cls[:, 0, :], cls[:, 1, :], ALU.add).then_inc(cls_done, 1)
                off = gb[:, 1, :].unsqueeze(2).to_broadcast([128, KP, PT])
                for j in range(NPT):
                    pool.wait_ge(xg_ready, j + 1)
                    if j >= 2:
                        pool.wait_ge(y_ready, j - 1)
                    pool.tensor_tensor(xT[:, j % 2], xg[:, j % 2], off, ALU.add).then_inc(xT_ready, 1)
                pool.wait_ge(m.attn_in, m.attn_want)
                kb, kb_swap = m.wkb[0:LAT, :], m.wkb_swap[0:LAT, :]
                cos_q, sin_q = (a[:, 0, :].unsqueeze(1).to_broadcast([128, DK, D]) for a in (m.rot_cos, m.rot_sin))
                pool.tensor_tensor(m.wq[:], m.wq[:], cos_q, ALU.mult).then_inc(rot_parts, 1)
                pool.tensor_tensor(m.wq_swap[:], m.wq_swap[:], sin_q, ALU.mult).then_inc(rot_parts, 1)
                pool.tensor_tensor(kb, kb, m.rot_cos[0:LAT, 1, :], ALU.mult).then_inc(rot_parts, 1)
                pool.tensor_tensor(kb_swap, kb_swap, m.rot_sin[0:LAT, 1, :], ALU.mult).then_inc(rot_parts, 1)
                pool.wait_ge(rot_parts, 4)
                pool.tensor_tensor(m.wq[:], m.wq[:], m.wq_swap[:], ALU.add)
                pool.tensor_tensor(kb, kb, kb_swap, ALU.add)

            @block.scalar
            def _(act):
                act.wait_ge(eps_set, 1)
                for done, out_done, s, v in ((mv1_done, std1_done, std, mv), (mv2_done, std2_done, std2, mv2)):
                    for js in HALVES:
                        act.wait_ge(done, js.stop)
                        act.activation(s[:, js.start:js.stop], v[:, js.start:js.stop, 1], ACT.Sqrt, bias=eps[:, 0:1])\
                           .then_inc(out_done, 1)

            @block.vector
            def _(dve):
                dve.memset(eps[:], EPS).then_inc(eps_set, 1)
                dve.memset(m.zero_row[:], 0.0).then_inc(zero_set, 1)

                def patch_statistics(n):
                    dve.wait_ge(x_in[n], 16)
                    for j in HALVES[n]:
                        for c in range(2):
                            dve.bn_stats(st[:, j, c, :], x[:, j, c * (PATCH // 2):(c + 1) * (PATCH // 2)])\
                               .then_inc(st1_done, 1)
                    for j in HALVES[n]:
                        dve.wait_ge(st1_done, 2 * j + 2)
                        dve.bn_aggr(mv[:, j, :], st[:, j].rearrange("p c s -> p (c s)")).then_inc(mv1_done, 1)

                def invert(n, std_done, s, r, done):
                    js = HALVES[n]
                    dve.wait_ge(std_done, n + 1)
                    dve.reciprocal(r[:, js.start:js.stop], s[:, js.start:js.stop]).then_inc(done, 1)
                    dve.wait_ge(done, n + 1)

                def norm_patches(j):
                    if j >= NX:
                        dve.wait_ge(xp_ready, j - NX + 1)
                    dve.tensor_scalar(xn[:, j % NX, :], x[:, j, :], mv[:, j, 0:1], rstd[:, j:j + 1],
                                      ALU.subtract, ALU.mult).then_inc(xn_ready, 1)

                def project(j):
                    dve.wait_ge(y_ready, j + 1)
                    dve.tensor_tensor(tok[:, j, :], ps[0:PT, YB + j % 2, 0:D], rows[:, 0, :], ALU.add).then_inc(tok_ready, 1)
                    dve.wait_ge(tok_ready, j + 1)
                    dve.bn_stats(st2[:, j, :], tok[:, j, :]).then_inc(st2_done, 1)

                def token_statistics(n):
                    for j in HALVES[n]:
                        dve.wait_ge(st2_done, j + 1)
                        dve.bn_aggr(mv2[:, j, :], st2[:, j, :]).then_inc(mv2_done, 1)

                def norm_tokens(n):
                    invert(n, std2_done, std2, rstd2, rstd2_done)
                    for j in HALVES[n]:
                        dve.scalar_tensor_tensor(tok[:, j, :], tok[:, j, :], mv2[:, j, 0:1], rows[:, 1, :],
                                                 ALU.subtract, ALU.mult).then_inc(scaled, 1)
                    if n == 0:
                        dve.wait_ge(peb_done, 1)
                    for j in HALVES[n]:
                        dve.wait_ge(scaled, j + 1)
                        dve.scalar_tensor_tensor(tok[:, j, :], tok[:, j, :], rstd2[:, j:j + 1], pe_b[:],
                                                 ALU.mult, ALU.add).then_inc(placed, 1)

                patch_statistics(0)
                patch_statistics(1)
                invert(0, std1_done, std, rstd, rstd1_done)
                dve.wait_ge(mv1_done, NPT)
                norm_patches(0)
                norm_patches(1)
                invert(1, std1_done, std, rstd, rstd1_done)
                dve.wait_ge(small_in, 128)
                gain = gb[:, 0, :].unsqueeze(2).to_broadcast([128, KP, PT])
                for j in range(NPT):
                    if j + 2 < NPT:
                        norm_patches(j + 2)
                    dve.wait_ge(xp_ready, j + 1)
                    if j >= 2:
                        dve.wait_ge(xT_ready, j - 1)
                    dve.tensor_tensor(xg[:, j % 2], ps[:, j % NX, 0:KP * PT].rearrange("p (k t) -> p k t", k=KP), gain,
                                      ALU.mult).then_inc(xg_ready, 1)
                    if j >= 1:
                        project(j - 1)
                    if j == half:
                        token_statistics(0)
                    if j == half + 1:
                        norm_tokens(0)
                project(NPT - 1)
                token_statistics(1)
                norm_tokens(1)


def normalise(nc, sem, m, tag, source=None, source_pe=None, use_pe=None, on_sync=None, on_pool=None):
    with ExitStack() as ctx:
        def sb(name, shape, dt=F32):
            return ctx.enter_context(nc.sbuf_tensor(name + tag, shape, dt))

        st = sb("stats", [TP, NT, 6])
        mv = sb("mean_var", [TP, NT, 2])
        std = sb("std", [TP, NT])
        rstd = sb("rstd", [TP, NT])
        eps = sb("eps", [TP, 1])
        eps_set, h_ready, st_done, mv_done, std_done, rstd_done, xn_ready, xp_ready, xT_ready = (
            sem(n + tag) for n in ("eps_set", "h", "st", "mv", "std", "rstd", "xn", "xp", "xT"))
        ps = m.ps
        XB, BANKS = 2, 4
        last_group = len(GROUPS) - 1
        with nc.Block() as block:
            if on_sync is not None:
                @block.sync
                def _(sp):
                    on_sync(sp, h_ready, xn_ready)

            if on_pool is not None:
                @block.gpsimd
                def _(pool):
                    on_pool(pool)

            @block.vector
            def _(dve):
                dve.memset(eps[:], EPS).then_inc(eps_set, 1)

                def statistics(g):
                    if source is None:
                        dve.wait_ge(m.h_in[g], 16)
                    else:
                        for t in GROUPS[g]:
                            source(dve, t, h_ready)
                    for t in GROUPS[g]:
                        if source is not None:
                            dve.wait_ge(h_ready, t + 1)
                        dve.bn_stats(st[:, t, :], m.h[:, t, :]).then_inc(st_done, 1)
                    for t in GROUPS[g]:
                        dve.wait_ge(st_done, t + 1)
                        dve.bn_aggr(mv[:, t, :], st[:, t, :]).then_inc(mv_done, 1)

                def scale(g):
                    a, b = GROUPS[g].start, GROUPS[g].stop
                    dve.wait_ge(std_done, g + 1)
                    dve.reciprocal(rstd[:, a:b], std[:, a:b]).then_inc(rstd_done, 1)
                    dve.wait_ge(rstd_done, g + 1)
                    for t in GROUPS[g]:
                        dve.tensor_scalar(m.xn[:, t, :], m.h[:, t, :], mv[:, t, 0:1], rstd[:, t:t + 1],
                                          ALU.subtract, ALU.mult).then_inc(xn_ready, 1)

                statistics(0)
                for g in range(last_group):
                    statistics(g + 1)
                    scale(g)
                scale(last_group)

            @block.tensor
            def _(pe):
                def make(t):
                    if source_pe is not None:
                        source_pe(pe, t, h_ready)

                def turn(t):
                    pe.wait_ge(xn_ready, t + 1)
                    if t >= BANKS:
                        pe.wait_ge(xT_ready, t - BANKS + 1)
                    for c in range(DK):
                        last = pe.transpose(ps[:, XB + t % BANKS, c * TP:(c + 1) * TP], m.xn[:, t, c * 128:(c + 1) * 128],
                                            m.ident[0:TP, 0:TP])
                    last.then_inc(xp_ready, 1)

                def use(t):
                    if use_pe is not None:
                        pe.wait_ge(xT_ready, t + 1)
                        use_pe(pe, t)

                for t in (*GROUPS[0], *GROUPS[1]):
                    make(t)
                for g in range(last_group + 1):
                    ahead = list(GROUPS[g + 2]) if g + 2 <= last_group else []
                    for n, t in enumerate(GROUPS[g]):
                        turn(t)
                        for later in ahead[n * len(ahead) // len(GROUPS[g]):(n + 1) * len(ahead) // len(GROUPS[g])]:
                            make(later)
                        if t >= 2:
                            use(t - 2)
                use(NT - 2)
                use(NT - 1)

            @block.scalar
            def _(act):
                def deviation(g):
                    a, b = GROUPS[g].start, GROUPS[g].stop
                    act.wait_ge(mv_done, b)
                    act.activation(std[:, a:b], mv[:, a:b, 1], ACT.Sqrt, bias=eps[:, 0:1]).then_inc(std_done, 1)

                def keep(g):
                    for t in GROUPS[g]:
                        act.wait_ge(xp_ready, t + 1)
                        act.copy(m.xT[:, :, t * TP:(t + 1) * TP],
                                 ps[:, XB + t % BANKS, 0:DK * TP].rearrange("p (c t) -> p c t", c=DK)).then_inc(xT_ready, 1)

                act.wait_ge(eps_set, 1)
                deviation(0)
                for g in range(last_group):
                    deviation(g + 1)
                    keep(g)
                keep(last_group)


def attend0(nc, sem, m):
    with ExitStack() as ctx:
        def sb(name, shape, dt=F32):
            return ctx.enter_context(nc.sbuf_tensor(name, shape, dt))

        q = sb("q", [128, 2, DK, SEQ])
        k = sb("k", [128, 2, DK, SEQ])
        kd = sb("k_by_head", [128, 2, DK, 8, SEQ])
        qd = sb("q_rem_by_head", [128, 2, DK, 4, 2, REM_B])
        v = sb("v", [128, 2, NU, 3, 4 * OW])
        vr = sb("v_rem", [3 * REM, 2, NU, 4, OW])
        lat = sb("latents", [128, SEQ])
        lat3 = sb("latents_rem", [128, REM, 3])
        p = sb("probs", [128, 2, SEQ, 3])
        pT = sb("probs_T", [128, 2, 512])
        nmax = sb("neg_max", [128, 2, 3])
        rs = sb("recip_sum", [128, 2, 4, 4])
        o = sb("o", [128, 2, 2, NU, HD])

        names = ("v_blank qd_blank ones lat_ps lat_sb q_ps q_sb k_ps k_sb kd_ready qd_ready v_ps v_sb s_ready max_ready "
                 "exps_done pT_ready pT_sb o_ready recip_ready o_norm oT_ready oT_done").split()
        (v_blank, qd_blank, ones, lat_ps, lat_sb, q_ps, q_sb, k_ps, k_sb, kd_ready, qd_ready, v_ps, v_sb, s_ready, max_ready,
         exps_done, pT_ready, pT_sb, o_ready, recip_ready, o_norm, oT_ready, oT_done) = (sem("a0_" + n) for n in names)
        ps = m.ps
        S, T, O, QB, KB = 0, 2, 4, 6, 7
        LOOPS = (B - 2) // 2

        def turns(eng, step):
            step(0, 0, True, False)
            with eng.Fori(0, LOOPS) as i:
                step(i * 2 + 1, 1, False, False)
                step(i * 2 + 2, 0, False, False)
            step(B - 1, 1, False, True)

        with nc.Block() as block:
            @block.tensor
            def _(pe):
                def project_latents(t):
                    pe.wait_ge(oT_done, t + 1)
                    for c in range(DK):
                        last = pe.matmul(ps[:, KB, 0:SEQ], m.wlat[:, c, :], m.xT[:, c, bass.ds(t * SEQ, SEQ)],
                                         start=(c == 0), stop=(c == DK - 1))
                    last.then_inc(lat_ps, 1)

                def project_q(t):
                    for n in range(DK):
                        for c in range(DK):
                            last = pe.matmul(ps[:, QB, n * SEQ:(n + 1) * SEQ], m.wq[:, c, n * 128:(n + 1) * 128],
                                             m.xT[:, c, bass.ds(t * SEQ, SEQ)], start=(c == 0), stop=(c == DK - 1))
                    last.then_inc(q_ps, 1)

                def project_k(t):
                    pe.wait_ge(lat_sb, t + 1)
                    for n in range(DK):
                        last = pe.matmul(ps[:, KB, n * SEQ:(n + 1) * SEQ], m.wkb[0:LAT, n * 128:(n + 1) * 128],
                                         lat[0:LAT, :], start=True, stop=True)
                    last.then_inc(k_ps, 1)

                def project_v(t):
                    pe.wait_ge(q_sb, t + 1)
                    pe.wait_ge(lat_sb, t + 1)
                    pe.matmul(ps[:, QB, 0:D], lat[LAT:128, 0:MAIN], m.wvb[LAT:128, :], start=True, stop=True)
                    pe.matmul(ps[0:3 * REM, QB, D:2 * D], lat3[LAT:128].rearrange("p t r -> p (t r)"),
                              m.wvb[LAT:128, :], start=True, stop=True).then_inc(v_ps, 1)

                def scores(t, n, u):
                    if u == 0:
                        pe.wait_ge(kd_ready, t + 1)
                        pe.wait_ge(qd_ready, t + 1)
                    pe.wait_ge(exps_done, t * NU + u + 1)
                    c, pr = u // 4, u % 4
                    pe.matmul(ps[:, S + u % 2, 0:2 * SEQ], q[:, n, c, 0:MAIN],
                              kd[:, n, c, 2 * pr:2 * pr + 2].rearrange("p h t -> p (h t)"), start=True, stop=True)
                    pe.matmul(ps[:, S + u % 2, 2 * SEQ:3 * SEQ], qd[:, n, c, pr].rearrange("p a t -> p (a t)"),
                              k[:, n, c, :], start=True, stop=True).then_inc(s_ready, 1)

                def turn_probs(g, n):
                    pe.wait_ge(exps_done, g + 3)
                    for s in range(3):
                        pe.transpose(ps[:, T + n, s * 128:(s + 1) * 128], p[:, n, 0:MAIN, s], m.ident[:])
                    pe.transpose(ps[0:3 * REM, T + n, 384:512], p[:, n, MAIN:SEQ, :].rearrange("p t s -> p (t s)"),
                                 m.ident[:]).then_inc(pT_ready, 1)

                def weigh_values(t, n, u):
                    bank, at = O + u // 4, (u % 4) * 4 * OW
                    if u == 0:
                        pe.wait_ge(v_sb, t + 1)
                    if u % 4 == 0:
                        pe.wait_ge(o_norm, t * 2 + u // 4 + 1)
                    pe.wait_ge(pT_sb, t * NU + u + 1)
                    out = ps[:, bank, at:at + 4 * OW]
                    for s in range(3):
                        pe.matmul(out, pT[:, u % 2, s * 128:(s + 1) * 128], v[:, n, u, s, :],
                                  start=(u % 4 == 0 and s == 0), stop=False, skip_group_check=True)
                    last = pe.matmul(out, pT[0:3 * REM, u % 2, 384:512], vr[:, n, u].rearrange("p a w -> p (a w)"),
                                     start=False, stop=True, skip_group_check=True)
                    if u % 4 == 3:
                        last.then_inc(o_ready, 1)

                def turn_out(t):
                    pe.wait_ge(o_norm, t * 2 + 4)
                    for s in range(2):
                        for ab in range(2):
                            last = pe.transpose(ps[:, KB, (2 * s + ab) * 128:(2 * s + ab + 1) * 128],
                                                o[:, s, ab].rearrange("p u w -> p (u w)"), m.ident[:])
                    last.then_inc(oT_ready, 1)

                def step(t, n, first, last):
                    for u in range(NU):
                        scores(t, n, u)
                        if not (first and u == 0):
                            turn_probs(t * NU + u - 1, (u - 1) % 2)
                        if u == 5 and not first:
                            pe.wait_ge(k_sb, t + 1 if last else t + 2)
                            turn_out(t - 1)
                        if u >= 2:
                            weigh_values(t, n, u - 2)
                        elif not first:
                            weigh_values(t - 1, 1 - n, u + 6)
                        if not last:
                            if u == 0:
                                project_latents(t + 1)
                            if u == 1:
                                pe.wait_ge(v_sb, t + 1)
                                project_q(t + 1)
                            if u == 2:
                                project_k(t + 1)
                            if u == 3:
                                project_v(t + 1)

                project_latents(0)
                project_q(0)
                project_k(0)
                project_v(0)
                turns(pe, step)
                turn_probs(B * NU - 1, 1)
                weigh_values(B - 1, 1, NU - 2)
                weigh_values(B - 1, 1, NU - 1)
                turn_out(B - 1)

            @block.vector
            def _(dve):
                dve.memset(v[:], 0.0).then_inc(v_blank, 1)
                dve.memset(ps[:, S:S + 4, :], 0.0)
                dve.wait_ge(v_blank, 1)
                for n in range(2):
                    for s, blk in ((0, 0), (1, 1), (2, 2), (2, 3)):
                        c = blk * OW + HD
                        dve.memset(v[:, n, :, s, c:c + 1], 1.0)
                    dve.tensor_copy(vr[:, n, :, :, HD], m.rem_mask[0:3 * REM, :].unsqueeze(1)
                                    .to_broadcast([3 * REM, NU, 4])).then_inc(ones, 1)

                def keep_k(t, n):
                    dve.wait_ge(k_ps, t + 1)
                    dve.tensor_copy(k[:, n], ps[:, KB, 0:DK * SEQ].rearrange("p (c t) -> p c t", c=DK)).then_inc(k_sb, 1)

                def keep_v(t, n):
                    dve.wait_ge(v_ps, t + 1)
                    vps = ps[:, QB, 0:D].rearrange("p (u a w) -> p u a w", u=NU, a=2)
                    rps = ps[0:3 * REM, QB, D:2 * D].rearrange("p (u a w) -> p u a w", u=NU, a=2)
                    vb = v[:, n].rearrange("p u s (a w) -> p u s a w", a=4)
                    for ab in range(2):
                        dve.tensor_copy(vb[:, :, ab, ab, 0:HD], vps[:, :, ab])
                    dve.tensor_copy(vb[:, :, 2, 2:4, 0:HD], vps)
                    for s in range(2):
                        last = dve.tensor_tensor(
                            vr[:, n, :, 2 * s:2 * s + 2, 0:HD], rps,
                            m.rem_mask[0:3 * REM, 2 * s:2 * s + 2].unsqueeze(1).unsqueeze(3)
                            .to_broadcast([3 * REM, NU, 2, HD]), ALU.mult)
                    last.then_inc(v_sb, 1)

                def normalise_out(t, half):
                    out = ps[:, O + half, 0:16 * OW].rearrange("p (u a w) -> p u a w", u=4, a=4)
                    dve.wait_ge(o_ready, t * 2 + half + 1)
                    dve.reciprocal(rs[:, half], out[:, :, :, HD]).then_inc(recip_ready, 1)
                    dve.wait_ge(recip_ready, t * 2 + half + 1)
                    dve.tensor_tensor(o[:].rearrange("p s a u w -> p u (s a) w")[:, 4 * half:4 * half + 4],
                                      out[:, :, :, 0:HD],
                                      rs[:, half].unsqueeze(3).to_broadcast([128, 4, 4, HD]), ALU.mult)\
                       .then_inc(o_norm, 1)

                def keep_probs(g, n):
                    dve.wait_ge(pT_ready, g + 1)
                    dve.tensor_copy(pT[:, n], ps[:, T + n, :]).then_inc(pT_sb, 1)

                def step(t, n, first, last):
                    for u in range(NU):
                        dve.wait_ge(s_ready, t * NU + u + 1)
                        dve.tensor_reduce(nmax[:, u % 2, :], ps[:, S + u % 2, 0:3 * SEQ]
                                          .rearrange("p (s t) -> p s t", s=3), AX.X, ALU.max, negate=True)\
                           .then_inc(max_ready, 1)
                        if not (first and u == 0):
                            keep_probs(t * NU + u - 1, (u - 1) % 2)
                        if u == 1 and not first:
                            normalise_out(t - 1, 1)
                        if u == 5:
                            normalise_out(t, 0)
                        if not last:
                            if u == 2:
                                keep_k(t + 1, 1 - n)
                            if u == 3:
                                keep_v(t + 1, 1 - n)

                dve.wait_ge(ones, 2)
                keep_k(0, 0)
                keep_v(0, 0)
                turns(dve, step)
                keep_probs(B * NU - 1, 1)
                normalise_out(B - 1, 1)

            @block.gpsimd
            def _(pool):
                pool.memset(qd[:], 0.0).then_inc(qd_blank, 1)
                pool.wait_ge(qd_blank, 1)

                def split_heads(t, n):
                    mask = m.head_mask[:]
                    pool.wait_ge(k_sb, t + 1)
                    for c in range(DK):
                        last = pool.tensor_tensor(kd[:, n, c], k[:, n, c].unsqueeze(1).to_broadcast([128, 8, SEQ]),
                                                  mask.unsqueeze(2).to_broadcast([128, 8, SEQ]), ALU.mult)
                    last.then_inc(kd_ready, 1)
                    pool.wait_ge(q_sb, t + 1)
                    for c in range(DK):
                        last = pool.tensor_tensor(
                            qd[:, n, c, :, :, 0:REM].rearrange("p u a t -> p (u a) t"),
                            q[:, n, c, MAIN:SEQ].unsqueeze(1).to_broadcast([128, 8, REM]),
                            mask.unsqueeze(2).to_broadcast([128, 8, REM]), ALU.mult)
                    last.then_inc(qd_ready, 1)

                with pool.Fori(0, B // 2) as i:
                    for n in range(2):
                        split_heads(i * 2 + n, n)

            @block.scalar
            def _(act):
                act.sem_inc(exps_done, 2)
                act.sem_inc(o_norm, 2)
                act.sem_inc(oT_done, 3)

                def keep_latents(t):
                    act.wait_ge(lat_ps, t + 1)
                    act.copy(lat[:], ps[:, KB, 0:SEQ])
                    act.copy(lat3[LAT:128], ps[LAT:128, KB, MAIN:SEQ].unsqueeze(2).to_broadcast([LAT, REM, 3]))\
                       .then_inc(lat_sb, 1)

                def keep_q(t, n):
                    act.wait_ge(q_ps, t + 1)
                    act.copy(q[:, n], ps[:, QB, 0:DK * SEQ].rearrange("p (c t) -> p c t", c=DK)).then_inc(q_sb, 1)

                def out_back(t):
                    act.wait_ge(oT_ready, t + 1)
                    act.copy(m.xT[:, :, bass.ds(t * SEQ, MAIN)],
                             ps[:, KB, 0:256].rearrange("p (a t) -> p a t", a=2))
                    for ab in range(2):
                        c0 = 256 + ab * (128 + REM_B)
                        last = act.copy(m.xT[:, ab, bass.ds(t * SEQ + MAIN, REM)], ps[:, KB, c0:c0 + REM])
                    last.then_inc(oT_done, 1)

                def step(t, n, first, last):
                    for u in range(NU):
                        act.wait_ge(max_ready, t * NU + u + 1)
                        for s in range(3):
                            x = act.activation(p[:, u % 2, :, s], ps[:, S + u % 2, s * SEQ:(s + 1) * SEQ], ACT.Exp,
                                               bias=nmax[:, u % 2, s:s + 1])
                        x.then_inc(exps_done, 1)
                        if u == 0 and not last:
                            keep_latents(t + 1)
                        if u == 1 and not last:
                            keep_q(t + 1, 1 - n)
                        if u == 6 and not first:
                            out_back(t - 1)

                keep_latents(0)
                keep_q(0, 0)
                turns(act, step)
                out_back(B - 1)


def project0_and_norm(nc, sem, m, d):
    y_ready = sem("wo_ready")
    ps = m.ps

    def on_sync(sp, h_ready, xn_ready):
        sp.dma_start(m.w_red[:], d["w_red"].rearrange("(c p) n -> p c n", p=128)).then_inc(m.w_red_in, 16)
        sources = (d["wg"], d["spread16"], d["diag_mask"], d["iota8"].to_broadcast([TP, E]),
                   d["rows128"].to_broadcast([TP, 21]), d["tiles_j"],
                   d["keep"].unsqueeze(0).to_broadcast([TP, E, NT]), d["before"])
        for dst, src in zip(m.route_tables, sources):
            sp.dma_start(dst[:], src).then_inc(m.route_tables_in, 16)
        sp.wait_ge(m.zero_out, 16)
        for e in range(E):
            sp.dma_start(m.w2[:, e], d["w2"][e].rearrange("(c p) n -> p c n", p=128)).then_inc(m.expert_in, 16)

    def source_pe(pe, t, h_ready):
        if t >= 2:
            pe.wait_ge(h_ready, t - 1)
        for c in range(DK):
            last = pe.matmul(ps[0:TP, t % 2, 0:D], m.xT[:, c, t * TP:(t + 1) * TP], m.wo[:, c, :],
                             start=(c == 0), stop=(c == DK - 1))
        last.then_inc(y_ready, 1)

    def source(dve, t, h_ready):
        dve.wait_ge(y_ready, t + 1)
        dve.tensor_tensor(m.h[:, t, :], m.h[:, t, :], ps[0:TP, t % 2, 0:D], ALU.add).then_inc(h_ready, 1)

    def use_pe(pe, t):
        if t == 0:
            pe.wait_ge(m.w_red_in, 16)
        for c in range(DK):
            pe.matmul(ps[0:TP, RB, t * GD:(t + 1) * GD], m.xT[:, c, t * TP:(t + 1) * TP], m.w_red[:, c, :],
                      start=(c == 0), stop=(c == DK - 1))

    normalise(nc, sem, m, "_1", source, source_pe, use_pe, on_sync)


def combine0_and_norm(nc, sem, m, d):
    gathered = [sem(f"c0_gathered_{g}") for g in range(len(GROUPS))]

    def on_pool(pool):
        for g, tiles in enumerate(GROUPS):
            for t in tiles:
                pool.indirect_dma_start(m.back[:, t, :], None, m.ys,
                                        bass.IndirectOffsetOnAxis(m.slot[:, t:t + 1], 0)).then_inc(gathered[g], 16)

    def source(dve, t, h_ready):
        g = next(g for g, tiles in enumerate(GROUPS) if t in tiles)
        if t == GROUPS[g].start:
            dve.wait_ge(gathered[g], 16 * len(GROUPS[g]))
        dve.scalar_tensor_tensor(m.h[:, t, :], m.back[:, t, :], m.gate[:, t:t + 1], m.h[:, t, :],
                                 ALU.mult, ALU.add).then_inc(h_ready, 1)

    def on_sync(sp, h_ready, xn_ready):
        for dst, src in [(m.wqk[:], d["wqk"].rearrange("(c p) n -> p c n", p=128)),
                         (m.wv[:], d["wv"].rearrange("(c p) n -> p c n", p=128)), (m.cst[:], d["a1_cst"]),
                         (m.bv[:], d["bv"].to_broadcast([128, D])), (m.rel1[:], d["rel_emb"]),
                         (m.buckets[:], d["buckets"]), (m.mask1[:], d["mask1"])]:
            sp.dma_start(dst, src).then_inc(m.attn1_in, 16)

    normalise(nc, sem, m, "_2", source=source, on_sync=on_sync, on_pool=on_pool)


def norm_and_router1(nc, sem, m, d, out):
    def on_sync(sp, h_ready, xn_ready):
        sp.dma_start(m.rw[:], d["router_w"].rearrange("(c p) n -> p c n", p=128)).then_inc(m.router_in, 16)
        sp.dma_start(m.rb[:], d["router_b"].to_broadcast([TP, E])).then_inc(m.router_in, 16)
        sources = (d["bits"], d["before"], d["keep"].unsqueeze(0).to_broadcast([TP, E, NT]), d["tile_row"],
                   d["iota128"].to_broadcast([TP, 128]))
        for dst, src in zip(m.choice_tables, sources):
            sp.dma_start(dst[:], src).then_inc(m.choice_tables_in, 16)
        sp.dma_start(out.rearrange("(t p) d -> p t d", p=TP), m.h[:]).then_inc(m.rows_out, 16)
        for tiles in GROUPS:
            sp.wait_ge(xn_ready, tiles.stop)
            sp.dma_start(m.xrows.rearrange("(t p) d -> p t d", p=TP)[:, tiles.start:tiles.stop],
                         m.xn[:, tiles.start:tiles.stop]).then_inc(m.rows_out, 16)

    def use_pe(pe, t):
        if t == 0:
            pe.wait_ge(m.router_in, 32)
        for c in range(DK):
            pe.matmul(ps[0:TP, RB, t * E:(t + 1) * E], m.xT[:, c, t * TP:(t + 1) * TP], m.rw[:, c, :],
                      start=(c == 0), stop=(c == DK - 1))

    ps = m.ps
    normalise(nc, sem, m, "_3", use_pe=use_pe, on_sync=on_sync)


def build(nc, d, out):
    with ExitStack() as ctx:
        def sb(name, shape, dt=F32, into=ctx):
            return into.enter_context(nc.sbuf_tensor(name, shape, dt))

        def kept(name):
            return ctx.enter_context(nc.semaphore(name))

        stage_sems = []

        def sem(name):
            handle = nc.alloc_semaphore(name)
            stage_sems.append(handle)
            return handle

        def chunked(a):
            return a.rearrange("(c p) n -> p c n", p=128)

        m = Mem()
        m.ps = ctx.enter_context(nc.psum_tensor("psum", [128, 8, 512], F32))
        m.h0 = nc.dram_tensor("h0", [TOK, D], F32).ap()
        m.xs = nc.dram_tensor("expert_rows", [SLOTS, D], F32).ap()
        m.ys = nc.dram_tensor("expert_outs", [SLOTS, D], F32).ap()
        m.relv = nc.dram_tensor("rel_values", [128, 512], F32).ap()
        m.xrows = nc.dram_tensor("normed_rows", [TOK, D], F32).ap()
        m.ident = sb("ident", [128, 128])
        m.h = sb("h", [TP, NT, D])
        m.xT = sb("xT", [128, DK, TOK])
        m.gate = sb("gate", [TP, NT])
        m.slot = sb("slot", [TP, NT], I32)
        m.tile_expert = sb("tile_expert", [1, SLOT_TILES], I32)
        m.zero_out, m.attn_in, m.expert_in = kept("zero_out"), kept("attn_in"), kept("expert_in")
        m.h_in = [kept(f"h_in_{g}") for g in range(len(GROUPS))]
        m.ring_in = [kept("expert1_in_0"), kept("expert1_in_1")]
        m.w_red_in, m.router_in, m.rows_out = kept("w_red_in"), kept("router_in"), kept("rows_out")
        m.attn1_in = kept("attn1_in")
        m.route_tables_in, m.choice_tables_in = kept("route_tables_in"), kept("choice_tables_in")

        with ExitStack() as layer0:
            m.w1 = sb("w1", [128, E, DK, F], into=layer0)
            m.expert_loads = [(m.w1[:, e], chunked(d["w1"][e])) for e in range(E)]
            m.wo = sb("wo", [128, DK, D], into=layer0)
            with ExitStack() as attn:
                m.wq = sb("wq", [128, DK, D], into=attn)
                m.wlat = sb("wlat", [128, DK, 128], into=attn)
                m.wkb = sb("wkb", [128, D], into=attn)
                m.wvb = sb("wvb", [128, D], into=attn)
                m.rem_mask = sb("rem_mask", [128, 4], into=attn)
                m.head_mask = sb("head_mask", [128, 8], into=attn)
                m.zero_row = sb("zero_row", [128, D], into=attn)
                with ExitStack() as first:
                    m.wq_swap = sb("wq_swap", [128, DK, D], into=first)
                    m.wkb_swap = sb("wkb_swap", [128, D], into=first)
                    m.rot_cos = sb("rot_cos", [128, 2, D], into=first)
                    m.rot_sin = sb("rot_sin", [128, 2, D], into=first)
                    m.attn_loads = [
                        (m.wq[:], chunked(d["wq"])), (m.wlat[:], chunked(d["wlat"])),
                        (m.wkb[0:LAT], d["wkb"]), (m.wvb[LAT:128], d["wvb"]),
                        (m.rem_mask[:], d["rem_mask"]), (m.head_mask[:], d["head_mask"]),
                        (m.wo[:], chunked(d["wo"])), (m.wq_swap[:], chunked(d["wq_swap"])),
                        (m.wkb_swap[0:LAT], d["wkb_swap"]),
                        (m.rot_cos[:], d["rot_cos"].unsqueeze(0).to_broadcast([128, 2, D])),
                        (m.rot_sin[:], d["rot_sin"].unsqueeze(0).to_broadcast([128, 2, D]))]
                    m.attn_want = 16 * len(m.attn_loads)
                    tokenise(nc, sem, m, d)
                with nc.sbuf_tensor("xn_0", [TP, NT, D], F32) as m.xn:
                    normalise(nc, sem, m, "_0")
                attend0(nc, sem, m)
            m.w2 = sb("w2", [128, E, FK, D], into=layer0)
            m.w_red = sb("w_red", [128, DK, GD], into=layer0)
            m.route_tables = [
                sb("wg", [E, GD], into=layer0),
                sb("spread16", [GD, 128], into=layer0),
                sb("diag_mask", [128, 8, E], into=layer0),
                sb("iota8", [TP, E], into=layer0),
                sb("rows128", [TP, 21], into=layer0),
                sb("tiles_j", [1, SLOT_TILES], into=layer0),
                sb("scan_keep", [TP, E, NT], into=layer0),
                sb("before", [TP, TP], into=layer0)]
            with nc.sbuf_tensor("xn_1", [TP, NT, D], F32) as m.xn:
                project0_and_norm(nc, sem, m, d)
                route0(nc, sem, m)
            experts0(nc, sem, m, d)
        nc.clear_and_free_semaphores(stage_sems)
        nc.all_engine_barrier()
        stage_sems.clear()

        m.score = sb("score", [TP, NT, E])
        m.gate1 = sb("gate1", [128, E * 4])
        m.row1 = sb("row1", [128, E * 4], I32)
        m.ring1 = sb("expert_w1", [128, 2, DK, F])
        m.ring2 = sb("expert_w2", [128, 2, FK, D])
        with ExitStack() as attn:
            m.wqk = sb("wqk", [128, DK, 128], into=attn)
            m.wv = sb("wv", [128, DK, D], into=attn)
            m.cst = sb("qk_constants", [128, 5], into=attn)
            m.bv = sb("bv", [128, D], into=attn)
            m.rel1 = sb("rel_emb", [32, 1], into=attn)
            m.buckets = sb("buckets", [32, 512], into=attn)
            m.mask1 = sb("mask1", [128, PAIR + REM], into=attn)
            with nc.sbuf_tensor("xn_2", [TP, NT, D], F32) as m.xn:
                with nc.sbuf_tensor("expert_rows_back", [TP, NT, D], F32) as m.back:
                    combine0_and_norm(nc, sem, m, d)
            attend1(nc, sem, m, d)
        with ExitStack() as routing:
            m.xn = sb("xn_3", [TP, NT, D], into=routing)
            m.rw = sb("router_w", [128, DK, E], into=routing)
            m.rb = sb("router_b", [TP, E], into=routing)
            m.choice_tables = [
                sb("bits", [TP, NBITS // 2, 3], I32, into=routing),
                sb("before_1", [TP, TP], into=routing),
                sb("scan_keep_1", [TP, E, NT], into=routing),
                sb("tile_row", [TP, NT, 2], into=routing),
                sb("iota128", [TP, 128], F16, into=routing)]
            norm_and_router1(nc, sem, m, d, out)
            scores1(nc, sem, m)
            choose1(nc, sem, m)
        experts1(nc, sem, m, d, out)


def route0(nc, sem, m):
    with ExitStack() as ctx:
        def tmp(name, shape, dt=F32):
            return ctx.enter_context(nc.sbuf_tensor(name, shape, dt))

        wg, spread, diag, iota8, rows128, tiles_j, keep, before = m.route_tables
        tabs_in = m.route_tables_in
        wg2 = tmp("wg_squares", [E, GD])
        wgs = tmp("wg_norm", [E, 4])
        wgT = tmp("wg_T", [GD, E])
        red = tmp("reduced", [TP, NT * GD])
        redT = tmp("reduced_T", [128, 3, TP])
        wgd = tmp("wg_diag", [128, 8, E])
        ones = tmp("ones_tp", [TP, TP])
        mx = tmp("logit_max", [TP, NT])
        z = tmp("shifted", [TP, NT, E])
        eq = tmp("is_max", [TP, NT, E])
        first = tmp("first_max", [TP, NT])
        oh = tmp("one_hot", [TP, NT, E])
        cs = tmp("tile_counts", [TP, E, NT])
        incl = tmp("counts_incl", [TP, E, NT])
        big = tmp("over_128j", [TP, E, 21])
        ntile = tmp("expert_tiles", [TP, E])
        cumt = tmp("expert_tiles_incl", [TP, E])
        base = tmp("expert_base", [TP, E])
        rank = z
        slotf = tmp("slot_f", [TP, NT])
        past = tmp("past_expert", [1, SLOT_TILES, E])
        ejf = tmp("tile_expert_f", [1, SLOT_TILES])

        wg8_ps, wgd_sb = sem("r0_wg8_ps"), sem("r0_wgd_sb")
        red_ps, red_sb, lg_ps, wg_ps, rank_ps, cnt_ps = (
            sem("r0_" + n) for n in ("red_ps", "red_sb", "lg_ps", "wg_ps", "rank_ps", "cnt_ps"))
        wgsq, wgsum, wgrt, wgmx, wgrc, wgn, wgT_sb = (
            sem("r0_" + n) for n in ("wgsq", "wgsum", "wgrt", "wgmx", "wgrc", "wgn", "wgT"))
        step, exps, slots_ready, scattered = sem("r0_step"), sem("r0_exps"), sem("r0_slots"), sem("r0_scattered")
        ps = m.ps
        with nc.Block() as block:
            @block.tensor
            def _(pe):
                pe.wait_ge(tabs_in, 16 * 8)
                pe.wait_ge(wgn, 1)
                pe.transpose(ps[0:GD, 7, 0:E], wg2[:], m.ident[0:E, 0:E]).then_inc(wg_ps, 1)
                pe.wait_ge(wgT_sb, 1)
                pe.matmul(ps[:, 7, 64:64 + E], spread[:], wgT[:], start=True, stop=True).then_inc(wg8_ps, 1)
                pe.wait_ge(red_sb, 1)
                groups = [(g, min(8, NT - 8 * g)) for g in range(3)]
                for g, n in groups:
                    last = pe.transpose(ps[0:n * GD, 1, g * TP:(g + 1) * TP], red[:, g * 128:g * 128 + n * GD],
                                        m.ident[0:TP, 0:TP])
                last.then_inc(red_ps, 1)
                pe.wait_ge(red_sb, 2)
                pe.wait_ge(wgd_sb, 1)
                for g, n in groups:
                    last = pe.matmul(ps[0:TP, 2, g * 64:g * 64 + n * E], redT[0:n * GD, g, :],
                                     wgd[0:n * GD].rearrange("p t e -> p (t e)")[:, 0:n * E], start=True, stop=True)
                last.then_inc(lg_ps, 1)
                pe.wait_ge(step, 6)
                oh_f = oh[:].rearrange("p t e -> p (t e)")
                pe.matmul(ps[0:TP, 3, 0:NT * E], ones[:], oh_f, start=True, stop=True).then_inc(cnt_ps, 1)
                pe.matmul(ps[0:TP, 4, 0:NT * E], before[:], oh_f, start=True, stop=True).then_inc(rank_ps, 1)

            @block.scalar
            def _(act):
                act.wait_ge(wgsum, 1)
                act.activation(wgs[:, 1:2], wgs[:, 0:1], ACT.Sqrt).then_inc(wgrt, 1)
                act.copy(red[:], ps[0:TP, RB, 0:NT * GD]).then_inc(red_sb, 1)
                act.wait_ge(red_ps, 1)
                act.copy(redT[:], ps[:, 1, 0:3 * TP].rearrange("p (g t) -> p g t", g=3)).then_inc(red_sb, 1)
                act.wait_ge(step, 2)
                act.activation(z[:], z[:], ACT.Exp).then_inc(exps, 1)

            @block.vector
            def _(dve):
                dve.memset(ones[:], 1.0)
                dve.wait_ge(tabs_in, 16 * 8)
                dve.tensor_tensor(wg2[:], wg[:], wg[:], ALU.mult).then_inc(wgsq, 1)
                dve.wait_ge(wgsq, 1)
                dve.tensor_reduce(wgs[:, 0:1], wg2[:], AX.X, ALU.add).then_inc(wgsum, 1)
                dve.wait_ge(wgrt, 1)
                dve.tensor_scalar(wgs[:, 2:3], wgs[:, 1:2], 1e-4, None, ALU.max).then_inc(wgmx, 1)
                dve.wait_ge(wgmx, 1)
                dve.reciprocal(wgs[:, 3:4], wgs[:, 2:3]).then_inc(wgrc, 1)
                dve.wait_ge(wgrc, 1)
                dve.tensor_scalar(wg2[:], wg[:], wgs[:, 3:4], None, ALU.mult).then_inc(wgn, 1)
                dve.wait_ge(wg_ps, 1)
                dve.tensor_copy(wgT[:], ps[0:GD, 7, 0:E]).then_inc(wgT_sb, 1)
                dve.wait_ge(wg8_ps, 1)
                dve.tensor_tensor(wgd[:], ps[:, 7, 64:64 + E].unsqueeze(1).to_broadcast([128, 8, E]), diag[:],
                                  ALU.mult).then_inc(wgd_sb, 1)

                def over(a):
                    return a.unsqueeze(2).to_broadcast([TP, NT, E])

                dve.wait_ge(lg_ps, 1)
                lps = ps[0:TP, 2, 0:NT * E].rearrange("p (t e) -> p t e", e=E)
                dve.tensor_reduce(mx[:], lps, AX.X, ALU.max).then_inc(step, 1)
                dve.wait_ge(step, 1)
                dve.tensor_tensor(z[:], lps, over(mx[:]), ALU.subtract).then_inc(step, 1)
                dve.tensor_tensor(eq[:], lps, over(mx[:]), ALU.is_equal).then_inc(step, 1)
                dve.wait_ge(step, 3)
                i8 = iota8[:].unsqueeze(1).to_broadcast([TP, NT, E])
                dve.tensor_tensor(eq[:], eq[:], i8, ALU.mult).then_inc(step, 1)
                dve.wait_ge(step, 4)
                dve.tensor_reduce(first[:], eq[:], AX.X, ALU.min).then_inc(step, 1)
                dve.wait_ge(step, 5)
                dve.tensor_tensor(oh[:], over(first[:]), i8, ALU.is_equal).then_inc(step, 1)
                dve.wait_ge(exps, 1)
                dve.tensor_reduce(mx[:], z[:], AX.X, ALU.add).then_inc(step, 1)
                dve.wait_ge(step, 7)
                dve.reciprocal(m.gate[:], mx[:]).then_inc(step, 1)
                dve.wait_ge(cnt_ps, 1)
                dve.tensor_copy(cs[:], ps[0:TP, 3, 0:NT * E].rearrange("p (t e) -> p e t", e=E)).then_inc(step, 1)
                dve.wait_ge(step, 9)
                dve.tensor_tensor_scan(incl[:].rearrange("p e t -> p (e t)"), keep[:].rearrange("p e t -> p (e t)"),
                                       cs[:].rearrange("p e t -> p (e t)"), 0.0, ALU.mult, ALU.add).then_inc(step, 1)
                dve.wait_ge(step, 10)
                dve.tensor_tensor(big[:], incl[:, :, NT - 1].unsqueeze(2).to_broadcast([TP, E, 21]),
                                  rows128[:].unsqueeze(1).to_broadcast([TP, E, 21]), ALU.is_gt).then_inc(step, 1)
                dve.tensor_tensor(cs[:], incl[:], cs[:], ALU.subtract).then_inc(step, 1)
                dve.wait_ge(step, 12)
                dve.tensor_reduce(ntile[:], big[:], AX.X, ALU.add).then_inc(step, 1)
                dve.wait_ge(step, 13)
                dve.tensor_tensor_scan(cumt[:], ones[:, 0:E], ntile[:], 0.0, ALU.mult, ALU.add).then_inc(step, 1)
                dve.wait_ge(step, 14)
                dve.tensor_tensor(base[:], cumt[:], ntile[:], ALU.subtract).then_inc(step, 1)
                dve.wait_ge(step, 15)
                dve.tensor_scalar(base[:], base[:], float(SLOT), None, ALU.mult).then_inc(step, 1)
                dve.wait_ge(rank_ps, 1)
                dve.tensor_tensor(rank[:], ps[0:TP, 4, 0:NT * E].rearrange("p (t e) -> p t e", e=E),
                                  cs[:].rearrange("p e t -> p t e"), ALU.add).then_inc(step, 1)
                dve.wait_ge(step, 17)
                dve.tensor_tensor(rank[:], rank[:], base[:].unsqueeze(1).to_broadcast([TP, NT, E]), ALU.add)\
                   .then_inc(step, 1)
                dve.wait_ge(step, 18)
                dve.tensor_tensor(rank[:], rank[:], oh[:], ALU.mult).then_inc(step, 1)
                dve.wait_ge(step, 19)
                dve.tensor_reduce(slotf[:], rank[:], AX.X, ALU.add).then_inc(step, 1)
                dve.wait_ge(step, 20)
                dve.tensor_copy(m.slot[:], slotf[:]).then_inc(slots_ready, 1)
                dve.tensor_tensor(past[:], tiles_j[:].unsqueeze(2).to_broadcast([1, SLOT_TILES, E]),
                                  cumt[0:1, :].unsqueeze(1).to_broadcast([1, SLOT_TILES, E]), ALU.is_ge).then_inc(step, 1)
                dve.wait_ge(step, 21)
                dve.tensor_reduce(ejf[:], past[:], AX.X, ALU.add).then_inc(step, 1)
                dve.wait_ge(step, 22)
                dve.tensor_scalar(m.tile_expert[:], ejf[:], float(E - 1), None, ALU.min)

            @block.gpsimd
            def _(pool):
                pool.wait_ge(slots_ready, 1)
                pool.wait_ge(m.zero_out, 16)
                for t in range(NT):
                    pool.indirect_dma_start(m.xs, bass.IndirectOffsetOnAxis(m.slot[:, t:t + 1], 0),
                                            m.xn[:, t, :], None).then_inc(scattered, 16)
                pool.wait_ge(scattered, 16 * NT)


def experts0(nc, sem, m, d):
    with ExitStack() as ctx:
        def tmp(name, shape, dt=F32):
            return ctx.enter_context(nc.sbuf_tensor(name, shape, dt))

        b1T = tmp("b1T", [128, E * FK])
        b2 = tmp("b2", [128, E, D])
        b_in = sem("e0_b_in")
        x = tmp("e0_x", [128, 2, D])
        xT = tmp("e0_xT", [128, 2, DK, SLOT])
        u = tmp("e0_u", [128, F])
        hT = tmp("e0_hT", [128, FK, SLOT])
        y = tmp("e0_y", [128, 2, D])
        x_in, y_out = [sem("e0_x_in_0"), sem("e0_x_in_1")], sem("e0_y_out")
        xp_ready, xT_ready, u_ready, u_sb, up_ready, hT_ready, y_ready, y_sb = (
            sem("e0_" + n) for n in ("xp", "xT", "u", "u_sb", "up", "hT", "y", "y_sb"))
        ps = m.ps
        XB, UB, TB, YB = 0, 1, 3, 5
        xs_t = m.xs.rearrange("(t p) d -> p t d", p=SLOT)
        ys_t = m.ys.rearrange("(t p) d -> p t d", p=SLOT)
        LOOPS = (SLOT_TILES - 2) // 2
        assert SLOT_TILES % 2 == 0

        def expert_of(eng, j):
            return eng.value_load(m.tile_expert[0:1, bass.ds(j, 1)], min_val=0, max_val=E - 1)

        with nc.Block() as block:
            @block.sync
            def _(sp):
                sp.dma_start(b1T[:], d["b1T"]).then_inc(b_in, 16)
                sp.dma_start(b2[:], d["b2"].unsqueeze(0).to_broadcast([128, E, D])).then_inc(b_in, 16)
                for n in range(2):
                    sp.dma_start(x[:, n:n + 1, :], xs_t[:, n:n + 1, :]).then_inc(x_in[n], 16)
                with sp.Fori(0, SLOT_TILES // 2 - 1) as i:
                    for n in range(2):
                        sp.wait_ge(xp_ready, i * 2 + n + 1)
                        sp.dma_start(x[:, n:n + 1, :], xs_t[:, bass.ds(i * 2 + n + 2, 1), :]).then_inc(x_in[n], 16)

            @block.tensor
            def _(pe):
                w1f = m.w1[:].rearrange("p e c f -> p (e c f)")
                w2f = m.w2[:].rearrange("p e c f -> p (e c f)")

                def turn_x(j, n, loads):
                    pe.wait_ge(x_in[n], loads * 16)
                    for c in range(DK):
                        last = pe.transpose(ps[:, XB, c * 128:(c + 1) * 128], x[:, n, c * 128:(c + 1) * 128],
                                            m.ident[:])
                    last.then_inc(xp_ready, 1)

                def up(j, n):
                    e = expert_of(pe, j)
                    pe.wait_ge(xT_ready, j + 1)
                    for f in range(2):
                        for c in range(DK):
                            last = pe.matmul(ps[:, UB + f, :], xT[:, n, c, :],
                                             w1f[:, bass.ds(e * (DK * F) + c * F + f * 512, 512)],
                                             start=(c == 0), stop=(c == DK - 1))
                        last.then_inc(u_ready, 1)

                def turn_u(j):
                    for f in range(2):
                        pe.wait_ge(u_sb, j * 2 + f + 1)
                        for c in range(4):
                            last = pe.transpose(ps[:, TB + f, c * 128:(c + 1) * 128],
                                                u[:, f * 512 + c * 128:f * 512 + (c + 1) * 128], m.ident[:])
                        last.then_inc(up_ready, 1)

                def down(j, n):
                    e = expert_of(pe, j)
                    pe.wait_ge(hT_ready, j * 2 + 2)
                    pe.wait_ge(y_sb, j + 1)
                    for c in range(FK):
                        last = pe.matmul(ps[:, YB + n, 0:D], hT[:, c, :],
                                         w2f[:, bass.ds(e * (FK * D) + c * D, D)],
                                         start=(c == 0), stop=(c == FK - 1))
                    last.then_inc(y_ready, 1)

                def step(j, n, loads, more):
                    up(j, n)
                    down(j - 1, 1 - n)
                    if more:
                        turn_x(j + 1, 1 - n, loads)
                    turn_u(j)

                pe.wait_ge(m.expert_in, 32 * E)
                turn_x(0, 0, 1)
                up(0, 0)
                turn_x(1, 1, 1)
                turn_u(0)
                with pe.Fori(0, LOOPS) as i:
                    step(i * 2 + 1, 1, i + 2, True)
                    step(i * 2 + 2, 0, i + 2, True)
                step(SLOT_TILES - 1, 1, 0, False)
                down(SLOT_TILES - 1, 1)

            @block.scalar
            def _(act):
                act.sem_inc(y_sb, 2)
                act.wait_ge(b_in, 32)

                def tile(j):
                    e = expert_of(act, j)
                    for f in range(2):
                        act.wait_ge(up_ready, j * 2 + f + 1)
                        for c in range(4):
                            last = act.activation(hT[:, f * 4 + c, :], ps[:, TB + f, c * 128:(c + 1) * 128],
                                                  ACT.Gelu, bias=b1T[:, bass.ds(e * FK + f * 4 + c, 1)])
                        last.then_inc(hT_ready, 1)

                with act.Fori(0, SLOT_TILES // 4) as i:
                    for n in range(4):
                        tile(i * 4 + n)

            @block.vector
            def _(dve):
                dve.wait_ge(b_in, 32)

                def turned_x(n, count):
                    dve.wait_ge(xp_ready, count)
                    dve.tensor_copy(xT[:, n], ps[:, XB, 0:256].rearrange("p (c t) -> p c t", c=DK)).then_inc(xT_ready, 1)

                def hidden(j):
                    for f in range(2):
                        dve.wait_ge(u_ready, j * 2 + f + 1)
                        dve.tensor_copy(u[:, f * 512:(f + 1) * 512], ps[:, UB + f, :]).then_inc(u_sb, 1)

                def finish(j, n, stored):
                    e = expert_of(dve, j)
                    dve.wait_ge(y_ready, j + 1)
                    if stored is not None:
                        dve.wait_ge(y_out, stored)
                    dve.tensor_tensor(y[:, n:n + 1, :], ps[:, YB + n, 0:D].unsqueeze(1), b2[:, bass.ds(e, 1), :],
                                      ALU.add).then_inc(y_sb, 1)

                turned_x(0, 1)
                hidden(0)
                turned_x(1, 2)
                hidden(1)
                finish(0, 0, None)
                turned_x(0, 3)
                hidden(2)
                finish(1, 1, None)
                turned_x(1, 4)
                with dve.Fori(1, LOOPS) as i:
                    for n in range(2):
                        j = i * 2 + 1 + n
                        hidden(j)
                        finish(j - 1, n, i * 32)
                        turned_x(n, j + 2)
                hidden(SLOT_TILES - 1)
                finish(SLOT_TILES - 2, 0, 16 * (SLOT_TILES - 2))
                finish(SLOT_TILES - 1, 1, 16 * (SLOT_TILES - 2))

            @block.gpsimd
            def _(pool):
                with pool.Fori(0, SLOT_TILES // 2) as i:
                    for n in range(2):
                        pool.wait_ge(y_sb, i * 2 + n + 3)
                        pool.dma_start(ys_t[:, bass.ds(i * 2 + n, 1), :], y[:, n:n + 1, :]).then_inc(y_out, 16)
                pool.wait_ge(y_out, 16 * SLOT_TILES)


def attend1(nc, sem, m, d):
    with ExitStack() as ctx:
        def sb(name, shape, dt=F32):
            return ctx.enter_context(nc.sbuf_tensor(name, shape, dt))

        PAIRS = B // 2
        W = PAIR + REM
        w_in, wqk, wv, cst, bv = m.attn1_in, m.wqk, m.wv, m.cst, m.bv
        rel1, buckets, mask = m.rel1, m.buckets, m.mask1
        rel = sb("a1_rel", [32, 128])
        relv = sb("a1_relv", [128, 512])
        bias = sb("a1_bias", [128, W])
        xr = sb("a1_x_rem", [128, 2, DK, 2, 64])
        qk = sb("a1_qk", [128, 2, PAIR])
        y = sb("a1_y", [128, 2, W])
        z = sb("a1_y_is_zero", [128, 2, W])
        r = sb("a1_recip", [128, 2, W])
        gl = sb("a1_gelu", [128, 2, W])
        at = sb("a1_attn", [128, 2, W])
        q = sb("a1_q", [128, TOK])
        k = sb("a1_k", [128, TOK])
        v = sb("a1_v", [128, PAIRS, 3, D])

        names = ("zero rel_wide rel_ps rel_sb rel_out bias_in bias_sc x_rem qk_ps qk_sb q_sb k_sb v_ps v_sum v_sb "
                 "s_ps y_raw y_zero y_sb recip masked gelu attn o_ps o_sb turned added").split()
        (zero, rel_wide, rel_ps, rel_sb, rel_out, bias_in, bias_sc, x_rem, qk_ps, qk_sb, q_sb, k_sb, v_ps, v_sum,
         v_sb, s_ps, y_raw, y_zero, y_sb, recip, masked, gelu, attn, o_ps, o_sb, turned, added) = (
            sem("a1_" + n) for n in names)
        ps = m.ps
        QB, VB = 0, 2
        TB, OB, SB = 0, 2, 6
        REL = 7
        STD = float(np.sqrt(0.25 * np.pi))
        MU = float(np.sqrt(0.5))

        def tiles_of(p):
            return range(p * PAIR // TP, (p + 1) * PAIR // TP)

        with nc.Block() as block:
            @block.sync
            def _(sp):
                sp.wait_ge(rel_sb, 1)
                sp.dma_start(m.relv, relv[:]).then_inc(rel_out, 16)
                sp.wait_ge(rel_out, 16)
                def strip(rows, cols):
                    return bass.AP(m.relv.tensor, m.relv.offset + SEQ - 1, [[511, rows], [1, cols]])
                sp.wait_ge(zero, 2)
                for b in range(2):
                    sp.dma_start(bias[:, b * SEQ:(b + 1) * SEQ], strip(128, SEQ)).then_inc(bias_in, 16)
                    sp.dma_start(bias[64 * b:64 * b + REM, PAIR:W], strip(REM, REM)).then_inc(bias_in, 16)
                for e in range(2):
                    sp.dma_start(m.ring1[:, e], d["w1_1"][e].rearrange("(c p) f -> p c f", p=128)).then_inc(m.ring_in[e], 16)
                    sp.dma_start(m.ring2[:, e], d["w2_1"][e].rearrange("(c p) n -> p c n", p=128)).then_inc(m.ring_in[e], 16)

            @block.tensor
            def _(pe):
                pe.wait_ge(w_in, 16 * 7)
                pe.wait_ge(rel_wide, 1)
                pe.matmul(ps[:, REL, :], rel[:], buckets[:], start=True, stop=True).then_inc(rel_ps, 1)
                for p in range(PAIRS):
                    if p >= 2:
                        pe.wait_ge(qk_sb, p - 1)
                    for c in range(DK):
                        last = pe.matmul(ps[:, QB + p % 2, 0:PAIR], wqk[:, c, :], m.xT[:, c, p * PAIR:(p + 1) * PAIR],
                                         start=(c == 0), stop=(c == DK - 1))
                    last.then_inc(qk_ps, 1)
                    if p >= 2:
                        pe.wait_ge(v_sum, p - 1)
                    bank = VB + 2 * (p % 2)
                    for b in range(2):
                        o = (2 * p + b) * SEQ
                        for c in range(DK):
                            pe.matmul(ps[:, bank, b * D:(b + 1) * D], m.xT[:, c, o:o + MAIN], wv[:, c, :],
                                      start=(c == 0), stop=(c == DK - 1))
                    pe.wait_ge(x_rem, p + 1)
                    for c in range(DK):
                        last = pe.matmul(ps[:, bank + 1, 0:D], xr[:, p % 2, c].rearrange("p b t -> p (b t)"), wv[:, c, :],
                                         start=(c == 0), stop=(c == DK - 1))
                    last.then_inc(v_ps, 1)

                def scores(p):
                    if p >= 2:
                        pe.wait_ge(y_raw, p - 1)
                    for b in range(2):
                        o = (2 * p + b) * SEQ
                        pe.matmul(ps[:, SB + p % 2, b * SEQ:(b + 1) * SEQ], k[:, o:o + MAIN], q[:, o:o + SEQ],
                                  start=True, stop=True)
                    for b in range(2):
                        o = (2 * p + b) * SEQ
                        last = pe.matmul(ps[64 * b:64 * b + REM, SB + p % 2, PAIR:W], k[:, o + MAIN:o + SEQ],
                                         q[:, o + MAIN:o + SEQ], start=True, stop=True)
                    last.then_inc(s_ps, 1)

                def weigh_values(p):
                    pe.wait_ge(attn, p + 1)
                    if p >= 2:
                        pe.wait_ge(o_sb, p - 1)
                    for b in range(2):
                        bank = OB + 2 * (p % 2) + b
                        rows = slice(64 * b, 64 * b + REM)
                        for c in range(DK):
                            pe.matmul(ps[:, bank, c * SEQ:(c + 1) * SEQ], v[:, p, b, c * 128:(c + 1) * 128],
                                      at[:, p % 2, b * SEQ:(b + 1) * SEQ], start=True, stop=False, skip_group_check=True)
                            last = pe.matmul(ps[:, bank, c * SEQ + MAIN:(c + 1) * SEQ], v[rows, p, 2, c * 128:(c + 1) * 128],
                                             at[rows, p % 2, PAIR:W], start=False, stop=True, skip_group_check=True)
                    last.then_inc(o_ps, 1)

                def turn_back(p):
                    pe.wait_ge(o_sb, p + 1)
                    for t in tiles_of(p):
                        if t >= 2:
                            pe.wait_ge(added, t - 1)
                        for c in range(DK):
                            last = pe.transpose(ps[0:TP, TB + t % 2, c * 128:(c + 1) * 128],
                                                m.xT[:, c, t * TP:(t + 1) * TP], m.ident[:])
                        last.then_inc(turned, 1)

                pe.wait_ge(q_sb, PAIRS)
                pe.wait_ge(k_sb, PAIRS)
                pe.wait_ge(v_sb, PAIRS)
                scores(0)
                scores(1)
                for p in range(PAIRS):
                    if p + 2 < PAIRS:
                        scores(p + 2)
                    if p >= 2:
                        turn_back(p - 2)
                    if p >= 1:
                        weigh_values(p - 1)
                weigh_values(PAIRS - 1)
                turn_back(PAIRS - 2)
                turn_back(PAIRS - 1)

            @block.gpsimd
            def _(pool):
                pool.memset(xr[:], 0.0).then_inc(zero, 1)
                pool.memset(bias[:], 0.0).then_inc(zero, 1)
                pool.wait_ge(w_in, 16 * 7)
                pool.tensor_copy(rel[:], rel1[:].to_broadcast([32, 128])).then_inc(rel_wide, 1)
                pool.wait_ge(zero, 2)
                for p in range(PAIRS):
                    if p >= 2:
                        pool.wait_ge(v_ps, p - 1)
                    pair = m.xT[:, :, p * PAIR:(p + 1) * PAIR].rearrange("p c (b t) -> p c b t", b=2)
                    pool.tensor_copy(xr[:, p % 2, :, :, 0:REM], pair[:, :, :, MAIN:SEQ]).then_inc(x_rem, 1)

                def find_zeros(p):
                    pool.wait_ge(y_raw, p + 1)
                    pool.tensor_scalar(z[:, p % 2], y[:, p % 2], 0.0, 1e-6, ALU.is_equal, ALU.mult).then_inc(y_zero, 1)
                    pool.wait_ge(y_zero, p + 1)
                    pool.tensor_tensor(y[:, p % 2], y[:, p % 2], z[:, p % 2], ALU.add).then_inc(y_sb, 1)

                def apply_mask(p):
                    pool.wait_ge(recip, p + 1)
                    pool.tensor_tensor(r[:, p % 2], r[:, p % 2], mask[:], ALU.mult).then_inc(masked, 1)

                find_zeros(0)
                for p in range(PAIRS):
                    if p + 1 < PAIRS:
                        find_zeros(p + 1)
                    apply_mask(p)

            @block.vector
            def _(dve):
                dve.memset(ps[:, SB, :], 0.0)
                dve.wait_ge(rel_ps, 1)
                dve.tensor_scalar(relv[:], ps[:, REL, :], float(128 ** 0.5), None, ALU.mult).then_inc(rel_sb, 1)
                dve.wait_ge(w_in, 16 * 7)
                for p in range(PAIRS):
                    n, cols = p % 2, slice(p * PAIR, (p + 1) * PAIR)
                    dve.wait_ge(qk_sb, p + 1)
                    dve.tensor_scalar(q[:, cols], qk[:, n], cst[:, 1:2], cst[:, 3:4], ALU.mult, ALU.add).then_inc(q_sb, 1)
                    dve.tensor_scalar(k[:, cols], qk[:, n], cst[:, 2:3], cst[:, 4:5], ALU.mult, ALU.add).then_inc(k_sb, 1)
                    dve.wait_ge(v_ps, p + 1)
                    bank = VB + 2 * n
                    dve.tensor_tensor(v[:, p], ps[:, bank:bank + 2, :].rearrange("p k (b n) -> p (k b) n", b=2)[:, 0:3],
                                      bv[:].unsqueeze(1).to_broadcast([128, 3, D]), ALU.add).then_inc(v_sum, 1)
                dve.wait_ge(bias_in, 64)
                dve.tensor_scalar(bias[:], bias[:], 1.0 / STD, -MU / STD, ALU.mult, ALU.add).then_inc(bias_sc, 1)
                dve.wait_ge(bias_sc, 1)

                def argument(p):
                    dve.wait_ge(s_ps, p + 1)
                    if p >= 2:
                        dve.wait_ge(gelu, p - 1)
                        dve.wait_ge(recip, p - 1)
                    dve.scalar_tensor_tensor(y[:, p % 2], ps[:, SB + p % 2, 0:W], 1.0 / (SEQ * STD), bias[:],
                                             ALU.mult, ALU.add).then_inc(y_raw, 1)

                def invert(p):
                    dve.wait_ge(y_sb, p + 1)
                    if p >= 2:
                        dve.wait_ge(attn, p - 1)
                    dve.reciprocal(r[:, p % 2], y[:, p % 2]).then_inc(recip, 1)

                def attention(p):
                    dve.wait_ge(masked, p + 1)
                    dve.wait_ge(gelu, p + 1)
                    if p >= 2:
                        dve.wait_ge(o_ps, p - 1)
                    dve.tensor_tensor(at[:, p % 2], gl[:, p % 2], r[:, p % 2], ALU.mult).then_inc(attn, 1)

                def add_back(p):
                    for t in tiles_of(p):
                        dve.wait_ge(turned, t + 1)
                        dve.tensor_tensor(m.h[:, t, :], m.h[:, t, :], ps[0:TP, TB + t % 2, 0:D], ALU.add).then_inc(added, 1)

                argument(0)
                for p in range(PAIRS):
                    if p + 1 < PAIRS:
                        argument(p + 1)
                    invert(p)
                    if p >= 1:
                        attention(p - 1)
                    if p >= 2:
                        add_back(p - 2)
                attention(PAIRS - 1)
                add_back(PAIRS - 2)
                add_back(PAIRS - 1)

            @block.scalar
            def _(act):
                act.wait_ge(w_in, 16 * 7)
                for p in range(PAIRS):
                    act.wait_ge(qk_ps, p + 1)
                    if p >= 2:
                        act.wait_ge(q_sb, p - 1)
                        act.wait_ge(k_sb, p - 1)
                    act.activation(qk[:, p % 2], ps[:, QB + p % 2, 0:PAIR], ACT.Silu, bias=cst[:, 0:1]).then_inc(qk_sb, 1)
                    act.wait_ge(v_sum, p + 1)
                    act.activation(v[:, p], v[:, p], ACT.Silu).then_inc(v_sb, 1)

                def phi(p):
                    act.wait_ge(y_sb, p + 1)
                    if p >= 2:
                        act.wait_ge(attn, p - 1)
                    act.activation(gl[:, p % 2], y[:, p % 2], ACT.Gelu).then_inc(gelu, 1)

                def keep_out(p):
                    act.wait_ge(o_ps, p + 1)
                    bank = OB + 2 * (p % 2)
                    pair = m.xT[:, :, p * PAIR:(p + 1) * PAIR].rearrange("p c (b t) -> p b c t", b=2)
                    act.copy(pair, ps[:, bank:bank + 2, 0:2 * SEQ].rearrange("p b (c t) -> p b c t", c=DK))\
                       .then_inc(o_sb, 1)

                for p in range(PAIRS):
                    phi(p)
                    if p >= 2:
                        keep_out(p - 2)
                keep_out(PAIRS - 2)
                keep_out(PAIRS - 1)


def scores1(nc, sem, m):
    with ExitStack() as ctx:
        def tmp(name, shape, dt=F32):
            return ctx.enter_context(nc.sbuf_tensor(name, shape, dt))

        mx = tmp("s1_max", [TP, NT])
        rsum = tmp("s1_rsum", [TP, NT])
        z = tmp("s1_z", [TP, NT, E])
        step, exps = sem("s1_step"), sem("s1_exps")
        ps = m.ps
        with nc.Block() as block:
            @block.scalar
            def _(act):
                act.wait_ge(step, 3)
                act.activation(z[:], z[:], ACT.Exp).then_inc(exps, 1)

            @block.vector
            def _(dve):
                def over(a):
                    return a.unsqueeze(2).to_broadcast([TP, NT, E])

                dve.tensor_tensor(z[:], ps[0:TP, RB, 0:NT * E].rearrange("p (t e) -> p t e", e=E),
                                  m.rb[:].unsqueeze(1).to_broadcast([TP, NT, E]), ALU.add).then_inc(step, 1)
                dve.wait_ge(step, 1)
                dve.tensor_reduce(mx[:], z[:], AX.X, ALU.max).then_inc(step, 1)
                dve.wait_ge(step, 2)
                dve.tensor_tensor(z[:], z[:], over(mx[:]), ALU.subtract).then_inc(step, 1)
                dve.wait_ge(exps, 1)
                dve.tensor_reduce(mx[:], z[:], AX.X, ALU.add).then_inc(step, 1)
                dve.wait_ge(step, 4)
                dve.reciprocal(rsum[:], mx[:]).then_inc(step, 1)
                dve.wait_ge(step, 5)
                dve.tensor_tensor(m.score[:], z[:], over(rsum[:]), ALU.mult)


def choose1(nc, sem, m):
    with ExitStack() as ctx:
        def tmp(name, shape, dt=F32):
            return ctx.enter_context(nc.sbuf_tensor(name, shape, dt))

        NB = NBITS // 2
        UNROLL = 3
        bits, before, keep, tilerow, iota = m.choice_tables
        ld = m.choice_tables_in
        thr = tmp("threshold", [TP, UNROLL, 4, E])
        cand = tmp("candidates", [TP, 3, E], I32)
        ge = tmp("at_least", [TP, 3, NT, E])
        cnts = tmp("candidate_counts", [TP, 3, E])
        cnt = tmp("count", [TP, E])
        ones = tmp("ones_c1", [TP, TP])
        gt = tmp("above", [TP, NT, E])
        eq = tmp("ties", [TP, NT, E])
        need = tmp("need", [TP, E])
        cs = tmp("c1_counts", [TP, E, NT])
        incl = tmp("c1_incl", [TP, E, NT])
        rank = tmp("c1_rank", [TP, NT, E])
        rest = tmp("c1_rest", [TP, NT, E])
        left = tmp("c1_left", [TP, NT, E])
        rec = tmp("records", [TP, NT, E, 5], BF16)
        place = tmp("placed_records", [TP, NT, E, 4, 5], BF16)
        quart = tmp("row_tile", [TP, NT, E])
        inq = tmp("in_row_tile", [TP, NT, E, 4], BF16)
        part = tmp("row_in_tile", [TP, NT, E], F16)
        zeros = tmp("c1_zeros", [TP, 256], BF16)
        hot = tmp("slot_hot", [TP, 2, E, 128], BF16)
        found = tmp("found", [128, E * 4, 5])
        rowf = tmp("row_f", [128, E * 4])

        init = sem("c1_init")
        c_cand, c_ge, c_cnt, c_tot, c_ok, c_thr = (sem("c1_" + n) for n in ("cand", "ge", "cnt", "tot", "ok", "thr"))
        rec_step, part_ready = sem("c1_rec"), sem("c1_part")
        step, tie_ps, pos_ps, hot_ready, hot_used, found_ps = (
            sem("c1_" + n) for n in ("step", "tie_ps", "pos_ps", "hot", "hot_used", "found_ps"))
        ps = m.ps
        NE = NT * E

        def flat(a):
            return a[:].rearrange("p t e -> p (t e)")

        def by_tile(a):
            return a.rearrange("p (t e) -> p t e", e=E)

        def spread(a):
            return a.unsqueeze(1).to_broadcast([TP, NT, E])

        with nc.Block() as block:
            @block.sync
            def _(sp):
                sp.wait_ge(m.rows_out, 16 * (1 + len(GROUPS)))

            @block.vector
            def _(dve):
                dve.memset(thr[:], 0).then_inc(init, 1)
                dve.memset(ones[:], 1.0).then_inc(init, 1)
                dve.memset(zeros[:], 0.0).then_inc(init, 1)
                dve.wait_ge(ld, 16 * 5)
                dve.wait_ge(init, 3)
                dve.sem_inc(c_thr, 1)
                with dve.Fori(0, NB // UNROLL) as i:
                    for n in range(UNROLL):
                        k = i * UNROLL + n
                        dve.wait_ge(c_thr, k + 1)
                        dve.tensor_tensor(cand[:], thr[:, n, 0, :].bitcast(I32).unsqueeze(1).to_broadcast([TP, 3, E]),
                                          bits[:, bass.ds(k, 1), :].rearrange("p a b -> p (a b)").unsqueeze(2)
                                          .to_broadcast([TP, 3, E]), ALU.bitwise_or).then_inc(c_cand, 1)
                        dve.wait_ge(c_cand, k + 1)
                        dve.tensor_tensor(ge[:], m.score[:].unsqueeze(1).to_broadcast([TP, 3, NT, E]),
                                          cand[:].bitcast(F32).unsqueeze(2).to_broadcast([TP, 3, NT, E]), ALU.is_ge)\
                           .then_inc(c_ge, 1)
                        dve.wait_ge(c_ge, k + 1)
                        dve.tensor_reduce(cnts[:], ge[:].rearrange("p c t e -> p c e t"), AX.X, ALU.add).then_inc(c_cnt, 1)
                        dve.wait_ge(c_tot, k + 1)
                        dve.scalar_tensor_tensor(thr[:, n, 1:4, :], ps[0:TP, 0, 0:3 * E].rearrange("p (c e) -> p c e", e=E),
                                                 float(TOPK), cand[:].bitcast(F32), ALU.is_ge, ALU.mult).then_inc(c_ok, 1)
                        dve.wait_ge(c_ok, k + 1)
                        dve.tensor_reduce(thr[:, (n + 1) % UNROLL, 0, :], thr[:, n].rearrange("p c e -> p e c"), AX.X, ALU.max)\
                           .then_inc(c_thr, 1)
                dve.wait_ge(c_thr, NB + 1)
                tf = spread(thr[:, 0, 0, :])
                dve.tensor_tensor(gt[:], m.score[:], tf, ALU.is_gt).then_inc(step, 1)
                dve.tensor_tensor(eq[:], m.score[:], tf, ALU.is_equal).then_inc(step, 1)
                dve.wait_ge(step, 2)
                dve.tensor_reduce(cnt[:], gt[:].rearrange("p t e -> p e t"), AX.X, ALU.add).then_inc(step, 1)
                dve.wait_ge(tie_ps, 1)
                dve.tensor_scalar(need[:], ps[0:TP, 1, 0:E], -1.0, float(TOPK), ALU.mult, ALU.add).then_inc(step, 1)

                def prefix(bank, at):
                    dve.tensor_copy(cs[:], by_tile(ps[0:TP, bank, 0:NE]).rearrange("p t e -> p e t")).then_inc(step, 1)
                    dve.wait_ge(step, at + 1)
                    dve.tensor_tensor_scan(incl[:].rearrange("p e t -> p (e t)"), keep[:].rearrange("p e t -> p (e t)"),
                                           cs[:].rearrange("p e t -> p (e t)"), 0.0, ALU.mult, ALU.add).then_inc(step, 1)
                    dve.wait_ge(step, at + 2)
                    dve.tensor_tensor(cs[:], incl[:], cs[:], ALU.subtract).then_inc(step, 1)
                    dve.wait_ge(step, at + 3)
                    dve.tensor_tensor(rank[:], by_tile(ps[0:TP, bank + 1, 0:NE]), cs[:].rearrange("p e t -> p t e"),
                                      ALU.add).then_inc(step, 1)
                    dve.wait_ge(step, at + 4)

                prefix(2, 4)
                dve.tensor_tensor(rest[:], rank[:], spread(need[:]), ALU.is_lt).then_inc(step, 1)
                dve.wait_ge(step, 9)
                dve.tensor_tensor(eq[:], eq[:], rest[:], ALU.mult).then_inc(step, 1)
                dve.wait_ge(step, 10)
                dve.tensor_tensor(gt[:], gt[:], eq[:], ALU.add).then_inc(step, 1)
                dve.wait_ge(pos_ps, 1)
                prefix(4, 11)
                dve.scalar_tensor_tensor(rank[:], rank[:], 1.0, gt[:], ALU.add, ALU.mult).then_inc(step, 1)
                dve.wait_ge(step, 16)
                dve.tensor_scalar(rank[:], rank[:], -1.0, None, ALU.add).then_inc(step, 1)
                dve.wait_ge(step, 17)
                dve.tensor_scalar(quart[:], rank[:], 128.0, None, ALU.is_ge).then_inc(step, 1)
                for c in (2, 3):
                    dve.wait_ge(step, 16 + c)
                    dve.scalar_tensor_tensor(quart[:], rank[:], 128.0 * c, quart[:], ALU.is_ge, ALU.add).then_inc(step, 1)
                dve.wait_ge(step, 20)
                dve.scalar_tensor_tensor(part[:], quart[:], -128.0, rank[:], ALU.mult, ALU.add).then_inc(part_ready, 1)
                for c in range(4):
                    dve.tensor_scalar(inq[:, :, :, c], quart[:], float(c), None, ALU.is_equal).then_inc(step, 1)
                dve.wait_ge(step, 24)
                dve.wait_ge(rec_step, 6)
                for c in range(5):
                    dve.tensor_tensor(place[:, :, :, :, c], inq[:],
                                      rec[:, :, :, c].unsqueeze(3).to_broadcast([TP, NT, E, 4]), ALU.mult).then_inc(step, 1)
                dve.wait_ge(part_ready, 1)

                with dve.Fori(0, NT // 2) as i:
                    for n in range(2):
                        dve.wait_ge(hot_used, i * 2 + n + 1)
                        dve.tensor_tensor(hot[:, n], iota[:].unsqueeze(1).to_broadcast([TP, E, 128]),
                                          part[:, bass.ds(i * 2 + n, 1), :].rearrange("p a e -> p (a e)")
                                          .unsqueeze(2).to_broadcast([TP, E, 128]), ALU.is_equal).then_inc(hot_ready, 1)
                dve.wait_ge(found_ps, 1)
                dve.tensor_copy(found[:], ps[:, 6, 0:E * 20].rearrange("p (s r) -> p s r", r=5)).then_inc(step, 1)
                dve.wait_ge(step, 30)
                dve.scalar_tensor_tensor(rowf[:], found[:, :, 0], float(TP), found[:, :, 1], ALU.mult, ALU.add)\
                   .then_inc(step, 1)
                dve.tensor_tensor(m.gate1[:], found[:, :, 2], found[:, :, 3], ALU.add).then_inc(step, 1)
                dve.wait_ge(step, 32)
                dve.tensor_copy(m.row1[:], rowf[:])
                dve.tensor_tensor(m.gate1[:], m.gate1[:], found[:, :, 4], ALU.add)

            @block.gpsimd
            def _(pool):
                pool.wait_ge(ld, 16 * 5)
                pool.tensor_copy(rec[:, :, :, 2], m.score[:]).then_inc(rec_step, 1)
                for c in range(2):
                    pool.tensor_copy(rec[:, :, :, c], tilerow[:, :, c].unsqueeze(2).to_broadcast([TP, NT, E]))\
                        .then_inc(rec_step, 1)
                pool.wait_ge(rec_step, 3)
                pool.tensor_tensor(left[:], m.score[:], rec[:, :, :, 2], ALU.subtract).then_inc(rec_step, 1)
                pool.wait_ge(rec_step, 4)
                pool.tensor_copy(rec[:, :, :, 3], left[:]).then_inc(rec_step, 1)
                pool.wait_ge(rec_step, 5)
                pool.tensor_tensor(rec[:, :, :, 4], left[:], rec[:, :, :, 3], ALU.subtract).then_inc(rec_step, 1)

            @block.tensor
            def _(pe):
                pe.wait_ge(init, 3)
                pe.wait_ge(ld, 16 * 5)
                with pe.Fori(0, NB // UNROLL) as i:
                    for n in range(UNROLL):
                        pe.wait_ge(c_cnt, i * UNROLL + n + 1)
                        pe.matmul(ps[0:TP, 0, 0:3 * E], ones[:], cnts[:].rearrange("p c e -> p (c e)"),
                                  start=True, stop=True).then_inc(c_tot, 1)
                pe.wait_ge(step, 3)
                pe.matmul(ps[0:TP, 1, 0:E], ones[:], cnt[:], start=True, stop=True)
                pe.matmul(ps[0:TP, 2, 0:NE], ones[:], flat(eq), start=True, stop=True)
                pe.matmul(ps[0:TP, 3, 0:NE], before[:], flat(eq), start=True, stop=True).then_inc(tie_ps, 1)
                pe.wait_ge(step, 11)
                pe.matmul(ps[0:TP, 4, 0:NE], ones[:], flat(gt), start=True, stop=True)
                pe.matmul(ps[0:TP, 5, 0:NE], before[:], flat(gt), start=True, stop=True).then_inc(pos_ps, 1)
                pe.matmul(ps[:, 6, 0:E * 20], zeros[:, 0:128], zeros[:, 0:E * 20], start=True, stop=False,
                          skip_group_check=True)
                pe.wait_ge(step, 29)
                pe.sem_inc(hot_used, 2)
                with pe.Fori(0, NT // 2) as i:
                    for n in range(2):
                        pe.wait_ge(hot_ready, i * 2 + n + 1)
                        for e in range(E):
                            r = place[:, bass.ds(i * 2 + n, 1), e].rearrange("p a s r -> p (a s r)")
                            last = pe.matmul(ps[:, 6, e * 20:(e + 1) * 20], hot[:, n, e, :], r,
                                             start=False, stop=False, skip_group_check=True)
                        last.then_inc(hot_used, 1)
                pe.matmul(ps[:, 6, 0:E * 20], zeros[:, 0:128], zeros[:, 0:E * 20], start=False, stop=True,
                          skip_group_check=True).then_inc(found_ps, 1)


def experts1(nc, sem, m, d, out):
    with ExitStack() as ctx:
        def tmp(name, shape, dt=F32):
            return ctx.enter_context(nc.sbuf_tensor(name, shape, dt))

        NS = TOPK // 128
        WN = DK * F
        CH = WN // NS
        assert WN == FK * D
        b1T = tmp("e1_b1T", [128, E, FK])
        b2 = tmp("e1_b2", [128, E, D])
        xT = tmp("e1_xT", [128, 2, DK, TOPK], F32R)
        h = tmp("e1_h", [128, 2, TOPK])
        ysum = tmp("e1_ysum", [128, 2, D])
        x, y = (m.xT[:].rearrange("p c t -> p (c t)")[:, a * 2 * NS * D:(a + 1) * 2 * NS * D]
                .rearrange("p (n s k) -> p n s k", n=2, s=NS) for a in range(2))
        raw = [[w[:, n].rearrange("p c f -> p (c f)") for n in range(2)] for w in (m.ring1, m.ring2)]
        ws = [tmp(f"e1_w{w}_parts", [128, 2, 2, WN], F32R) for w in (1, 2)]
        hT = [tmp(f"e1_hT_{part}", [128, FK, TOPK], F32R) for part in ("high", "low")]

        b_in, x_in = sem("e1_b_in"), [sem("e1_x_in_0"), sem("e1_x_in_1")]
        names = "w_high w_low xp xT xT_high hidden h_high h_low y_ready ysum y_sb y_free added".split()
        w_high, w_low, xp_ready, xT_ready, xT_high, h_ready, h_high, h_low, y_ready, ysum_ready, y_sb, y_free, added = (
            sem("e1_" + n) for n in names)
        ps = m.ps
        HB, XB, YB = 0, 4, 6
        w_in = m.ring_in

        def turns(eng, step, loops):
            with eng.Fori(0, loops) as i:
                step(i * 2, 0, i, False)
                step(i * 2 + 1, 1, i, False)
            for e in range(2 * loops, E):
                step(e, e % 2, e // 2, e == E - 1)

        with nc.Block() as block:
            @block.sync
            def _(sp):
                sp.dma_start(b1T[:], d["b1T_1"]).then_inc(b_in, 16)
                sp.dma_start(b2[:], d["b2_1"].unsqueeze(0).to_broadcast([128, E, D])).then_inc(b_in, 16)
                with sp.Fori(0, E // 2 - 1) as i:
                    for n in range(2):
                        sp.wait_ge(w_low, i * 4 * NS + (n + 1) * 2 * NS)
                        sp.dma_start(m.ring1[:, n:n + 1], d["w1_1"].rearrange("e (c p) f -> p e c f", p=128)
                                     [:, bass.ds(i * 2 + n + 2, 1)]).then_inc(w_in[n], 16)
                        sp.dma_start(m.ring2[:, n:n + 1], d["w2_1"].rearrange("e (c p) f -> p e c f", p=128)
                                     [:, bass.ds(i * 2 + n + 2, 1)]).then_inc(w_in[n], 16)

            @block.gpsimd
            def _(pool):
                def gather(e):
                    for s in range(NS):
                        c = e * NS + s
                        pool.indirect_dma_start(x[:, e % 2, s, :], None, m.xrows,
                                                bass.IndirectOffsetOnAxis(m.row1[:, c:c + 1], 0)).then_inc(x_in[e % 2], 16)

                def add_rows(e):
                    if e >= 1:
                        pool.wait_ge(added, 16 * NS * e)
                        pool.sem_inc(y_free, 1)
                    for s in range(NS):
                        pool.wait_ge(y_sb, e * NS + s + 1)
                        c = e * NS + s
                        pool.indirect_dma_start(out, bass.IndirectOffsetOnAxis(m.row1[:, c:c + 1], 0),
                                                y[:, e % 2, s, :], None, compute_op=ALU.add).then_inc(added, 16)

                pool.sem_inc(y_free, 2)
                gather(0)
                gather(1)
                for e in range(E):
                    if e >= 1:
                        add_rows(e - 1)
                    if e + 2 < E:
                        pool.wait_ge(xp_ready, 2 * (e + 1))
                        gather(e + 2)
                add_rows(E - 1)
                pool.wait_ge(added, 16 * NS * E)

            @block.tensor
            def _(pe):
                w1 = ws[0][:].rearrange("p n s (c f) -> p n s c f", c=DK)
                w2 = ws[1][:].rearrange("p n s (c f) -> p n s c f", c=FK)

                def turn_x(e, n, loads):
                    pe.wait_ge(x_in[n], loads * (16 * NS))
                    pe.wait_ge(xT_ready, e * 2 + 2)
                    for c in range(DK):
                        for s in range(NS):
                            last = pe.transpose(ps[:, XB + c, s * 128:(s + 1) * 128],
                                                x[:, n, s, c * 128:(c + 1) * 128], m.ident[:])
                        last.then_inc(xp_ready, 1)

                def step(e, n, turn, last_expert):
                    pe.wait_ge(w_low, e * 2 * NS + NS)
                    pe.wait_ge(xT_ready, e * 2 + 4)
                    for f in range(FK):
                        pe.wait_ge(h_high, e * FK + f + 1)
                        for k, (a, b) in enumerate(PARTS):
                            for c in range(DK):
                                last = pe.matmul(ps[:, HB + f % 4, :], w1[:, n, a, c, f * 128:(f + 1) * 128], xT[:, b, c, :],
                                                 start=(k == c == 0), stop=(k == 2 and c == DK - 1))
                        last.then_inc(h_ready, 1)
                    if not last_expert:
                        turn_x(e + 1, 1 - n, turn + 1 + n)
                    pe.wait_ge(w_low, e * 2 * NS + 2 * NS)
                    for s in range(NS):
                        pe.wait_ge(ysum_ready, e * NS + s + 1)
                        for f in range(FK):
                            if s == 0:
                                pe.wait_ge(h_low, e * FK + f + 3)
                            for k, (a, b) in enumerate(PARTS):
                                last = pe.matmul(ps[:, YB + s % 2, 0:D], hT[a][:, f, s * 128:(s + 1) * 128],
                                                 w2[:, n, b, f, :], start=(f == k == 0), stop=(f == FK - 1 and k == 2))
                        last.then_inc(y_ready, 1)

                turn_x(0, 0, 1)
                turns(pe, step, E // 2 - 1)

            @block.scalar
            def _(act):
                act.sem_inc(h_high, 4)
                act.wait_ge(b_in, 32)

                def weights_high(e, n, loads):
                    act.wait_ge(w_in[n], loads * 32)
                    for w in range(2):
                        for a in range(0, WN, 2 * CH):
                            act.copy(ws[w][:, n, 0, a:a + 2 * CH], raw[w][n][:, a:a + 2 * CH]).then_inc(w_high, 1)

                def step(e, n, turn, last_expert):
                    for f in range(FK):
                        act.wait_ge(h_ready, e * FK + f + 1)
                        act.wait_ge(h_low, e * FK + f + 1)
                        bias = b1T[:, bass.ds(e, 1), f]
                        act.activation(h[:, f % 2, :], ps[:, HB + f % 4, :], ACT.Relu, bias=bias)
                        act.activation(hT[0][:, f, :], ps[:, HB + f % 4, :], ACT.Relu, bias=bias).then_inc(h_high, 1)
                    if not last_expert:
                        weights_high(e + 1, 1 - n, turn + 1 + n)

                weights_high(0, 0, 1)
                turns(act, step, E // 2 - 1)

            @block.vector
            def _(dve):
                dve.sem_inc(ysum_ready, 2)
                dve.sem_inc(xT_ready, 2)
                dve.sem_inc(h_low, 2)
                dve.wait_ge(b_in, 32)

                def weights_low(e, n, w, j):
                    a = j * CH
                    dve.wait_ge(w_high, e * NS + (2 * w + j // 2 + 1))
                    dve.tensor_tensor(ws[w][:, n, 1, a:a + CH], raw[w][n][:, a:a + CH],
                                      ws[w][:, n, 0, a:a + CH].bitcast(F32), ALU.subtract).then_inc(w_low, 1)

                def split_x(e):
                    for c in range(DK):
                        dve.wait_ge(xp_ready, e * 2 + c + 1)
                        dve.tensor_copy(xT[:, 0, c, :], ps[:, XB + c, :]).then_inc(xT_high, 1)
                        dve.wait_ge(xT_high, e * 2 + c + 1)
                        dve.tensor_tensor(xT[:, 1, c, :], ps[:, XB + c, :], xT[:, 0, c, :].bitcast(F32), ALU.subtract)\
                           .then_inc(xT_ready, 1)

                def step(e, n, turn, last_expert):
                    for f in range(FK):
                        if f < NS:
                            weights_low(e, n, 1, f)
                        dve.wait_ge(h_high, e * FK + f + 5)
                        dve.tensor_tensor(hT[1][:, f, :], h[:, f % 2, :], hT[0][:, f, :].bitcast(F32), ALU.subtract)\
                           .then_inc(h_low, 1)
                    if not last_expert:
                        split_x(e + 1)
                    for s in range(NS):
                        if not last_expert:
                            weights_low(e + 1, 1 - n, 0, s)
                        dve.wait_ge(y_ready, e * NS + s + 1)
                        dve.tensor_tensor(ysum[:, s % 2:s % 2 + 1], ps[:, YB + s % 2, 0:D].unsqueeze(1),
                                          b2[:, bass.ds(e, 1)], ALU.add).then_inc(ysum_ready, 1)
                        dve.wait_ge(ysum_ready, e * NS + s + 3)
                        if s == 0:
                            dve.wait_ge(y_free, e + 1)
                        dve.tensor_scalar(y[:, n, s, :], ysum[:, s % 2, :], m.gate1[:, bass.ds(e * NS + s, 1)],
                                          None, ALU.mult).then_inc(y_sb, 1)

                for j in range(NS):
                    weights_low(0, 0, 0, j)
                split_x(0)
                turns(dve, step, E // 2 - 1)


def layouts(inputs):
    f32 = np.float32
    g = {n: np.asarray(a) for n, a in inputs.items()}
    x = g["x"].reshape(B, 3, HP, 16, HP, 16).transpose(0, 2, 4, 3, 5, 1).reshape(B * NPATCH, PATCH)
    inv = (1.0 / 10000.0 ** (np.arange(0, HD, 2, dtype=f32) / f32(HD))).astype(f32)
    ang = np.repeat(np.arange(NH, dtype=f32)[:, None] * inv[None, :], 2, 1).reshape(-1)
    sign = np.where(np.arange(D) % 2, 1, -1)
    scale = np.array([[0.25], [1.0]], f32)
    cos, sin = (np.cos(ang) * scale).astype(f32), (np.sin(ang) * sign * scale).astype(f32)
    swap = np.arange(D) ^ 1
    rem_mask = np.zeros((128, 4), f32)
    rem_mask[0:3 * REM:3, 0] = 1
    rem_mask[1:3 * REM:3, 1] = 1
    rem_mask[2:3 * REM:3, 2:4] = 1
    head_mask = (np.arange(128)[:, None] // HD == np.arange(8)[None]).astype(f32)
    o_order = np.concatenate([(2 * u + ab) * HD + np.arange(HD) for ab in range(2) for u in range(NU)])

    yy, xx = np.meshgrid(np.arange(HP), np.arange(HP), indexing="ij")
    omega = (1.0 / 10000.0 ** (np.arange(D // 4, dtype=f32) / f32(D // 4 - 1))).astype(f32)
    yy, xx = yy.reshape(-1, 1).astype(f32) * omega, xx.reshape(-1, 1).astype(f32) * omega
    pos = np.concatenate([np.sin(xx), np.cos(xx), np.sin(yy), np.cos(yy)], 1).astype(f32)

    n = np.maximum(np.arange(512) - (SEQ - 1), 0)
    large = 16 + (np.log(np.maximum(n, 1).astype(f32) / 16) / math.log(128 / 16) * 16).astype(np.int32)
    bucket = np.where(n < 16, n, np.minimum(large, 31))
    buckets = (np.arange(32)[:, None] == bucket[None, :]).astype(f32)
    j, i = np.arange(128)[:, None], np.arange(SEQ)[None, :]
    main, rem = j <= i, (j[:, :1] % 64 <= i[:, :REM]) & (j % 64 < REM)
    mask1 = np.concatenate([main, main, rem], 1).astype(f32)

    def gb(a):
        return a.reshape(KP, 128).T

    d = {
        "patches": x, "txt": g["txt"], "ident": np.eye(128, dtype=f32),
        "ln1_gb": np.stack([gb(g["L0_tok_ln1_g"]), gb(g["L0_tok_ln1_b"])], 1),
        "tok_bias": g["L0_tok_bias"][None], "ln2_g": g["L0_tok_ln2_g"][None], "ln2_b": g["L0_tok_ln2_b"][None],
        "pos": np.concatenate([pos, pos], 0), "cls": g["L0_tok_cls_token"][0],
        "cls_pos": g["L0_tok_cls_pos_embedding"][0], "tok_w": g["L0_tok_W"],
        "wq": g["L0_attn_wq"].T, "wq_swap": g["L0_attn_wq"][swap].T,
        "wlat": np.concatenate([g["L0_attn_wk_a"].T, g["L0_attn_wv_a"].T], 1),
        "wkb": g["L0_attn_wk_b"].T, "wkb_swap": g["L0_attn_wk_b"][swap].T, "head_mask": head_mask,
        "wvb": g["L0_attn_wv_b"].T, "wo": g["L0_attn_wo"].T[o_order],
        "rot_cos": cos, "rot_sin": sin, "rem_mask": rem_mask,
        "w1": g["L0_ffn_w1"], "w2": g["L0_ffn_w2"], "w_red": g["L0_ffn_w_red"], "wg": g["L0_ffn_wg"],
        "b1T": g["L0_ffn_b1"].reshape(E, FK, 128).transpose(2, 0, 1).reshape(128, E * FK), "b2": g["L0_ffn_b2"],
        "iota8": (np.arange(E, dtype=f32) - E)[None], "rows128": (np.arange(21, dtype=f32) * 128)[None],
        "tiles_j": np.arange(SLOT_TILES, dtype=f32)[None],
        "keep": np.tile(np.arange(NT) > 0, (E, 1)).astype(f32),
        "spread16": np.tile(np.eye(GD, dtype=f32), (1, 8)),
        "diag_mask": np.repeat(np.eye(8, dtype=f32), GD, 0)[:, :, None] * np.ones((1, 1, E), f32),
        "before": np.triu(np.ones((TP, TP), f32), 1),
        "wqk": g["L1_attn_Wqk"], "wv": g["L1_attn_Wv"], "bv": g["L1_attn_bv"][None],
        "a1_cst": np.stack([g["L1_attn_bqk"], *g["L1_attn_gamma"], *g["L1_attn_beta"]], 1),
        "rel_emb": g["L1_attn_rel_emb"], "buckets": buckets, "mask1": mask1,
        "router_w": g["L1_ffn_router_w"], "router_b": g["L1_ffn_router_b"][None],
        "bits": np.tile((np.arange(1, 4) << np.arange(28, -1, -2)[:, None]).astype(np.int32), (TP, 1, 1)),
        "tile_row": np.stack(np.broadcast_arrays(np.arange(NT)[None], np.arange(TP)[:, None]), 2).astype(f32),
        "iota128": np.arange(128).astype(np.float16)[None],
        "b1T_1": g["L1_ffn_b1"].reshape(E, FK, 128).transpose(2, 0, 1), "b2_1": g["L1_ffn_b2"],
        "w1_1": g["L1_ffn_w1"], "w2_1": g["L1_ffn_w2"],
    }
    return {n: np.ascontiguousarray(a) for n, a in d.items()}


def kernel(**inputs):
    import concourse.bacc as _bacc
    from concourse.bass_utils import run_bass_kernel_spmd as _run

    nc = _bacc.Bacc("TRN2", target_bir_lowering=False, num_devices=1)
    arrays = {f"in_{n}": a for n, a in layouts(inputs).items()}
    d = {n[3:]: nc.dram_tensor(n, a.shape, mybir.dt.from_np(a.dtype), kind="ExternalInput").ap()
         for n, a in arrays.items()}
    out = nc.dram_tensor("out", (TOK, D), F32, kind="ExternalOutput").ap()
    build(nc, d, out)
    r = _run(nc, [arrays], core_ids=[0])
    return r.results[0]["out"].reshape(B, SEQ, D)
```
